# Optimizing a Trainium2 kernel written in Bass

```python
import numpy as np
import jax
import jax.numpy as jnp

def _softmax(x, axis=-1):
    return jax.nn.softmax(x, axis=axis)

def _gelu(x):
    return jax.nn.gelu(x, approximate=True)

def _silu(x):
    return jax.nn.silu(x)

def _sigmoid(x):
    return jax.nn.sigmoid(x)

def _layernorm(x, axis=-1, eps=1e-05):
    m = jnp.mean(x, axis=axis, keepdims=True)
    v = jnp.var(x, axis=axis, keepdims=True)
    return (x - m) / jnp.sqrt(v + eps)

def _scatter_add(tgt, idx, src, axis=0):
    return tgt.at[idx].add(src)

def _segment_sum(src, seg, n):
    return jax.ops.segment_sum(src, seg, n)
kernel_name = 'mk_conv_attn_hybrid_d2_conv_nchw128_r2_aab419'

def setup_inputs(seed: int=0):
    np.random.seed(seed)
    _w = jnp.asarray

    def _rec_inputs():
        import jax
        import jax.numpy as jnp
        _gk = jax.random.key(seed)
        x = -0.0005207 + 1.001 * jax.random.normal(jax.random.fold_in(_gk, 1), (4, 64, 32, 32), jnp.float32)
        return x
    x = _rec_inputs()

    def _L0_conv_setup():
        import jax, jax.numpy as jnp
        import numpy as np
        D_MODEL = 64
        D_INNER = 128
        D_STATE = 16
        DT_RANK = 8
        D_CONV = 2
        GROUPS = 4
        EPS = 1e-05

        def _mamba_dir(x, W_in, conv_w, conv_b, W_x, W_dt, b_dt, A_log, D, W_out):
            B, L, _ = x.shape
            xz = x @ W_in
            xp, z = (xz[..., :D_INNER], xz[..., D_INNER:])
            xprev = jnp.pad(xp, ((0, 0), (1, 0), (0, 0)))[:, :L]
            xc = jax.nn.silu(xprev * conv_w[:, 0] + xp * conv_w[:, 1] + conv_b)
            xdb = xc @ W_x
            dt_r = xdb[..., :DT_RANK]
            Bc = xdb[..., DT_RANK:DT_RANK + D_STATE]
            Cc = xdb[..., DT_RANK + D_STATE:]
            dt = jax.nn.softplus(dt_r @ W_dt + b_dt)
            A = -jnp.exp(A_log)

            def step(h, inp):
                dt_t, B_t, C_t, x_t = inp
                dA = jnp.exp(dt_t[:, :, None] * A)
                h = dA * h + (dt_t * x_t)[:, :, None] * B_t[:, None, :]
                y = jnp.einsum('bds,bs->bd', h, C_t)
                return (h, y)
            h0 = jnp.zeros((B, D_INNER, D_STATE), x.dtype)
            xs = (jnp.moveaxis(dt, 1, 0), jnp.moveaxis(Bc, 1, 0), jnp.moveaxis(Cc, 1, 0), jnp.moveaxis(xc, 1, 0))
            _, ys = jax.lax.scan(step, h0, xs)
            y = jnp.moveaxis(ys, 0, 1) + D * xc
            y = y * jax.nn.silu(z)
            return y @ W_out

        def _groupnorm_silu(x, gamma, beta):
            B, C, H, W = x.shape
            xg = x.reshape(B, GROUPS, C // GROUPS, H, W)
            mu = xg.mean(axis=(2, 3, 4), keepdims=True)
            var = xg.var(axis=(2, 3, 4), keepdims=True)
            xn = ((xg - mu) * jax.lax.rsqrt(var + EPS)).reshape(B, C, H, W)
            return jax.nn.silu(xn * gamma[None, :, None, None] + beta[None, :, None, None])
        key = jax.random.key(seed)
        ks = jax.random.split(key, 24)
        s = 0.02
        A_log = jnp.log(jnp.tile(jnp.arange(1, D_STATE + 1, dtype=jnp.float32)[None, :], (D_INNER, 1)))
        inp = {'x': jax.random.normal(ks[0], (4, D_MODEL, 32, 32), jnp.float32)}
        for i, sfx in enumerate(('f', 'b')):
            o = 1 + 9 * i
            inp[f'W_in_{sfx}'] = jax.random.normal(ks[o], (D_MODEL, 2 * D_INNER)) * s
            inp[f'conv_w_{sfx}'] = jax.random.normal(ks[o + 1], (D_INNER, D_CONV)) * 0.5
            inp[f'conv_b_{sfx}'] = jnp.zeros((D_INNER,))
            inp[f'W_x_{sfx}'] = jax.random.normal(ks[o + 2], (D_INNER, DT_RANK + 2 * D_STATE)) * s
            inp[f'W_dt_{sfx}'] = jax.random.normal(ks[o + 3], (DT_RANK, D_INNER)) * s
            inp[f'b_dt_{sfx}'] = jnp.full((D_INNER,), -3.0)
            inp[f'A_log_{sfx}'] = A_log
            inp[f'D_{sfx}'] = jnp.ones((D_INNER,))
            inp[f'W_out_{sfx}'] = jax.random.normal(ks[o + 4], (D_INNER, D_MODEL)) * s
        inp['gn_gamma'] = jnp.ones((D_MODEL,))
        inp['gn_beta'] = jnp.zeros((D_MODEL,))
        return inp
    _L0_conv_all = _L0_conv_setup()
    _L0_conv_in = {k: v for k, v in _L0_conv_all.items() if k in ('W_in_f', 'conv_w_f', 'conv_b_f', 'W_x_f', 'W_dt_f', 'b_dt_f', 'A_log_f', 'D_f', 'W_out_f', 'W_in_b', 'conv_w_b', 'conv_b_b', 'W_x_b', 'W_dt_b', 'b_dt_b', 'A_log_b', 'D_b', 'W_out_b', 'gn_gamma', 'gn_beta')}
    del _L0_conv_all

    def _L1_attn_setup():
        import jax, jax.numpy as jnp
        import numpy as np
        B, T, C = (16, 1024, 64)
        HEAD_SIZE = 64
        key = jax.random.key(seed)
        k1, k2, k3, k4 = jax.random.split(key, 4)
        x = jax.random.normal(k1, (B, T, C), dtype=jnp.float32)
        scale = (1.0 / np.sqrt(C)).astype(np.float32)
        Wq = jax.random.normal(k2, (HEAD_SIZE, C), dtype=jnp.float32) * scale
        Wk = jax.random.normal(k3, (HEAD_SIZE, C), dtype=jnp.float32) * scale
        Wv = jax.random.normal(k4, (HEAD_SIZE, C), dtype=jnp.float32) * scale
        return {'x': x, 'Wq': Wq, 'Wk': Wk, 'Wv': Wv}
    _L1_attn_all = _L1_attn_setup()
    _L1_attn_in = {k: v for k, v in _L1_attn_all.items() if k in ('Wq', 'Wk', 'Wv')}
    del _L1_attn_all

    def _L1_ffn_setup():
        import jax, jax.numpy as jnp
        import numpy as np
        PADDED_SL = 4096
        TEMPERATURE = 1.0
        SIGMA_POW = 0.25

        def _stu_conv(phi, u, n):
            b, sl, d = u.shape
            sgn = jnp.where(jnp.arange(sl) % 2 == 0, 1.0, -1.0).astype(u.dtype)
            sgn3 = sgn[None, :, None]
            Vf = jnp.fft.rfft(phi, n=n, axis=0)
            Uf_p = jnp.fft.rfft(u, n=n, axis=1)
            Uf_m = jnp.fft.rfft(u * sgn3, n=n, axis=1)
            U_plus = jnp.fft.irfft(Vf[None, :, :, None] * Uf_p[:, :, None, :], n=n, axis=1)[:, :sl]
            U_minus = jnp.fft.irfft(Vf[None, :, :, None] * Uf_m[:, :, None, :], n=n, axis=1)[:, :sl]
            U_minus = U_minus * sgn[None, :, None, None]
            return (U_plus, U_minus)

        def _compute_spectral(u, sigma, phi, Mpp, Mpm):
            U_plus, U_minus = _stu_conv(phi, u, PADDED_SL)
            s = sigma ** SIGMA_POW
            out = jnp.einsum('btkd,k,kde->bte', U_plus, s, Mpp)
            out = out + jnp.einsum('btkd,k,kde->bte', U_minus, s, Mpm)
            return out

        def _compute_ar_u(Mu, u):
            sl = u.shape[1]
            out = jnp.zeros(u.shape[:2] + (Mu.shape[-1],), dtype=u.dtype)
            for i in range(Mu.shape[0]):
                ui = jnp.pad(u, ((0, 0), (i, 0), (0, 0)))[:, :sl]
                out = out + jnp.einsum('btd,de->bte', ui, Mu[i])
            return out

        def _stu(u, sigma, phi, Mu, Mpp, Mpm):
            return _compute_spectral(u, sigma, phi, Mpp, Mpm) + _compute_ar_u(Mu, u)
        key = jax.random.key(seed)
        ks = jax.random.split(key, 8)
        b, sl, d, K, k_u = (2, 2048, 64, 16, 3)
        x = jax.random.normal(ks[0], (b, sl, d), dtype=jnp.float32)
        sigma = jax.random.uniform(ks[1], (K,), dtype=jnp.float32, minval=0.001, maxval=1.0)
        phi = jax.random.normal(ks[2], (sl, K), dtype=jnp.float32) / np.sqrt(sl)
        M_u = jax.random.normal(ks[3], (4, k_u, d, d), dtype=jnp.float32) * 0.02
        M_phi_plus = jax.random.normal(ks[4], (4, K, d, d), dtype=jnp.float32) * 0.02
        M_phi_minus = jax.random.normal(ks[5], (4, K, d, d), dtype=jnp.float32) * 0.02
        log_weights = jnp.ones((4,), dtype=jnp.float32)
        u01 = jax.random.uniform(ks[6], (4,), dtype=jnp.float32, minval=1e-06, maxval=1.0 - 1e-06)
        gumbel = -jnp.log(-jnp.log(u01))
        return {'x': x, 'sigma': sigma, 'phi': phi, 'M_u': M_u, 'M_phi_plus': M_phi_plus, 'M_phi_minus': M_phi_minus, 'log_weights': log_weights, 'gumbel': gumbel}
    _L1_ffn_all = _L1_ffn_setup()
    _L1_ffn_in = {k: v for k, v in _L1_ffn_all.items() if k in ('sigma', 'phi', 'M_u', 'M_phi_plus', 'M_phi_minus', 'log_weights', 'gumbel')}
    del _L1_ffn_all
    return {'x': x, 'L0_conv_W_in_f': _L0_conv_in['W_in_f'], 'L0_conv_conv_w_f': _L0_conv_in['conv_w_f'], 'L0_conv_conv_b_f': _L0_conv_in['conv_b_f'], 'L0_conv_W_x_f': _L0_conv_in['W_x_f'], 'L0_conv_W_dt_f': _L0_conv_in['W_dt_f'], 'L0_conv_b_dt_f': _L0_conv_in['b_dt_f'], 'L0_conv_A_log_f': _L0_conv_in['A_log_f'], 'L0_conv_D_f': _L0_conv_in['D_f'], 'L0_conv_W_out_f': _L0_conv_in['W_out_f'], 'L0_conv_W_in_b': _L0_conv_in['W_in_b'], 'L0_conv_conv_w_b': _L0_conv_in['conv_w_b'], 'L0_conv_conv_b_b': _L0_conv_in['conv_b_b'], 'L0_conv_W_x_b': _L0_conv_in['W_x_b'], 'L0_conv_W_dt_b': _L0_conv_in['W_dt_b'], 'L0_conv_b_dt_b': _L0_conv_in['b_dt_b'], 'L0_conv_A_log_b': _L0_conv_in['A_log_b'], 'L0_conv_D_b': _L0_conv_in['D_b'], 'L0_conv_W_out_b': _L0_conv_in['W_out_b'], 'L0_conv_gn_gamma': _L0_conv_in['gn_gamma'], 'L0_conv_gn_beta': _L0_conv_in['gn_beta'], 'L1_attn_Wq': _L1_attn_in['Wq'], 'L1_attn_Wk': _L1_attn_in['Wk'], 'L1_attn_Wv': _L1_attn_in['Wv'], 'L1_ffn_sigma': _L1_ffn_in['sigma'], 'L1_ffn_phi': _L1_ffn_in['phi'], 'L1_ffn_M_u': _L1_ffn_in['M_u'], 'L1_ffn_M_phi_plus': _L1_ffn_in['M_phi_plus'], 'L1_ffn_M_phi_minus': _L1_ffn_in['M_phi_minus'], 'L1_ffn_log_weights': _L1_ffn_in['log_weights'], 'L1_ffn_gumbel': _L1_ffn_in['gumbel']}

def reference(x, L0_conv_W_in_f, L0_conv_conv_w_f, L0_conv_conv_b_f, L0_conv_W_x_f, L0_conv_W_dt_f, L0_conv_b_dt_f, L0_conv_A_log_f, L0_conv_D_f, L0_conv_W_out_f, L0_conv_W_in_b, L0_conv_conv_w_b, L0_conv_conv_b_b, L0_conv_W_x_b, L0_conv_W_dt_b, L0_conv_b_dt_b, L0_conv_A_log_b, L0_conv_D_b, L0_conv_W_out_b, L0_conv_gn_gamma, L0_conv_gn_beta, L1_attn_Wq, L1_attn_Wk, L1_attn_Wv, L1_ffn_sigma, L1_ffn_phi, L1_ffn_M_u, L1_ffn_M_phi_plus, L1_ffn_M_phi_minus, L1_ffn_log_weights, L1_ffn_gumbel):
    import jax
    import jax.numpy as jnp

    def _L0_conv_ref(x, W_in_f, conv_w_f, conv_b_f, W_x_f, W_dt_f, b_dt_f, A_log_f, D_f, W_out_f, W_in_b, conv_w_b, conv_b_b, W_x_b, W_dt_b, b_dt_b, A_log_b, D_b, W_out_b, gn_gamma, gn_beta):
        import jax, jax.numpy as jnp
        import numpy as np
        D_MODEL = 64
        D_INNER = 128
        D_STATE = 16
        DT_RANK = 8
        D_CONV = 2
        GROUPS = 4
        EPS = 1e-05

        def _mamba_dir(x, W_in, conv_w, conv_b, W_x, W_dt, b_dt, A_log, D, W_out):
            B, L, _ = x.shape
            xz = x @ W_in
            xp, z = (xz[..., :D_INNER], xz[..., D_INNER:])
            xprev = jnp.pad(xp, ((0, 0), (1, 0), (0, 0)))[:, :L]
            xc = jax.nn.silu(xprev * conv_w[:, 0] + xp * conv_w[:, 1] + conv_b)
            xdb = xc @ W_x
            dt_r = xdb[..., :DT_RANK]
            Bc = xdb[..., DT_RANK:DT_RANK + D_STATE]
            Cc = xdb[..., DT_RANK + D_STATE:]
            dt = jax.nn.softplus(dt_r @ W_dt + b_dt)
            A = -jnp.exp(A_log)

            def step(h, inp):
                dt_t, B_t, C_t, x_t = inp
                dA = jnp.exp(dt_t[:, :, None] * A)
                h = dA * h + (dt_t * x_t)[:, :, None] * B_t[:, None, :]
                y = jnp.einsum('bds,bs->bd', h, C_t)
                return (h, y)
            h0 = jnp.zeros((B, D_INNER, D_STATE), x.dtype)
            xs = (jnp.moveaxis(dt, 1, 0), jnp.moveaxis(Bc, 1, 0), jnp.moveaxis(Cc, 1, 0), jnp.moveaxis(xc, 1, 0))
            _, ys = jax.lax.scan(step, h0, xs)
            y = jnp.moveaxis(ys, 0, 1) + D * xc
            y = y * jax.nn.silu(z)
            return y @ W_out

        def _groupnorm_silu(x, gamma, beta):
            B, C, H, W = x.shape
            xg = x.reshape(B, GROUPS, C // GROUPS, H, W)
            mu = xg.mean(axis=(2, 3, 4), keepdims=True)
            var = xg.var(axis=(2, 3, 4), keepdims=True)
            xn = ((xg - mu) * jax.lax.rsqrt(var + EPS)).reshape(B, C, H, W)
            return jax.nn.silu(xn * gamma[None, :, None, None] + beta[None, :, None, None])
        B, C, H, W = x.shape
        xs = x.transpose(0, 2, 3, 1).reshape(B, H * W, C)
        y_f = _mamba_dir(xs, W_in_f, conv_w_f, conv_b_f, W_x_f, W_dt_f, b_dt_f, A_log_f, D_f, W_out_f)
        xr = xs[:, ::-1]
        y_b = _mamba_dir(xr, W_in_b, conv_w_b, conv_b_b, W_x_b, W_dt_b, b_dt_b, A_log_b, D_b, W_out_b)[:, ::-1]
        y = y_f + y_b
        y = y.reshape(B, H, W, C).transpose(0, 3, 1, 2)
        y = _groupnorm_silu(y, gn_gamma, gn_beta)
        return y + x

    def _L1_attn_ref(x, Wq, Wk, Wv):
        import jax, jax.numpy as jnp
        import numpy as np
        B, T, C = (16, 1024, 64)
        HEAD_SIZE = 64
        Bd, Td, Cd = x.shape
        q = jnp.einsum('btc,hc->bth', x, Wq)
        k = jnp.einsum('btc,hc->bth', x, Wk)
        v = jnp.einsum('btc,hc->bth', x, Wv)
        scores = jnp.einsum('bth,bsh->bts', q, k) * Cd ** (-0.5)
        causal = jnp.tril(jnp.ones((Td, Td), dtype=bool))
        scores = jnp.where(causal, scores, -jnp.inf)
        attn = jax.nn.softmax(scores, axis=-1)
        out = jnp.einsum('bts,bsh->bth', attn, v)
        return out

    def _L1_ffn_ref(x, sigma, phi, M_u, M_phi_plus, M_phi_minus, log_weights, gumbel):
        import jax, jax.numpy as jnp
        import numpy as np
        PADDED_SL = 4096
        TEMPERATURE = 1.0
        SIGMA_POW = 0.25

        def _stu_conv(phi, u, n):
            b, sl, d = u.shape
            sgn = jnp.where(jnp.arange(sl) % 2 == 0, 1.0, -1.0).astype(u.dtype)
            sgn3 = sgn[None, :, None]
            Vf = jnp.fft.rfft(phi, n=n, axis=0)
            Uf_p = jnp.fft.rfft(u, n=n, axis=1)
            Uf_m = jnp.fft.rfft(u * sgn3, n=n, axis=1)
            U_plus = jnp.fft.irfft(Vf[None, :, :, None] * Uf_p[:, :, None, :], n=n, axis=1)[:, :sl]
            U_minus = jnp.fft.irfft(Vf[None, :, :, None] * Uf_m[:, :, None, :], n=n, axis=1)[:, :sl]
            U_minus = U_minus * sgn[None, :, None, None]
            return (U_plus, U_minus)

        def _compute_spectral(u, sigma, phi, Mpp, Mpm):
            U_plus, U_minus = _stu_conv(phi, u, PADDED_SL)
            s = sigma ** SIGMA_POW
            out = jnp.einsum('btkd,k,kde->bte', U_plus, s, Mpp)
            out = out + jnp.einsum('btkd,k,kde->bte', U_minus, s, Mpm)
            return out

        def _compute_ar_u(Mu, u):
            sl = u.shape[1]
            out = jnp.zeros(u.shape[:2] + (Mu.shape[-1],), dtype=u.dtype)
            for i in range(Mu.shape[0]):
                ui = jnp.pad(u, ((0, 0), (i, 0), (0, 0)))[:, :sl]
                out = out + jnp.einsum('btd,de->bte', ui, Mu[i])
            return out

        def _stu(u, sigma, phi, Mu, Mpp, Mpm):
            return _compute_spectral(u, sigma, phi, Mpp, Mpm) + _compute_ar_u(Mu, u)
        T = x.shape[1]
        outs = []
        for i, frac in enumerate((1, 2, 4, 8)):
            xi = x[:, :T // frac]
            si = _stu(xi, sigma, phi, M_u[i], M_phi_plus[i], M_phi_minus[i])
            si = jnp.pad(si, ((0, 0), (0, T - si.shape[1]), (0, 0)))
            outs.append(si)
        y_soft = jax.nn.softmax((log_weights + gumbel) / TEMPERATURE)
        y_hard = jax.nn.one_hot(jnp.argmax(y_soft), 4, dtype=y_soft.dtype)
        weights = y_hard - jax.lax.stop_gradient(y_soft) + y_soft
        stacked = jnp.stack(outs, axis=-1)
        return jnp.sum(stacked * weights, axis=-1)

    def _gn(v, G=32, eps=1e-05):
        B_, C_, H_, W_ = v.shape
        g = v.reshape(B_, G, C_ // G, H_, W_)
        m = jnp.mean(g, axis=(2, 3, 4), keepdims=True)
        s = jnp.var(g, axis=(2, 3, 4), keepdims=True)
        return ((g - m) / jnp.sqrt(s + eps)).reshape(v.shape)

    def _ln_c(v, eps=1e-06):
        m = jnp.mean(v, axis=1, keepdims=True)
        s = jnp.var(v, axis=1, keepdims=True)
        return (v - m) / jnp.sqrt(s + eps)

    def _ln_t(v, eps=1e-05):
        m = jnp.mean(v, axis=-1, keepdims=True)
        s = jnp.var(v, axis=-1, keepdims=True)
        return (v - m) / jnp.sqrt(s + eps)

    def _to_tokens(v):
        B_, C_, H_, W_ = v.shape
        return v.reshape(B_, C_, H_ * W_).transpose(0, 2, 1)

    def _from_tokens(t, like):
        B_, C_, H_, W_ = like.shape
        return t.transpose(0, 2, 1).reshape(B_, C_, H_, W_)
    x = _L0_conv_ref(x, L0_conv_W_in_f, L0_conv_conv_w_f, L0_conv_conv_b_f, L0_conv_W_x_f, L0_conv_W_dt_f, L0_conv_b_dt_f, L0_conv_A_log_f, L0_conv_D_f, L0_conv_W_out_f, L0_conv_W_in_b, L0_conv_conv_w_b, L0_conv_conv_b_b, L0_conv_W_x_b, L0_conv_W_dt_b, L0_conv_b_dt_b, L0_conv_A_log_b, L0_conv_D_b, L0_conv_W_out_b, L0_conv_gn_gamma, L0_conv_gn_beta)
    t = _to_tokens(x)
    t = t + _L1_attn_ref(_ln_t(t), L1_attn_Wq, L1_attn_Wk, L1_attn_Wv)
    t = t + _L1_ffn_ref(_ln_t(t), L1_ffn_sigma, L1_ffn_phi, L1_ffn_M_u, L1_ffn_M_phi_plus, L1_ffn_M_phi_minus, L1_ffn_log_weights, L1_ffn_gumbel)
    x = _from_tokens(t, x)
    return x

_drawn_inputs = setup_inputs


def setup_inputs(seed=0):
    import zlib

    import numpy as np

    out = dict(_drawn_inputs(seed))
    spreads = {'L0_conv_conv_b_f': (0.0, 0.1),
     'L0_conv_b_dt_f': (-3.0, 0.6),
     'L0_conv_D_f': (1.0, 0.2),
     'L0_conv_conv_b_b': (0.0, 0.1),
     'L0_conv_b_dt_b': (-3.0, 0.6),
     'L0_conv_D_b': (1.0, 0.2),
     'L0_conv_gn_gamma': (1.0, 0.2),
     'L0_conv_gn_beta': (0.0, 0.1),
     'L1_ffn_log_weights': (1.0, 0.2)}
    factors = {'L0_conv_W_x_f': 64.0,
     'L0_conv_W_dt_f': 64.0,
     'L0_conv_A_log_f': 64.0,
     'L0_conv_W_x_b': 64.0,
     'L0_conv_W_dt_b': 64.0,
     'L0_conv_A_log_b': 64.0}
    for name, (base, spread) in spreads.items():
        noise = np.random.default_rng([zlib.crc32(name.encode()), seed]).standard_normal(out[name].shape)
        drawn = base * np.exp(spread * noise) if base else spread * noise
        out[name] = jnp.asarray(drawn.astype(out[name].dtype))
    for name, factor in factors.items():
        out[name] = (out[name] * factor).astype(out[name].dtype)
    return out
```

```python
from contextlib import ExitStack

import concourse.bass as bass
from concourse import mybir

F32 = mybir.dt.float32
BF16 = mybir.dt.bfloat16
F32R = mybir.dt.float32r
ALU = mybir.AluOpType
ACT = mybir.ActivationFunctionType
AX = mybir.AxisListType

B = 4
C = 64
L = 1024
H = 512
D = 128
N = 16
R = 8
GROUP = 16
GN_EPS = 1e-5
LN_EPS = 1e-5
DIRS = "fb"
DEEP = 4
PAIR = 2
Y_LAG = 3
TILES = L // 128
SPANS = TILES // 2
SPAN = 2 * 128
EXPERTS = 4
FILTERS = 16
AR_TAPS = 3
A_LOG_MAX = 60.0
PARTS = 3
BC = 2 * N
DT_ROW = PARTS * BC


def at_least(engine, semaphore, count):
    if isinstance(count, int) and count <= 0:
        return
    engine.wait_ge(semaphore, count)


def mamba_stage(nc, ins, x1):
    with ExitStack() as ctx:
        def sb(name, shape, dt=F32):
            return ctx.enter_context(nc.sbuf_tensor(name, shape, dt))

        def sem(name):
            return ctx.enter_context(nc.semaphore(name))

        x_pair = [sb(f"x_pair_{d}", [2 * C, B * L]) for d in DIRS]
        w_in = [sb(f"w_in_{d}", [2 * C, D]) for d in DIRS]
        taps = [sb(f"taps_{d}", [2 * C, D]) for d in DIRS]
        w_conv = [sb(f"w_conv_{d}", [2 * C, D]) for d in DIRS]
        w_gate = [sb(f"w_gate_{d}", [2 * C, D]) for d in DIRS]
        w_x = [sb(f"w_x_{d}", [D, DT_ROW + R]) for d in DIRS]
        w_dt = [sb(f"w_dt_{d}", [128, D]) for d in DIRS]
        w_out = [sb(f"w_out_{d}", [D, C]) for d in DIRS]
        cols = [sb(f"cols_{d}", [D, 2]) for d in DIRS]
        a_log = [sb(f"a_log_{d}", [D, N]) for d in DIRS]
        a_neg = [sb(f"a_neg_{d}", [D, N]) for d in DIRS]
        gn_cols = sb("gn_cols", [C, 2])
        ident = sb("ident", [128, 128])
        pick = sb("pick", [DT_ROW, BC], BF16)
        spread = sb("spread", [DT_ROW, BC, 128], BF16)
        xc = [sb(f"xc_{d}", [D, L]) for d in DIRS]
        gate = [sb(f"gate_{d}", [D, L]) for d in DIRS]
        dt = [sb(f"dt_{d}", [D, L]) for d in DIRS]
        dtx = [sb(f"dtx_{d}", [D, L]) for d in DIRS]
        bc_parts = [sb(f"bc_parts_{d}", [DT_ROW, L], BF16) for d in DIRS]
        gated = [sb(f"gated_{d}", [D, L]) for d in DIRS]
        scratch = sb("scratch", [D, L])
        soft = sb("soft", [D, L])
        one_plus = sb("one_plus", [D, L])
        dt_low = sb("dt_low", [128, L])
        decay = [sb(f"decay_{i}", [D, L]) for i in range(DEEP)]
        hidden = [sb(f"hidden_{i}", [D, L]) for i in range(DEEP)]
        c_wide = [sb(f"c_wide_{i}", [D, L]) for i in range(DEEP)]
        drive = [sb(f"drive_{i}", [D, L]) for i in range(PAIR)]
        prod = [sb(f"prod_{i}", [D, L]) for i in range(PAIR)]
        mixed = sb("mixed", [C, L])
        bn = sb("bn", [C, 2, 6])
        stats = sb("stats", [C, 32])
        stats_t = sb("stats_t", [C, 32])
        group_t = sb("group_t", [C, 2])
        group_w = sb("group_w", [C, 32])
        group = sb("group", [C, 32])
        gn = sb("gn", [C, 6])
        minus_half = sb("minus_half", [C, 1])

        ps_b = ctx.enter_context(nc.psum_tensor("ps_b", [128, L], F32))
        ps_c = ctx.enter_context(nc.psum_tensor("ps_c", [128, L], F32))
        ps_y = ctx.enter_context(nc.psum_tensor("ps_y", [128, L], F32))
        ps_w = ctx.enter_context(nc.psum_tensor("ps_w", [128, L], F32))

        names = """weights_in x_in consts w_conv_ready spread_ready a_exp_ready a_ready
            b_wide_ready c_psum_ready c_wide_ready decay_ready drive_ready hidden_ready prod_ready prod_summed
            xp_ready xc_ready z_ready gate_ready xdb_ready high_ready dt_low_ready rest_ready mid_ready
            parts_ready dt_psum_ready abs_ready exp_ready ln_ready relu_ready dt_ready dtx_ready
            y_taken gated_ready out_ready mixed_ready gn_step rstd_ready gn_ready act_ready x1_ready
            aggregate a_log_ready one_plus_ready lost_ready"""
        (weights_in, x_in, consts, w_conv_ready, spread_ready, a_exp_ready, a_ready,
         b_wide_ready, c_psum_ready, c_wide_ready, decay_ready, drive_ready, hidden_ready, prod_ready, prod_summed,
         xp_ready, xc_ready, z_ready, gate_ready, xdb_ready, high_ready, dt_low_ready, rest_ready, mid_ready,
         parts_ready, dt_psum_ready, abs_ready, exp_ready, ln_ready, relu_ready, dt_ready, dtx_ready,
         y_taken, gated_ready, out_ready, mixed_ready, gn_step, rstd_ready, gn_ready, act_ready, x1_ready,
         aggregate, a_log_ready, one_plus_ready, lost_ready) = [sem(name) for name in names.split()]
        GN_STEPS = 12
        WEIGHTS = 16 * (2 * 14 + 1)
        X_LOADS = 16 * 4
        CONSTS = 9 + 1 + PARTS

        def halves(t):
            return [t[:, h * H:(h + 1) * H] for h in range(L // H)]

        with nc.Block() as block:

            @block.sync
            def _(sp):
                for i, d in enumerate(DIRS):
                    for rows, tap in ((0, 1), (C, 0)):
                        sp.dma_start(w_in[i][rows:rows + C, :], ins[f"W_in_{d}"][:, 0:D]).then_inc(weights_in, 16)
                        sp.dma_start(taps[i][rows:rows + C, :],
                                     bass.AP(ins[f"conv_w_{d}"].tensor, tap * D, [[0, C], [1, D]])
                                     ).then_inc(weights_in, 16)
                    sp.dma_start(w_gate[i][0:C, :], ins[f"W_in_{d}"][:, D:]).then_inc(weights_in, 16)
                src = ins["x"].rearrange("b c t -> c b t")
                for i, d in enumerate(DIRS):
                    dst = x_pair[i].rearrange("c (b t) -> c b t", b=B)
                    sp.dma_start(dst[0:C, :, :], src).then_inc(x_in, 16)
                    if d == "f":
                        sp.dma_start(dst[C:, :, 1:L], src[:, :, 0:L - 1]).then_inc(x_in, 16)
                    else:
                        sp.dma_start(dst[C:, :, 0:L - 1], src[:, :, 1:L]).then_inc(x_in, 16)
                for i, d in enumerate(DIRS):
                    for k in range(PARTS):
                        sp.dma_start(w_x[i][:, BC * k:BC * (k + 1)],
                                     ins[f"W_x_{d}"][:, R:R + BC]).then_inc(weights_in, 16)
                    sp.dma_start(w_x[i][:, DT_ROW:], ins[f"W_x_{d}"][:, 0:R]).then_inc(weights_in, 16)
                    sp.dma_start(w_dt[i][DT_ROW:DT_ROW + R, :], ins[f"W_dt_{d}"]).then_inc(weights_in, 16)
                    sp.dma_start(w_dt[i][DT_ROW + R:DT_ROW + R + 1, :], ins[f"b_dt_{d}"]).then_inc(weights_in, 16)
                    sp.dma_start(w_out[i][:, :], ins[f"W_out_{d}"]).then_inc(weights_in, 16)
                    sp.dma_start(a_log[i][:, :], ins[f"A_log_{d}"]).then_inc(weights_in, 16)
                    sp.dma_start(cols[i][:, :], ins[f"cols_{d}"]).then_inc(weights_in, 16)
                sp.dma_start(gn_cols[:, :], ins["gn_cols"]).then_inc(weights_in, 16)

            @block.gpsimd
            def _(pool):
                shifted = [x.rearrange("c (b t) -> c b t", b=B)[C:, :, :] for x in x_pair]
                zeros = [shifted[0][:, :, 0:1], shifted[1][:, :, L - 1:L], w_gate[0][C:, :], w_gate[1][C:, :],
                         ident[:, :], pick[:, :], stats[:, :]]
                for i, part in enumerate(zeros):
                    nc.gpsimd.memset(part, 0.0).then_inc(consts, 1)
                    pool.wait_ge(consts, i + 1)
                nc.gpsimd.memset(minus_half[:, :], -0.5).then_inc(consts, 1)
                pool.wait_ge(consts, 8)
                nc.gpsimd.memset(dt_low[DT_ROW:, :], 1.0).then_inc(consts, 1)
                pool.wait_ge(consts, 9)
                nc.gpsimd.affine_select(out=ident[:, :], in_=ident[:, :], compare_op=ALU.not_equal, fill=1.0,
                                        base=0, pattern=[[-1, 128]], channel_multiplier=1).then_inc(consts, 1)
                for k in range(PARTS):
                    pool.wait_ge(consts, 10 + k)
                    nc.gpsimd.affine_select(out=pick[:, :], in_=pick[:, :], compare_op=ALU.not_equal, fill=1.0,
                                            base=-BC * k, pattern=[[-1, BC]], channel_multiplier=1).then_inc(consts, 1)

                def rstd(b):
                    pool.wait_ge(gn_step, GN_STEPS * b + 10)
                    nc.gpsimd.tensor_tensor(gn[:, 3:4], gn[:, 2:3], minus_half[:, :], ALU.pow).then_inc(rstd_ready, 1)

                def residual(b):
                    pool.wait_ge(act_ready, b + 1)
                    nc.gpsimd.tensor_tensor(x1[:, bass.ds(b * L, L)], mixed[:, :], x_pair[0][0:C, bass.ds(b * L, L)],
                                            ALU.add).then_inc(x1_ready, 1)

                def batch(b, first=False):
                    for i in range(2):
                        for s in range(N):
                            n, k = (2 * b + i) * N + s, i * N + s
                            pool.wait_ge(hidden_ready, n + 1)
                            pool.wait_ge(c_wide_ready, n + 1)
                            at_least(pool, prod_summed, n - PAIR + 1)
                            nc.gpsimd.tensor_tensor(prod[k % PAIR][:, :], hidden[k % DEEP][:, :],
                                                    c_wide[k % DEEP][:, :], ALU.mult).then_inc(prod_ready, 1)
                            if i == 0 and not first:
                                if s == 6:
                                    rstd(b - 1)
                                if s == 10:
                                    residual(b - 1)

                pool.wait_ge(x_in, X_LOADS)
                batch(0, first=True)
                with pool.Fori(1, B) as b:
                    batch(b)
                rstd(B - 1)
                residual(B - 1)

            @block.tensor
            def _(pe):
                def project(i, b, w, done):
                    for h, out in enumerate(halves(ps_w)):
                        mm = nc.tensor.matmul(out, w[:, :], x_pair[i][:, bass.ds(b * L + h * H, H)], start=True, stop=True)
                    mm.then_inc(done, 1)

                def conv_in(u, i, b):
                    at_least(pe, mixed_ready, b if i else b - 1)
                    at_least(pe, relu_ready, u)
                    project(i, b, w_conv[i], xp_ready)

                def gate_in(u, i, b):
                    pe.wait_ge(xc_ready, u + 1)
                    project(i, b, w_gate[i], z_ready)

                def low_rank(u, i):
                    pe.wait_ge(gate_ready, u + 1)
                    for h, out in enumerate(halves(ps_w)):
                        mm = nc.tensor.matmul(out[0:DT_ROW + R, :], w_x[i][:, :], halves(xc[i])[h], start=True, stop=True)
                    mm.then_inc(xdb_ready, 1)

                def dt_in(u, i):
                    pe.wait_ge(dt_low_ready, u + 1)
                    pe.wait_ge(rest_ready, u + 1)
                    for h, out in enumerate(halves(ps_w)):
                        mm = nc.tensor.matmul(out, w_dt[i][DT_ROW:DT_ROW + R + 1, :],
                                              halves(dt_low)[h][DT_ROW:DT_ROW + R + 1, :], start=True, stop=True)
                    mm.then_inc(dt_psum_ready, 1)

                def wide(n, s, i):
                    at_least(pe, drive_ready, n)
                    for h, out in enumerate(halves(ps_b)):
                        mm = nc.tensor.matmul(out, spread[:, s, :], halves(bc_parts[i])[h], start=True, stop=True)
                    mm.then_inc(b_wide_ready, 1)
                    at_least(pe, c_wide_ready, n)
                    for h, out in enumerate(halves(ps_c)):
                        mm = nc.tensor.matmul(out, spread[:, N + s, :], halves(bc_parts[i])[h], start=True, stop=True)
                    mm.then_inc(c_psum_ready, 1)

                def sum_states(n, k, u):
                    s = k % N
                    if s == 0:
                        at_least(pe, y_taken, u)
                    pe.wait_ge(prod_ready, n + 1)
                    for h, out in enumerate(halves(ps_y)):
                        mm = nc.tensor.matmul(out, ident[:, :], halves(prod[k % PAIR])[h], start=(s == 0), stop=(s == N - 1))
                    mm.then_inc(prod_summed, 1)

                def out_product(b):
                    pe.wait_ge(gated_ready, 2 * b + 2)
                    for h, out in enumerate(halves(ps_w)):
                        for i in range(2):
                            mm = nc.tensor.matmul(out[0:C, :], w_out[i][:, :], halves(gated[i])[h],
                                                  start=(i == 0), stop=(i == 1))
                    mm.then_inc(out_ready, 1)

                def batch(b, first=False, last=False):
                    for i in range(2):
                        u = 2 * b + i
                        pe.wait_ge(parts_ready, u + 1)
                        for s in range(N):
                            n, k = u * N + s, i * N + s
                            wide(n, s, i)
                            if not (first and k < Y_LAG):
                                sum_states(n - Y_LAG, (k - Y_LAG) % (2 * N), u if s >= Y_LAG else u - 1)
                            if i == 0 and s == 5 and not first:
                                out_product(b - 1)
                            if not (last and i == 1):
                                v, j, bv = u + 1, 1 - i, (b if i == 0 else b + 1)
                                if s == 6:
                                    conv_in(v, j, bv)
                                if s == 7:
                                    gate_in(v, j, bv)
                                if s == 8:
                                    low_rank(v, j)
                                if s == 10:
                                    dt_in(v, j)

                pe.wait_ge(x_in, X_LOADS)
                pe.wait_ge(consts, CONSTS)
                pe.wait_ge(w_conv_ready, 2)
                conv_in(0, 0, 0)
                gate_in(0, 0, 0)
                low_rank(0, 0)
                dt_in(0, 0)
                pe.wait_ge(spread_ready, 1)
                batch(0, first=True)
                with pe.Fori(1, B - 1) as b:
                    batch(b)
                batch(B - 1, last=True)
                for k in range(2 * N - Y_LAG, 2 * N):
                    sum_states(2 * N * (B - 1) + k, k, 2 * B - 1)
                out_product(B - 1)

            @block.scalar
            def _(act):
                def silus(u, i, norm=None):
                    act.wait_ge(xp_ready, u + 1)
                    at_least(act, y_taken, u - 1)
                    nc.scalar.activation(xc[i][:, :], ps_w[:, :], ACT.Silu, bias=cols[i][:, 0:1]).then_inc(xc_ready, 1)
                    act.wait_ge(z_ready, u + 1)
                    at_least(act, gated_ready, u - 1)
                    nc.scalar.activation(gate[i][:, :], ps_w[:, :], ACT.Silu).then_inc(gate_ready, 1)
                    if norm is not None:
                        norm_silu(norm)
                    nc.scalar.preload_act_table_set("natural_log_exp_and_others")

                def norm_silu(b):
                    act.wait_ge(gn_ready, b + 1)
                    nc.scalar.activation(mixed[:, :], mixed[:, :], ACT.Silu, scale=gn[:, 4:5],
                                         bias=gn[:, 5:6]).then_inc(act_ready, 1)

                def split_high(u, i):
                    act.wait_ge(xdb_ready, u + 1)
                    at_least(act, c_psum_ready, N * (u - 1))
                    nc.scalar.activation(bc_parts[i][:, :], ps_w[0:DT_ROW, :], ACT.Copy).then_inc(high_ready, 1)
                    at_least(act, dt_psum_ready, u)
                    nc.scalar.activation(dt_low[DT_ROW:DT_ROW + R, :], ps_w[DT_ROW:DT_ROW + R, :],
                                         ACT.Copy).then_inc(dt_low_ready, 1)

                def softplus(u, i):
                    act.wait_ge(dt_psum_ready, u + 1)
                    nc.scalar.activation(soft[:, :], ps_w[:, :], ACT.Abs).then_inc(abs_ready, 1)
                    act.wait_ge(abs_ready, u + 1)
                    nc.scalar.activation(soft[:, :], soft[:, :], ACT.Exp, scale=-1.0).then_inc(exp_ready, 1)
                    act.wait_ge(exp_ready, u + 2)
                    nc.scalar.activation(one_plus[:, :], soft[:, :], ACT.Identity, bias=1.0).then_inc(one_plus_ready, 1)
                    act.wait_ge(one_plus_ready, u + 1)
                    at_least(act, decay_ready, N * (u - 1))
                    at_least(act, dtx_ready, u - 1)
                    nc.scalar.activation(dt[i][:, :], one_plus[:, :], ACT.Ln).then_inc(ln_ready, 1)

                def state(n, k, i, s):
                    at_least(act, hidden_ready, n - DEEP + 1)
                    nc.scalar.activation(decay[k % DEEP][:, :], dt[i][:, :], ACT.Exp,
                                         scale=a_neg[i][:, s:s + 1]).then_inc(decay_ready, 1)
                    act.wait_ge(c_psum_ready, n + 1)
                    at_least(act, prod_ready, n - DEEP + 1)
                    nc.scalar.activation(c_wide[k % DEEP][:, :], ps_c[:, :], ACT.Copy).then_inc(c_wide_ready, 1)

                def batch(b, first=False, last=False):
                    for i in range(2):
                        u = 2 * b + i
                        act.wait_ge(dt_ready, u + 1)
                        for s in range(N):
                            state(u * N + s, i * N + s, i, s)
                            if last and i == 1:
                                continue
                            if s == 6:
                                silus(u + 1, 1 - i, norm=(b - 1 if i == 0 and not first else None))
                            if s == 8:
                                split_high(u + 1, 1 - i)
                            if s == 10:
                                softplus(u + 1, 1 - i)

                act.wait_ge(weights_in, WEIGHTS)
                act.wait_ge(a_log_ready, 2)
                nc.scalar.preload_act_table_set("natural_log_exp_and_others")
                for i in range(2):
                    last = nc.scalar.activation(a_neg[i][:, :], a_log[i][:, :], ACT.Exp)
                last.then_inc(exp_ready, 1)
                silus(0, 0)
                split_high(0, 0)
                softplus(0, 0)
                act.wait_ge(a_ready, 2)
                batch(0, first=True)
                with act.Fori(1, B - 1) as b:
                    batch(b)
                batch(B - 1, last=True)
                norm_silu(B - 1)

            @block.vector
            def _(dve):
                def split_low(u, i):
                    dve.wait_ge(high_ready, u + 1)
                    dve.wait_ge(dt_low_ready, u + 1)
                    at_least(dve, gated_ready, u - 1)
                    nc.vector.tensor_tensor(scratch[0:2 * BC, :], ps_w[0:2 * BC, :], bc_parts[i][0:2 * BC, :],
                                            ALU.subtract).then_inc(rest_ready, 1)

                def split_mid(u, i):
                    dve.wait_ge(rest_ready, u + 1)
                    nc.vector.tensor_copy(bc_parts[i][0:2 * BC, :], scratch[0:2 * BC, :]).then_inc(mid_ready, 1)

                def split_last(u, i):
                    dve.wait_ge(mid_ready, u + 1)
                    nc.vector.tensor_tensor(bc_parts[i][0:BC, :], scratch[0:BC, :], bc_parts[i][0:BC, :],
                                            ALU.subtract).then_inc(parts_ready, 1)

                def lost(u, i):
                    dve.wait_ge(one_plus_ready, u + 1)
                    dve.wait_ge(parts_ready, u + 1)
                    nc.vector.scalar_tensor_tensor(out=scratch[:, :], in0=one_plus[:, :], scalar=-1.0, in1=soft[:, :],
                                                   op0=ALU.add, op1=ALU.subtract).then_inc(lost_ready, 1)

                def relu(u, i):
                    dve.wait_ge(lost_ready, u + 1)
                    nc.vector.scalar_tensor_tensor(out=scratch[:, :], in0=ps_w[:, :], scalar=0.0, in1=scratch[:, :],
                                                   op0=ALU.max, op1=ALU.subtract).then_inc(relu_ready, 1)

                def dt_sum(u, i):
                    dve.wait_ge(ln_ready, u + 1)
                    dve.wait_ge(relu_ready, u + 1)
                    nc.vector.tensor_tensor(dt[i][:, :], scratch[:, :], dt[i][:, :], ALU.add).then_inc(dt_ready, 1)

                def dt_x(u, i):
                    dve.wait_ge(dt_ready, u + 1)
                    at_least(dve, drive_ready, N * (u - 1))
                    nc.vector.tensor_tensor(dtx[i][:, :], dt[i][:, :], xc[i][:, :], ALU.mult).then_inc(dtx_ready, 1)

                def take_y(u, i, last=False):
                    dve.wait_ge(prod_summed, N * (u + 1))
                    if not last:
                        dve.wait_ge(dt_ready, u + 2)
                    nc.vector.scalar_tensor_tensor(out=scratch[:, :], in0=xc[i][:, :], scalar=cols[i][:, 1:2],
                                                   in1=ps_y[:, :], op0=ALU.mult, op1=ALU.add).then_inc(y_taken, 1)

                def drive_step(n, k, i):
                    dve.wait_ge(b_wide_ready, n + 1)
                    at_least(dve, hidden_ready, n - PAIR + 1)
                    nc.vector.tensor_tensor(drive[k % PAIR][:, :], dtx[i][:, :], ps_b[:, :], ALU.mult).then_inc(drive_ready, 1)

                def scan_step(n, k):
                    dve.wait_ge(decay_ready, n + 1)
                    dve.wait_ge(drive_ready, n + 1)
                    at_least(dve, prod_ready, n - DEEP + 1)
                    order = slice(None) if k < N else slice(None, None, -1)
                    nc.vector.tensor_tensor_scan(hidden[k % DEEP][:, order], decay[k % DEEP][:, order],
                                                 drive[k % PAIR][:, order], 0.0, ALU.mult,
                                                 ALU.add).then_inc(hidden_ready, 1)

                def chain(step, instruction):
                    instruction.then_inc(gn_step, 1)
                    dve.wait_ge(gn_step, step)

                def norm_stats(b):
                    at = GN_STEPS * b
                    dve.wait_ge(out_ready, b + 1)
                    at_least(dve, x1_ready, b)
                    nc.vector.tensor_copy(mixed[:, :], ps_w[0:C, :]).then_inc(mixed_ready, 1)
                    dve.wait_ge(mixed_ready, b + 1)
                    for h, part in enumerate(halves(mixed)):
                        chain(at + h + 1, nc.vector.bn_stats(bn[:, h, :], part))
                    dve.sem_inc(aggregate, 1)
                    chain(at + 3, nc.vector.bn_aggr(stats[:, 0:2], bn[:, :, :].rearrange("c a b -> c (a b)")))
                    chain(at + 4, nc.vector.scalar_tensor_tensor(out=stats[:, 1:2], in0=stats[:, 0:1],
                                                                 scalar=stats[:, 0:1], in1=stats[:, 1:2],
                                                                 op0=ALU.mult, op1=ALU.add))
                    chain(at + 5, nc.vector.transpose(stats_t[:, :], stats[:, :]))
                    chain(at + 6, nc.vector.tensor_reduce(group_t[:, :],
                                                          stats_t[:, :].rearrange("c (g k) -> c g k", k=GROUP),
                                                          AX.X, ALU.add))
                    chain(at + 7, nc.vector.tensor_scalar(group_w[:, :].rearrange("c (g k) -> c g k", k=GROUP),
                                                          group_t[:, :].unsqueeze(2).to_broadcast([C, 2, GROUP]),
                                                          1.0 / GROUP, None, ALU.mult))
                    chain(at + 8, nc.vector.transpose(group[:, :], group_w[:, :]))
                    chain(at + 9, nc.vector.tensor_scalar(gn[:, 1:2], group[:, 0:1], group[:, 0:1], -1.0, ALU.mult, ALU.mult))
                    chain(at + 10, nc.vector.tensor_scalar(gn[:, 2:3], gn[:, 1:2], group[:, 1:2], GN_EPS, ALU.add, ALU.add))

                def norm_scale(b):
                    at = GN_STEPS * b
                    dve.wait_ge(rstd_ready, b + 1)
                    chain(at + 11, nc.vector.tensor_scalar(gn[:, 4:5], gn[:, 3:4], gn_cols[:, 0:1], None, ALU.mult))
                    chain(at + 12, nc.vector.tensor_scalar(gn[:, 1:2], group[:, 0:1], gn[:, 4:5], -1.0, ALU.mult, ALU.mult))
                    nc.vector.tensor_scalar(gn[:, 5:6], gn[:, 1:2], gn_cols[:, 1:2], None, ALU.add).then_inc(gn_ready, 1)

                def batch(b, first=False, last=False):
                    for i in range(2):
                        u = 2 * b + i
                        dve.wait_ge(dtx_ready, u + 1)
                        for s in range(N):
                            n, k = u * N + s, i * N + s
                            drive_step(n, k, i)
                            if not (first and k == 0):
                                scan_step(n - 1, (k - 1) % (2 * N))
                            if not (first and i == 0):
                                if s == 3:
                                    take_y(u - 1, 1 - i)
                                if s == 4:
                                    gate_of(u - 1, 1 - i, b)
                                if s == 6 and i == 0:
                                    norm_stats(b - 1)
                                if s == 7 and i == 0:
                                    norm_scale(b - 1)
                            if last and i == 1:
                                continue
                            for at, step in ((9, split_low), (10, split_mid), (11, split_last),
                                             (12, lost), (13, relu), (14, dt_sum), (15, dt_x)):
                                if s == at:
                                    step(u + 1, 1 - i)

                def gate_of(u, i, b):
                    dve.wait_ge(y_taken, u + 1)
                    at_least(dve, out_ready, b if i == 0 else b - 1)
                    nc.vector.tensor_tensor(gated[i][:, :], scratch[:, :], gate[i][:, :], ALU.mult).then_inc(gated_ready, 1)

                dve.wait_ge(weights_in, WEIGHTS)
                for i in range(2):
                    nc.vector.tensor_scalar(a_log[i][:, :], a_log[i][:, :], A_LOG_MAX, None, ALU.min).then_inc(a_log_ready, 1)
                for i in range(2):
                    nc.vector.tensor_tensor(w_conv[i][:, :], w_in[i][:, :], taps[i][:, :],
                                            ALU.mult).then_inc(w_conv_ready, 1)
                dve.wait_ge(consts, CONSTS)
                nc.vector.tensor_copy(spread[:, :, :], pick[:, :].unsqueeze(2).to_broadcast([DT_ROW, BC, 128])
                                      ).then_inc(spread_ready, 1)
                dve.wait_ge(exp_ready, 1)
                for i in range(2):
                    nc.vector.tensor_scalar(a_neg[i][:, :], a_neg[i][:, :], -1.0, None, ALU.mult).then_inc(a_ready, 1)
                for step in (split_low, split_mid, split_last, lost, relu, dt_sum, dt_x):
                    step(0, 0)
                batch(0, first=True)
                with dve.Fori(1, B - 1) as b:
                    batch(b)
                batch(B - 1, last=True)
                u = 2 * B - 1
                scan_step(N * (u + 1) - 1, 2 * N - 1)
                take_y(u, 1, last=True)
                gate_of(u, 1, B)
                norm_stats(B - 1)
                norm_scale(B - 1)


def layer_norm_steps(nc, dve, chain, at, v, cen, sq, small):
    wide = [128, TILES, C]
    chain(at + 1, nc.vector.tensor_reduce(small[:, 0, :], v, AX.X, ALU.add))
    chain(at + 2, nc.vector.scalar_tensor_tensor(out=cen, in0=small[:, 0, :].unsqueeze(2).to_broadcast(wide),
                                                 scalar=-1.0 / C, in1=v, op0=ALU.mult, op1=ALU.add))
    chain(at + 3, nc.vector.tensor_tensor(sq, cen, cen, ALU.mult))
    chain(at + 4, nc.vector.tensor_reduce(small[:, 1, :], sq, AX.X, ALU.add))
    chain(at + 5, nc.vector.tensor_scalar(small[:, 1, :], small[:, 1, :], 1.0 / C, LN_EPS, ALU.mult, ALU.add))


def attention_stage(nc, ins, x1, x2, u_all, u_high, u_low):
    with ExitStack() as ctx:
        def sb(name, shape, dt=F32):
            return ctx.enter_context(nc.sbuf_tensor(name, shape, dt))

        def sem(name):
            return ctx.enter_context(nc.semaphore(name))

        ident = sb("ident2", [128, 128])
        ident_bf = sb("ident_bf", [128, 128], BF16)
        mask = sb("mask", [128, 2, 2, 128], BF16)
        wq, wk, wv = (sb(name, [C, C]) for name in ("wq", "wk", "wv"))
        xs = sb("xs", [C, L])
        tok = sb("tok", [128, TILES, C])
        cen = sb("cen", [128, TILES, C])
        sq = sb("sq", [128, TILES, C])
        xn = sb("xn", [128, TILES, C])
        small = sb("small", [128, 3, TILES])
        small2 = sb("small2", [128, 3, TILES])
        minus_half = sb("minus_half2", [128, TILES])
        xn_t = sb("xn_t", [C, L])
        q_t = sb("q_t", [C, L])
        k_t = sb("k_t", [C, L])
        v_one = sb("v_one", [128, TILES, C + 1])
        probs = [sb(f"probs_{i}", [128, L]) for i in range(2)]
        probs_t = [sb(f"probs_t_{i}", [128, H]) for i in range(2)]
        neg_max = sb("neg_max", [128, TILES])
        inv = sb("inv", [128, TILES])
        tok2 = sb("tok2", [128, TILES, C])

        ps_s = [ctx.enter_context(nc.psum_tensor(f"ps_s{i}", [128, L], F32)) for i in range(2)]
        ps_t = [ctx.enter_context(nc.psum_tensor(f"ps_t{i}", [128, H], F32)) for i in range(2)]
        ps_o = [ctx.enter_context(nc.psum_tensor(f"ps_o{i}", [128, H], F32)) for i in range(2)]

        names = """qkv_in a_consts xs_ready tok_psum tok_ready ln_step ln_rstd xn_ready xnt_psum xnt_ready
            q_psum q_ready k_psum k_ready v_psum v_ready scores_ready max_ready probs_ready pt_psum pt_ready
            inv_ready pt_used tok2_ready ln2_step ln2_rstd u_ready u_high_ready u_low_ready x2_ready passed"""
        (qkv_in, a_consts, xs_ready, tok_psum, tok_ready, ln_step, ln_rstd, xn_ready, xnt_psum, xnt_ready,
         q_psum, q_ready, k_psum, k_ready, v_psum, v_ready, scores_ready, max_ready, probs_ready, pt_psum, pt_ready,
         inv_ready, pt_used, tok2_ready, ln2_step, ln2_rstd, u_ready, u_high_ready, u_low_ready, x2_ready, passed,
         ) = [sem(name) for name in names.split()]
        LN = 5
        MASKED = -1e30

        def width(i):
            return (i // 2 + 1) * SPAN

        groups = [[(i, g, min(4, width(i) // 128 - g)) for g in range(0, width(i) // 128, 4)] for i in range(TILES)]
        GROUPS = sum(len(g) for g in groups)

        def halves(t):
            return [t[:, h * H:(h + 1) * H] for h in range(L // H)]

        def batches(engine, batch):
            batch(0)
            with engine.Fori(1, B) as b:
                batch(b)

        with nc.Block() as block:

            @block.sync
            def _(sp):
                for w, name in ((wq, "Wq"), (wk, "Wk"), (wv, "Wv")):
                    sp.dma_start(w[:, :], ins[name]).then_inc(qkv_in, 16)

            @block.gpsimd
            def _(pool):
                nc.gpsimd.memset(ident[:, :], 0.0).then_inc(a_consts, 1)
                nc.gpsimd.memset(mask[:, :, :, :], 0.0).then_inc(a_consts, 1)
                nc.gpsimd.memset(minus_half[:, :], -0.5).then_inc(a_consts, 1)
                nc.gpsimd.memset(v_one[:, :, C:C + 1], 1.0).then_inc(a_consts, 1)
                pool.wait_ge(a_consts, 4)
                nc.gpsimd.affine_select(out=ident[:, :], in_=ident[:, :], compare_op=ALU.not_equal, fill=1.0,
                                        base=0, pattern=[[-1, 128]], channel_multiplier=1).then_inc(a_consts, 1)
                for parity in range(2):
                    pool.wait_ge(a_consts, 5 + parity)
                    nc.gpsimd.affine_select(out=mask[:, parity, :, :], in_=mask[:, parity, :, :],
                                            compare_op=ALU.is_ge, fill=MASKED, base=parity,
                                            pattern=[[-1, 2], [-2, 128]], channel_multiplier=2).then_inc(a_consts, 1)
                pool.wait_ge(a_consts, 7)
                nc.gpsimd.tensor_copy(ident_bf[:, :], ident[:, :]).then_inc(a_consts, 1)

                def batch(b):
                    pool.wait_ge(ln_step, LN * b + LN)
                    nc.gpsimd.tensor_tensor(small[:, 2, :], small[:, 1, :], minus_half[:, :], ALU.pow).then_inc(ln_rstd, 1)
                    pool.wait_ge(ln2_step, LN * b + LN)
                    nc.gpsimd.tensor_tensor(small2[:, 2, :], small2[:, 1, :], minus_half[:, :], ALU.pow).then_inc(ln2_rstd, 1)

                batches(pool, batch)

            @block.tensor
            def _(pe):
                def batch(b):
                    pe.wait_ge(xs_ready, b + 1)
                    at_least(pe, inv_ready, TILES * b)
                    at_least(pe, tok2_ready, TILES * b)
                    pe.sem_inc(passed, 1)
                    for i in range(TILES):
                        delta, parity = divmod(i, 2)
                        rows = xs[:, SPAN * delta + parity:SPAN * (delta + 1):2]
                        mm = nc.tensor.transpose(ps_o[0][:, i * C:(i + 1) * C], rows, ident[0:C, 0:C])
                    mm.then_inc(tok_psum, 1)
                    pe.wait_ge(xn_ready, b + 1)
                    at_least(pe, probs_ready, TILES * b)
                    pe.sem_inc(passed, 1)
                    for i in range(TILES):
                        mm = nc.tensor.transpose(ps_s[0][0:C, i * 128:(i + 1) * 128], xn[:, i, :], ident[:, :])
                    mm.then_inc(xnt_psum, 1)
                    pe.wait_ge(xnt_ready, b + 1)
                    pe.sem_inc(passed, 1)
                    for out, w, done in ((ps_s[1], wq, q_psum), (ps_s[0], wk, k_psum)):
                        for h in range(2):
                            mm = nc.tensor.matmul(out[0:C, h * H:(h + 1) * H], w[:, :], halves(xn_t)[h], start=True, stop=True)
                        mm.then_inc(done, 1)
                    pe.wait_ge(tok_ready, b + 1)
                    for i in range(TILES):
                        mm = nc.tensor.matmul(ps_o[0][:, i * C:(i + 1) * C], xn_t[:, i * 128:(i + 1) * 128], wv[:, :],
                                              start=True, stop=True)
                    mm.then_inc(v_psum, 1)

                    def scores(i):
                        pe.wait_ge(q_ready, b + 1)
                        pe.wait_ge(k_ready, b + 1)
                        if i >= 2:
                            pe.wait_ge(probs_ready, TILES * b + i - 1)
                        for at in range(0, width(i), H):
                            n = min(H, width(i) - at)
                            last = at + n == width(i)
                            mm = nc.tensor.matmul(ps_s[i % 2][:, at:at + n], q_t[:, i * 128:(i + 1) * 128],
                                                  k_t[:, at:at + n], start=True, stop=not last)
                        mm = nc.tensor.matmul(ps_s[i % 2][:, width(i) - SPAN:width(i)], ident_bf[:, :],
                                              mask[:, i % 2, :, :].rearrange("p a b -> p (a b)"), start=False, stop=True)
                        mm.then_inc(scores_ready, 1)

                    def attend(i):
                        pe.wait_ge(probs_ready, TILES * b + i + 1)
                        first = GROUPS * b + sum(len(g) for g in groups[:i])
                        for j, (_, at, n) in enumerate(groups[i]):
                            g = first + j
                            slot = (sum(len(x) for x in groups[:i]) + j) % 2
                            at_least(pe, pt_ready, g - 1)
                            for m in range(n):
                                mm = nc.tensor.transpose(ps_t[slot][:, m * 128:(m + 1) * 128],
                                                         probs[i % 2][:, (at + m) * 128:(at + m + 1) * 128], ident[:, :])
                            mm.then_inc(pt_psum, 1)
                        if i == 0:
                            pe.wait_ge(v_ready, b + 1)
                        if i >= 2:
                            pe.wait_ge(tok2_ready, TILES * b + i - 1)
                        for j, (_, at, n) in enumerate(groups[i]):
                            g = first + j
                            slot = (sum(len(x) for x in groups[:i]) + j) % 2
                            pe.wait_ge(pt_ready, g + 1)
                            for m in range(n):
                                mm = nc.tensor.matmul(ps_o[i % 2][:, 0:C + 1], probs_t[slot][:, m * 128:(m + 1) * 128],
                                                      v_one[:, at + m, :], start=(at + m == 0),
                                                      stop=(at + m + 1 == width(i) // 128))
                            mm.then_inc(pt_used, 1)

                    scores(0)
                    for i in range(TILES):
                        if i + 1 < TILES:
                            scores(i + 1)
                        attend(i)

                pe.wait_ge(qkv_in, 48)
                pe.wait_ge(a_consts, 8)
                batches(pe, batch)

            @block.scalar
            def _(act):
                def batch(b):
                    at_least(act, tok_psum, b)
                    nc.scalar.activation(xs[:, :], x1[:, bass.ds(b * L, L)], ACT.Copy).then_inc(xs_ready, 1)
                    act.wait_ge(tok_psum, b + 1)
                    at_least(act, tok2_ready, TILES * b)
                    nc.scalar.activation(tok[:, :, :].rearrange("p i c -> p (i c)"), ps_o[0][:, :],
                                         ACT.Copy).then_inc(tok_ready, 1)
                    act.wait_ge(xnt_psum, b + 1)
                    nc.scalar.activation(xn_t[:, :], ps_s[0][0:C, :], ACT.Copy).then_inc(xnt_ready, 1)
                    act.wait_ge(q_psum, b + 1)
                    nc.scalar.activation(q_t[:, :], ps_s[1][0:C, :], ACT.Copy, scale=float(C) ** -0.5).then_inc(q_ready, 1)
                    for i in range(TILES):
                        act.wait_ge(max_ready, TILES * b + i + 1)
                        nc.scalar.activation(probs[i % 2][:, 0:width(i)], ps_s[i % 2][:, 0:width(i)], ACT.Exp,
                                             bias=neg_max[:, i:i + 1]).then_inc(probs_ready, 1)
                    act.wait_ge(u_ready, b + 1)
                    nc.scalar.activation(x2[:, :, bass.ds(b, 1), :].rearrange("p i o c -> p i (o c)"), tok2[:, :, :],
                                         ACT.Copy).then_inc(x2_ready, 1)
                    nc.scalar.activation(u_all[:, :, bass.ds(b, 1), :].rearrange("p i o c -> p i (o c)"), xn[:, :, :],
                                         ACT.Copy).then_inc(x2_ready, 1)

                batches(act, batch)

            @block.vector
            def _(dve):
                def step(semaphore):
                    def chain(count, instruction):
                        instruction.then_inc(semaphore, 1)
                        dve.wait_ge(semaphore, count)
                    return chain

                def batch(b):
                    dve.wait_ge(tok_ready, b + 1)
                    layer_norm_steps(nc, dve, step(ln_step), LN * b, tok[:, :, :], cen[:, :, :], sq[:, :, :], small)
                    dve.wait_ge(ln_rstd, b + 1)
                    at_least(dve, x2_ready, 2 * b)
                    nc.vector.tensor_tensor(xn[:, :, :], cen[:, :, :],
                                            small[:, 2, :].unsqueeze(2).to_broadcast([128, TILES, C]),
                                            ALU.mult).then_inc(xn_ready, 1)
                    dve.wait_ge(k_psum, b + 1)
                    nc.vector.tensor_copy(k_t[:, :], ps_s[0][0:C, :]).then_inc(k_ready, 1)
                    dve.wait_ge(v_psum, b + 1)
                    nc.vector.tensor_copy(v_one[:, :, 0:C], ps_o[0][:, :].rearrange("p (i c) -> p i c", i=TILES)
                                          ).then_inc(v_ready, 1)

                    def max_step(i):
                        dve.wait_ge(scores_ready, TILES * b + i + 1)
                        nc.vector.tensor_reduce(neg_max[:, i:i + 1], ps_s[i % 2][:, 0:width(i)], AX.X, ALU.max,
                                                negate=True).then_inc(max_ready, 1)

                    max_step(0)
                    for i in range(TILES):
                        if i + 1 < TILES:
                            max_step(i + 1)
                        for j, (_, at, n) in enumerate(groups[i]):
                            k = sum(len(x) for x in groups[:i]) + j
                            g = GROUPS * b + k
                            dve.wait_ge(pt_psum, g + 1)
                            at_least(dve, pt_used, g - 1)
                            nc.vector.tensor_copy(probs_t[k % 2][:, 0:n * 128], ps_t[k % 2][:, 0:n * 128]).then_inc(pt_ready, 1)
                        dve.wait_ge(pt_used, GROUPS * b + sum(len(x) for x in groups[:i + 1]))
                        nc.vector.reciprocal(inv[:, i:i + 1], ps_o[i % 2][:, C:C + 1]).then_inc(inv_ready, 1)
                        dve.wait_ge(inv_ready, TILES * b + i + 1)
                        nc.vector.scalar_tensor_tensor(out=tok2[:, i, :], in0=ps_o[i % 2][:, 0:C], scalar=inv[:, i:i + 1],
                                                       in1=tok[:, i, :], op0=ALU.mult, op1=ALU.add).then_inc(tok2_ready, 1)
                    dve.wait_ge(tok2_ready, TILES * (b + 1))
                    layer_norm_steps(nc, dve, step(ln2_step), LN * b, tok2[:, :, :], cen[:, :, :], sq[:, :, :], small2)
                    dve.wait_ge(ln2_rstd, b + 1)
                    nc.vector.tensor_tensor(xn[:, :, :], cen[:, :, :],
                                            small2[:, 2, :].unsqueeze(2).to_broadcast([128, TILES, C]),
                                            ALU.mult).then_inc(u_ready, 1)
                    dve.wait_ge(u_ready, b + 1)
                    high = u_high[:, :, bass.ds(b, 1), :].rearrange("p i o c -> p i (o c)")
                    nc.vector.tensor_copy(high, xn[:, :, :]).then_inc(u_high_ready, 1)
                    dve.wait_ge(u_high_ready, b + 1)
                    nc.vector.tensor_tensor(u_low[:, :, bass.ds(b, 1), :].rearrange("p i o c -> p i (o c)"), xn[:, :, :],
                                            high.bitcast(F32), ALU.subtract).then_inc(u_low_ready, 1)

                batches(dve, batch)


def expert_stage(nc, ins, x2, u_all, u_high, u_low, out):
    PADS = 640
    EVEN_HIGH, EVEN_LOW, ODD_HIGH, ODD_LOW = range(4)
    BANDS = [(0, L // 16, 3), (L // 16, L // 8, 2), (L // 8, L // 4, 1), (L // 4, L // 2, 0)]
    TERMS = [(0, 0), (1, 0), (0, 1)]
    PAIRS = B // 2

    with ExitStack() as ctx:
        def sb(name, shape, dt=F32):
            return ctx.enter_context(nc.sbuf_tensor(name, shape, dt))

        def sem(name):
            return ctx.enter_context(nc.semaphore(name))

        filters = nc.dram_tensor("filters", (FILTERS, 4, PADS), F32, kind="Internal").ap()
        plus = sb("plus", [128, EXPERTS, FILTERS, C])
        minus = sb("minus", [128, EXPERTS, FILTERS, C])
        taps = sb("taps", [128, EXPERTS, AR_TAPS, C])
        mixes = sb("mixes", [128, FILTERS, EXPERTS, 2, C])
        logits = sb("logits", [128, 2, EXPERTS])
        sig = sb("sig", [128, FILTERS])
        quarter = sb("quarter", [128, FILTERS])
        sig4 = sb("sig4", [128, FILTERS])
        w = sb("w", [128, 8, EXPERTS])
        wk = sb("w_sigma", [128, EXPERTS, FILTERS])
        ident = sb("ident3", [128, 128])
        phi = sb("phi", [FILTERS, L])
        rows = sb("rows", [FILTERS, 4, PADS], F32R)
        hankel = [sb(f"hankel_{i}", [128, 4, H + 2], F32R) for i in range(2)]
        block_mix = [sb(f"block_mix_{i}", [128, EXPERTS, 2, 2, 128], F32R) for i in range(2)]
        ar_mix = sb("ar_mix", [128, EXPERTS, AR_TAPS, 2, 128], F32R)
        u_t = [[sb(f"u_t_{q}_{part}", [128, 2, H + 2], F32R) for part in range(2)] for q in range(PAIRS)]
        conv = [[sb(f"conv_{i}_{part}", [128, 2, H], F32R) for part in range(2)] for i in range(2)]
        spent = plus.rearrange("p i k e -> p (i k e)")
        result = [spent[:, q * L:(q + 1) * L] for q in range(PAIRS)]

        ps_conv = [ctx.enter_context(nc.psum_tensor(f"ps_conv{i}", [128, 2 * H], F32)) for i in range(2)]
        ps_out = [[ctx.enter_context(nc.psum_tensor(f"ps_out{q}{a}", [128, H], F32)) for a in range(2)]
                  for q in range(PAIRS)]

        names = """in3 consts3 w_step sig_ready wk_ready cum_step mixes_ready rows_step rows_ready filters_out
            ut_psum ut_high ut_low block_step block_ready conv_psum conv_high conv_low mixed_in
            result_ready out_done ar_step passed3"""
        (in3, consts3, w_step, sig_ready, wk_ready, cum_step, mixes_ready, rows_step, rows_ready, filters_out,
         ut_psum, ut_high, ut_low, block_step, block_ready, conv_psum, conv_high, conv_low, mixed_in,
         result_ready, out_done, ar_step, passed3) = [sem(name) for name in names.split()]
        hankel_in = [sem(f"hankel_in_{i}") for i in range(2)]
        STEPS = 2 * PAIRS
        IN3 = 16 * (2 + 1 + 2 * 3 + 1)

        with nc.Block() as block:

            @block.sync
            def _(sp):
                for j, name in enumerate(("log_weights", "gumbel")):
                    sp.dma_start(logits[:, j, :], bass.AP(ins[name].tensor, 0, [[0, 128], [1, EXPERTS]])).then_inc(in3, 16)
                sp.dma_start(sig[:, :], bass.AP(ins["sigma"].tensor, 0, [[0, 128], [1, FILTERS]])).then_inc(in3, 16)
                sp.dma_start(phi[:, :], ins["phi"][:, 0:L]).then_inc(in3, 16)
                for half in (0, C):
                    for dst, name in ((plus, "M_phi_plus"), (minus, "M_phi_minus"), (taps, "M_u")):
                        sp.dma_start(dst[half:half + C, :, :, :], ins[name].rearrange("i k d e -> d i k e")).then_inc(in3, 16)
                sp.wait_ge(rows_ready, 4)
                sp.dma_start(filters.rearrange("k r j -> k (r j)"), rows[:, :, :].bitcast(F32).rearrange("k r j -> k (r j)")).then_inc(filters_out, 16)
                sp.wait_ge(filters_out, 16)

                def load(k, slot):
                    sp.dma_start(hankel[slot][:, :, 0:H + 1].bitcast(F32),
                                 bass.AP(filters.tensor, k * 4 * PADS, [[1, 128], [PADS, 4], [1, H + 1]])).then_inc(hankel_in[slot], 16)

                load(0, 0)
                load(1, 1)
                with sp.Fori(1, FILTERS // 2) as pair:
                    for slot in range(2):
                        k = 2 * pair + slot
                        sp.wait_ge(conv_psum, STEPS * (k - 1))
                        load(k, slot)
                for q in range(PAIRS):
                    sp.wait_ge(result_ready, 2 * (q + 1))
                    sp.dma_start(out.rearrange("b c t -> (b c) t")[128 * q:128 * (q + 1), :], result[q][:, :]).then_inc(out_done, 16)
                sp.wait_ge(out_done, 16 * PAIRS)

            @block.gpsimd
            def _(pool):
                nc.gpsimd.memset(quarter[:, :], 0.25).then_inc(consts3, 1)
                nc.gpsimd.memset(ident[:, :], 0.0).then_inc(consts3, 1)
                pool.wait_ge(consts3, 2)
                nc.gpsimd.affine_select(out=ident[:, :], in_=ident[:, :], compare_op=ALU.not_equal, fill=1.0,
                                        base=0, pattern=[[-1, 128]], channel_multiplier=1).then_inc(consts3, 1)
                pool.wait_ge(in3, IN3)
                nc.gpsimd.tensor_tensor(sig4[:, :], sig[:, :], quarter[:, :], ALU.pow).then_inc(sig_ready, 1)
                for i in range(2):
                    nc.gpsimd.memset(block_mix[i][:, :, :, :, :].bitcast(F32), 0.0).then_inc(consts3, 1)
                for q in range(PAIRS):
                    for part in range(2):
                        nc.gpsimd.memset(u_t[q][part][:, :, 0:2].bitcast(F32), 0.0).then_inc(consts3, 1)
                pool.wait_ge(consts3, 3 + 2 + 2 * PAIRS)

                def blocks(slot, source, count):
                    for half in (0, C):
                        dst = block_mix[slot][half:half + C, :, :, :, half:half + C]
                        src = source[half:half + C]
                        nc.gpsimd.tensor_copy(dst[:, :, :, 0, :], src).then_inc(block_step, 1)
                    pool.wait_ge(block_step, count + 2)
                    pool.sem_inc(passed3, 1)
                    for half in (0, C):
                        dst = block_mix[slot][half:half + C, :, :, :, half:half + C]
                        nc.gpsimd.tensor_tensor(dst[:, :, :, 1, :], source[half:half + C], dst[:, :, :, 0, :].bitcast(F32),
                                                ALU.subtract).then_inc(block_ready, 1)

                def filter_blocks(k, slot):
                    blocks(slot, mixes[:, bass.ds(k, 1), :, :, :].rearrange("p o n m e -> p (o n) m e"), 2 * k)

                pool.wait_ge(mixes_ready, 2)
                filter_blocks(0, 0)
                filter_blocks(1, 1)
                with pool.Fori(1, FILTERS // 2) as pair:
                    for slot in range(2):
                        k = 2 * pair + slot
                        pool.wait_ge(mixed_in, STEPS * (k - 1))
                        pool.wait_ge(block_ready, 2 * k)
                        filter_blocks(k, slot)

            @block.tensor
            def _(pe):
                pairs = [[part[:, :, 2 * q:2 * q + 2, :].rearrange("p i b c -> p i (b c)") for part in (u_high, u_low)]
                         for q in range(PAIRS)]
                fresh = [[True, True] for q in range(PAIRS)]

                def add_out(q, a, lo, hi, w_block, data):
                    mm = nc.tensor.matmul(ps_out[q][a][:, lo:hi], w_block, data, start=fresh[q][a], stop=True,
                                          skip_group_check=True)
                    fresh[q][a] = False
                    return mm

                def convolve(k, slot, q, a, at):
                    dst = ps_conv[at % 2]
                    for lag in range(2):
                        parity = a ^ lag
                        shift = 1 if lag and not a else 0
                        for delta in range(SPANS):
                            first = 128 * delta
                            for n, (wp, dp) in enumerate(TERMS):
                                row = hankel[slot][:, 2 * lag + dp, first + shift:H + shift][:, ::-1]
                                mm = nc.tensor.matmul(dst[:, lag * H + first:(lag + 1) * H],
                                                      pairs[q][wp][:, 2 * delta + parity, :], row,
                                                      start=(delta == 0 and n == 0),
                                                      stop=(delta == SPANS - 1 and n == len(TERMS) - 1))
                    mm.then_inc(conv_psum, 1)

                def mix(slot, q, a, at):
                    for lag in range(2):
                        for lo, hi, band in BANDS:
                            for wp, dp in TERMS:
                                mm = add_out(q, a, lo, hi, block_mix[slot][:, band, lag, wp, :],
                                             conv[at % 2][dp][:, lag, lo:hi])
                    mm.then_inc(mixed_in, 1)

                pe.wait_ge(consts3, 3 + 2 + 2 * PAIRS)
                for q in range(PAIRS):
                    if q:
                        pe.wait_ge(ut_low, 2 * q)
                    for i in range(TILES):
                        at = (i % 2) * H + 128 * (i // 2)
                        mm = nc.tensor.transpose(ps_conv[0][:, at:at + 128],
                                                 u_all[:, i, 2 * q:2 * q + 2, :].rearrange("p b c -> p (b c)"), ident[:, :])
                    mm.then_inc(ut_psum, 1)
                for q in range(PAIRS):
                    for a in range(2):
                        for delta in range(SPANS):
                            add_out(q, a, 128 * delta, 128 * (delta + 1),
                                    x2[:, 2 * delta + a, 2 * q:2 * q + 2, :].rearrange("p b c -> p (b c)"), ident[:, :])
                pe.wait_ge(ut_low, 2 * PAIRS)
                pe.wait_ge(ar_step, 5)
                for q in range(PAIRS):
                    for a in range(2):
                        for tap in range(AR_TAPS):
                            parity = (a + tap) % 2
                            back = (tap + parity - a) // 2
                            for lo, hi, band in BANDS:
                                for wp, dp in TERMS:
                                    mm = add_out(q, a, lo, hi, ar_mix[:, band, tap, wp, :],
                                                 u_t[q][dp][:, parity, 2 + lo - back:2 + hi - back])

                steps = [(q, a) for q in range(PAIRS) for a in range(2)]

                def one_filter(pair, slot, first=False):
                    k = 2 * pair + slot
                    for j, (q, a) in enumerate(steps):
                        m = STEPS * k + j
                        if j == 0:
                            pe.wait_ge(hankel_in[slot], 16 * (pair + 1))
                        at_least(pe, conv_low, m - 1)
                        convolve(k, slot, q, a, j)
                        if j == 0:
                            if not first:
                                pe.wait_ge(conv_low, m)
                                mix(1 - slot, *steps[-1], STEPS - 1)
                        else:
                            pe.wait_ge(conv_low, m)
                            if j == 1:
                                pe.wait_ge(block_ready, 2 * (k + 1))
                            mix(slot, *steps[j - 1], j - 1)

                one_filter(0, 0, first=True)
                one_filter(0, 1)
                with pe.Fori(1, FILTERS // 2) as pair:
                    one_filter(pair, 0)
                    one_filter(pair, 1)
                pe.wait_ge(conv_low, STEPS * FILTERS)
                mix(1, *steps[-1], STEPS - 1)

            @block.scalar
            def _(act):
                act.wait_ge(w_step, 2)
                nc.scalar.activation(w[:, 2, :], w[:, 0, :], ACT.Exp, bias=w[:, 1, 0:1]).then_inc(sig_ready, 1)
                for q in range(PAIRS):
                    act.wait_ge(ut_psum, q + 1)
                    if q == 0:
                        act.wait_ge(consts3, 3 + 2 + 2 * PAIRS)
                    nc.scalar.activation(u_t[q][0][:, :, 2:], ps_conv[0][:, :].rearrange("p (a i) -> p a i", a=2),
                                         ACT.Copy).then_inc(ut_high, 1)

                def one_filter(k):
                    for j in range(STEPS):
                        m = STEPS * k + j
                        act.wait_ge(conv_psum, m + 1)
                        at_least(act, mixed_in, m - 1)
                        nc.scalar.activation(conv[j % 2][0][:, :, :], ps_conv[j % 2][:, :].rearrange("p (l i) -> p l i", l=2),
                                             ACT.Copy).then_inc(conv_high, 1)

                one_filter(0)
                with act.Fori(1, FILTERS) as k:
                    one_filter(k)
                act.wait_ge(mixed_in, STEPS * FILTERS)
                for q in range(PAIRS):
                    for a in range(2):
                        nc.scalar.activation(result[q][:, a::2], ps_out[q][a][:, :], ACT.Copy).then_inc(result_ready, 1)

            @block.vector
            def _(dve):
                def chain(semaphore, count, instruction):
                    instruction.then_inc(semaphore, 1)
                    dve.wait_ge(semaphore, count)

                dve.wait_ge(in3, IN3)
                chain(rows_step, 1, nc.vector.memset(rows[:, :, :].bitcast(F32), 0.0))
                for lag in range(2):
                    reverse = phi[:, lag::2][:, ::-1]
                    chain(rows_ready, 2 * lag + 1, nc.vector.tensor_copy(rows[:, 2 * lag, 0:H], reverse))
                    chain(rows_ready, 2 * lag + 2, nc.vector.tensor_tensor(
                        rows[:, 2 * lag + 1, 0:H], reverse, rows[:, 2 * lag, 0:H].bitcast(F32), ALU.subtract))
                chain(w_step, 1, nc.vector.tensor_tensor(w[:, 0, :], logits[:, 0, :], logits[:, 1, :], ALU.add))
                chain(w_step, 2, nc.vector.tensor_reduce(w[:, 1, 0:1], w[:, 0, :], AX.X, ALU.max, negate=True))
                dve.wait_ge(sig_ready, 2)
                chain(w_step, 3, nc.vector.tensor_reduce(w[:, 1, 1:2], w[:, 2, :], AX.X, ALU.add))
                chain(w_step, 4, nc.vector.reciprocal(w[:, 1, 2:3], w[:, 1, 1:2]))
                chain(w_step, 5, nc.vector.tensor_scalar(w[:, 3, :], w[:, 2, :], w[:, 1, 2:3], None, ALU.mult))
                chain(w_step, 6, nc.vector.tensor_reduce(w[:, 1, 3:4], w[:, 3, :], AX.X, ALU.max))
                chain(w_step, 7, nc.vector.tensor_scalar(w[:, 4, :], w[:, 3, :], w[:, 1, 3:4], None, ALU.is_equal))
                chain(w_step, 8, nc.vector.tensor_copy(w[:, 5, 0:1], w[:, 4, 0:1]))
                for j in range(1, EXPERTS):
                    chain(w_step, 8 + j, nc.vector.tensor_tensor(w[:, 5, j:j + 1], w[:, 5, j - 1:j], w[:, 4, j:j + 1], ALU.add))
                at = 8 + EXPERTS - 1
                chain(w_step, at + 1, nc.vector.tensor_scalar(w[:, 6, :], w[:, 5, :], 1.0, None, ALU.is_equal))
                chain(w_step, at + 2, nc.vector.tensor_tensor(w[:, 6, :], w[:, 6, :], w[:, 4, :], ALU.mult))
                chain(w_step, at + 3, nc.vector.tensor_tensor(w[:, 7, :], w[:, 6, :], w[:, 3, :], ALU.subtract))
                chain(w_step, at + 4, nc.vector.tensor_tensor(w[:, 7, :], w[:, 7, :], w[:, 3, :], ALU.add))
                for i in range(EXPERTS):
                    last = nc.vector.tensor_scalar(wk[:, i, :], sig4[:, :], w[:, 7, i:i + 1], None, ALU.mult)
                chain(wk_ready, 1, last)
                done = 0
                for m in (plus, minus):
                    for i in range(EXPERTS):
                        done += 1
                        chain(cum_step, done, nc.vector.tensor_tensor(
                            m[:, i, :, :], m[:, i, :, :], wk[:, i, :].unsqueeze(2).to_broadcast([128, FILTERS, C]), ALU.mult))
                        if i:
                            done += 1
                            chain(cum_step, done, nc.vector.tensor_tensor(m[:, i, :, :], m[:, i, :, :], m[:, i - 1, :, :], ALU.add))
                for i in range(EXPERTS):
                    done += 1
                    chain(cum_step, done, nc.vector.tensor_scalar(taps[:, i, :, :], taps[:, i, :, :], w[:, 7, i:i + 1], None, ALU.mult))
                    if i:
                        done += 1
                        chain(cum_step, done, nc.vector.tensor_tensor(taps[:, i, :, :], taps[:, i, :, :], taps[:, i - 1, :, :], ALU.add))
                for lag, op in ((0, ALU.add), (1, ALU.subtract)):
                    for i in range(EXPERTS):
                        last = nc.vector.tensor_tensor(mixes[:, :, i, lag, :], plus[:, i, :, :], minus[:, i, :, :], op)
                    last.then_inc(mixes_ready, 1)
                chain(ar_step, 1, nc.vector.memset(ar_mix[:, :, :, :, :].bitcast(F32), 0.0))
                for n, half in enumerate((0, C)):
                    dst = ar_mix[half:half + C, :, :, :, half:half + C]
                    chain(ar_step, 2 + n, nc.vector.tensor_copy(dst[:, :, :, 0, :], taps[half:half + C]))
                for n, half in enumerate((0, C)):
                    dst = ar_mix[half:half + C, :, :, :, half:half + C]
                    last = nc.vector.tensor_tensor(dst[:, :, :, 1, :], taps[half:half + C], dst[:, :, :, 0, :].bitcast(F32),
                                                   ALU.subtract)
                    chain(ar_step, 4 + n, last)
                for q in range(PAIRS):
                    dve.wait_ge(ut_high, q + 1)
                    nc.vector.tensor_tensor(u_t[q][1][:, :, 2:], ps_conv[0][:, :].rearrange("p (a i) -> p a i", a=2),
                                            u_t[q][0][:, :, 2:].bitcast(F32), ALU.subtract).then_inc(ut_low, 2)

                def one_filter(k):
                    for j in range(STEPS):
                        m = STEPS * k + j
                        dve.wait_ge(conv_high, m + 1)
                        nc.vector.tensor_tensor(conv[j % 2][1][:, :, :], ps_conv[j % 2][:, :].rearrange("p (l i) -> p l i", l=2),
                                                conv[j % 2][0][:, :, :].bitcast(F32), ALU.subtract).then_inc(conv_low, 1)

                one_filter(0)
                with dve.Fori(1, FILTERS) as k:
                    one_filter(k)


def build(nc, ins, out):
    with ExitStack() as ctx:
        x1 = ctx.enter_context(nc.sbuf_tensor("x1", [C, B * L], F32))
        mamba_stage(nc, ins, x1)
        x2 = ctx.enter_context(nc.sbuf_tensor("x2", [128, TILES, B, C], F32))
        u_all = ctx.enter_context(nc.sbuf_tensor("u_all", [128, TILES, B, C], F32))
        u_high = ctx.enter_context(nc.sbuf_tensor("u_high", [128, TILES, B, C], F32R))
        u_low = ctx.enter_context(nc.sbuf_tensor("u_low", [128, TILES, B, C], F32R))
        attention_stage(nc, ins, x1, x2, u_all, u_high, u_low)
        expert_stage(nc, ins, x2, u_all, u_high, u_low, out)


def kernel(**inputs):
    import numpy as np
    import concourse.bacc as bacc
    from concourse.bass_utils import run_bass_kernel_spmd

    nc = bacc.Bacc("TRN2", target_bir_lowering=False, num_devices=1)
    given = {k.replace("L0_conv_", "").replace("L1_attn_", "").replace("L1_ffn_", ""): np.asarray(v)
             for k, v in inputs.items()}
    arrays = {"x": given["x"].reshape(B, C, L)}
    for d in DIRS:
        for name in ("W_in", "W_x", "W_dt", "A_log", "W_out"):
            arrays[f"{name}_{d}"] = given[f"{name}_{d}"]
        arrays[f"conv_w_{d}"] = given[f"conv_w_{d}"].T
        arrays[f"cols_{d}"] = np.stack([given[f"conv_b_{d}"], given[f"D_{d}"]], axis=1)
        arrays[f"b_dt_{d}"] = given[f"b_dt_{d}"][None]
    for name in ("Wq", "Wk", "Wv"):
        arrays[name] = given[name].T
    for name in ("sigma", "M_phi_plus", "M_phi_minus", "M_u", "log_weights", "gumbel"):
        arrays[name] = given[name]
    arrays["phi"] = given["phi"].T
    arrays["gn_cols"] = np.stack([given["gn_gamma"], given["gn_beta"]], axis=1)
    feed, ins = {}, {}
    for name, a in arrays.items():
        a = np.ascontiguousarray(a)
        feed[f"in_{name}"] = a
        ins[name] = nc.dram_tensor(f"in_{name}", a.shape, mybir.dt.from_np(a.dtype), kind="ExternalInput").ap()
    out = nc.dram_tensor("out_0", (B, C, L), F32, kind="ExternalOutput").ap()
    build(nc, ins, out)
    r = run_bass_kernel_spmd(nc, [feed], core_ids=[0])
    return r.results[0]["out_0"].reshape(B, C, 32, 32)
```

```python
from contextlib import ExitStack

import concourse.bass as bass
from concourse import mybir

F32 = mybir.dt.float32
BF16 = mybir.dt.bfloat16
F32R = mybir.dt.float32r
ALU = mybir.AluOpType
ACT = mybir.ActivationFunctionType
AX = mybir.AxisListType

B = 4
C = 64
L = 1024
H = 512
D = 128
N = 16
R = 8
GROUP = 16
GN_EPS = 1e-5
LN_EPS = 1e-5
DIRS = "fb"
DEEP = 4
PAIR = 2
Y_LAG = 3
TILES = L // 128
SPANS = TILES // 2
SPAN = 2 * 128
EXPERTS = 4
FILTERS = 16
AR_TAPS = 3
PADS = 640
BLOCKS = 4
EXPERT_LOADS = 16 * (2 + 1 + 1 + 2 * 3)
A_LOG_MAX = 60.0
PARTS = 3
BC = 2 * N
DT_ROW = PARTS * BC


def at_least(engine, semaphore, count):
    if isinstance(count, int) and count <= 0:
        return
    engine.wait_ge(semaphore, count)


def mamba_stage(nc, ins, x1):
    with ExitStack() as ctx:
        def sb(name, shape, dt=F32):
            return ctx.enter_context(nc.sbuf_tensor(name, shape, dt))

        def sem(name):
            return ctx.enter_context(nc.semaphore(name))

        x_pair = [sb(f"x_pair_{d}", [2 * C, B * L]) for d in DIRS]
        packed_in = [sb(f"packed_in_{d}", [2 * C, 3, D]) for d in DIRS]
        w_in, taps, w_gate = ([p[:, j, :] for p in packed_in] for j in range(3))
        w_conv = [sb(f"w_conv_{d}", [2 * C, D]) for d in DIRS]
        packed_inner = [sb(f"packed_inner_{d}", [D, DT_ROW + R + C + N + 2]) for d in DIRS]
        w_x = [p[:, 0:DT_ROW + R] for p in packed_inner]
        w_out = [p[:, DT_ROW + R:DT_ROW + R + C] for p in packed_inner]
        a_log = [p[:, DT_ROW + R + C:DT_ROW + R + C + N] for p in packed_inner]
        cols = [p[:, DT_ROW + R + C + N:] for p in packed_inner]
        w_dt = [sb(f"w_dt_{d}", [128, D]) for d in DIRS]
        a_neg = [sb(f"a_neg_{d}", [D, N]) for d in DIRS]
        gn_cols = sb("gn_cols", [C, 2])
        ident = sb("ident", [128, 128])
        pick = sb("pick", [DT_ROW, BC], BF16)
        spread = sb("spread", [DT_ROW, BC, 128], BF16)
        xc = [sb(f"xc_{d}", [D, L]) for d in DIRS]
        gate = [sb(f"gate_{d}", [D, L]) for d in DIRS]
        dt = [sb(f"dt_{d}", [D, L]) for d in DIRS]
        dtx = [sb(f"dtx_{d}", [D, L]) for d in DIRS]
        bc_parts = [sb(f"bc_parts_{d}", [DT_ROW, L], BF16) for d in DIRS]
        gated = [sb(f"gated_{d}", [D, L]) for d in DIRS]
        z_raw = sb("z_raw", [D, L])
        scratch = sb("scratch", [D, L])
        soft = sb("soft", [D, L])
        one_plus = sb("one_plus", [D, L])
        dt_low = sb("dt_low", [128, L])
        decay = [sb(f"decay_{i}", [D, L]) for i in range(DEEP)]
        hidden = [sb(f"hidden_{i}", [D, L]) for i in range(DEEP)]
        c_wide = [sb(f"c_wide_{i}", [D, L]) for i in range(DEEP)]
        drive = [sb(f"drive_{i}", [D, L]) for i in range(PAIR)]
        prod = [sb(f"prod_{i}", [D, L]) for i in range(PAIR)]
        mixed = sb("mixed", [C, L])
        bn = sb("bn", [C, 2, 6])
        stats = sb("stats", [C, 32])
        stats_t = sb("stats_t", [C, 32])
        group_t = sb("group_t", [C, 2])
        group_w = sb("group_w", [C, 32])
        group = sb("group", [C, 32])
        gn = sb("gn", [C, 6])
        minus_half = sb("minus_half", [C, 1])

        ps_b = ctx.enter_context(nc.psum_tensor("ps_b", [128, L], F32))
        ps_c = ctx.enter_context(nc.psum_tensor("ps_c", [128, L], F32))
        ps_y = ctx.enter_context(nc.psum_tensor("ps_y", [128, L], F32))
        ps_w = ctx.enter_context(nc.psum_tensor("ps_w", [128, L], F32))

        names = """weights_in x_in z_taken consts w_conv_ready spread_ready a_exp_ready a_ready
            b_wide_ready c_psum_ready c_wide_ready decay_ready drive_ready hidden_ready prod_ready prod_summed
            xp_ready xc_ready z_ready gate_ready xdb_ready high_ready dt_low_ready rest_ready mid_ready
            parts_ready dt_psum_ready abs_ready exp_ready ln_ready relu_ready dt_ready dtx_ready
            y_taken gated_ready out_ready mixed_ready gn_step rstd_ready gn_ready act_ready x1_ready
            aggregate a_log_ready one_plus_ready lost_ready"""
        (weights_in, x_in, z_taken, consts, w_conv_ready, spread_ready, a_exp_ready, a_ready,
         b_wide_ready, c_psum_ready, c_wide_ready, decay_ready, drive_ready, hidden_ready, prod_ready, prod_summed,
         xp_ready, xc_ready, z_ready, gate_ready, xdb_ready, high_ready, dt_low_ready, rest_ready, mid_ready,
         parts_ready, dt_psum_ready, abs_ready, exp_ready, ln_ready, relu_ready, dt_ready, dtx_ready,
         y_taken, gated_ready, out_ready, mixed_ready, gn_step, rstd_ready, gn_ready, act_ready, x1_ready,
         aggregate, a_log_ready, one_plus_ready, lost_ready) = [sem(name) for name in names.split()]
        first_in = [sem(f"first_in_{d}") for d in DIRS]
        GN_STEPS = 12
        FIRST = 16 * 3
        WEIGHTS = 16 * (2 * 3 + 1)
        X_LOADS = 16 * 4
        CONSTS = 7 + 1 + PARTS

        AHEAD = [[0], [1, 2], [3, 4]] + [[s + 2] for s in range(3, N - 2)] + [[], []]

        def halves(t):
            return [t[:, h * H:(h + 1) * H] for h in range(L // H)]

        with nc.Block() as block:

            @block.sync
            def _(sp):
                src = ins["x"].rearrange("b c t -> c b t")

                def load_x(i, lo, hi, done):
                    dst = x_pair[i].rearrange("c (b t) -> c b t", b=B)[:, lo:hi, :]
                    sp.dma_start(dst[0:C, :, :], src[:, lo:hi, :]).then_inc(done, 16)
                    if i == 0:
                        sp.dma_start(dst[C:, :, 1:L], src[:, lo:hi, 0:L - 1]).then_inc(done, 16)
                    else:
                        sp.dma_start(dst[C:, :, 0:L - 1], src[:, lo:hi, 1:L]).then_inc(done, 16)

                for i, d in enumerate(DIRS):
                    sp.dma_start(packed_in[i][:, :, :], ins[f"packed_in_{d}"]).then_inc(first_in[i], 16)
                    load_x(i, 0, 1, first_in[i])
                    sp.dma_start(packed_inner[i][:, :], ins[f"packed_inner_{d}"]).then_inc(weights_in, 16)
                    sp.dma_start(w_dt[i][DT_ROW:DT_ROW + R, :], ins[f"W_dt_{d}"]).then_inc(weights_in, 16)
                    sp.dma_start(w_dt[i][DT_ROW + R:DT_ROW + R + 1, :], ins[f"b_dt_{d}"]).then_inc(weights_in, 16)
                sp.dma_start(gn_cols[:, :], ins["gn_cols"]).then_inc(weights_in, 16)
                for i in range(2):
                    load_x(i, 1, B, x_in)

            @block.gpsimd
            def _(pool):
                shifted = [x.rearrange("c (b t) -> c b t", b=B)[C:, :, :] for x in x_pair]
                zeros = [shifted[0][:, :, 0:1], shifted[1][:, :, L - 1:L], ident[:, :], pick[:, :], stats[:, :]]
                for i, part in enumerate(zeros):
                    nc.gpsimd.memset(part, 0.0).then_inc(consts, 1)
                    pool.wait_ge(consts, i + 1)
                nc.gpsimd.memset(minus_half[:, :], -0.5).then_inc(consts, 1)
                pool.wait_ge(consts, 6)
                nc.gpsimd.memset(dt_low[DT_ROW:, :], 1.0).then_inc(consts, 1)
                pool.wait_ge(consts, 7)
                nc.gpsimd.affine_select(out=ident[:, :], in_=ident[:, :], compare_op=ALU.not_equal, fill=1.0,
                                        base=0, pattern=[[-1, 128]], channel_multiplier=1).then_inc(consts, 1)
                for k in range(PARTS):
                    pool.wait_ge(consts, 8 + k)
                    nc.gpsimd.affine_select(out=pick[:, :], in_=pick[:, :], compare_op=ALU.not_equal, fill=1.0,
                                            base=-BC * k, pattern=[[-1, BC]], channel_multiplier=1).then_inc(consts, 1)

                def rstd(b):
                    pool.wait_ge(gn_step, GN_STEPS * b + 10)
                    nc.gpsimd.tensor_tensor(gn[:, 3:4], gn[:, 2:3], minus_half[:, :], ALU.pow).then_inc(rstd_ready, 1)

                def residual(b):
                    pool.wait_ge(act_ready, b + 1)
                    nc.gpsimd.tensor_tensor(x1[:, bass.ds(b * L, L)], mixed[:, :], x_pair[0][0:C, bass.ds(b * L, L)],
                                            ALU.add).then_inc(x1_ready, 1)

                def batch(b, first=False):
                    for i in range(2):
                        for s in range(N):
                            n, k = (2 * b + i) * N + s, i * N + s
                            pool.wait_ge(hidden_ready, n + 1)
                            pool.wait_ge(c_wide_ready, n + 1)
                            at_least(pool, prod_summed, n - PAIR + 1)
                            nc.gpsimd.tensor_tensor(prod[k % PAIR][:, :], hidden[k % DEEP][:, :],
                                                    c_wide[k % DEEP][:, :], ALU.mult).then_inc(prod_ready, 1)
                            if i == 1 and not first:
                                if s == 1:
                                    rstd(b - 1)
                                if s == 8:
                                    residual(b - 1)

                for i in range(2):
                    pool.wait_ge(first_in[i], FIRST)
                pool.wait_ge(x_in, X_LOADS)
                batch(0, first=True)
                with pool.Fori(1, B) as b:
                    batch(b)
                rstd(B - 1)
                residual(B - 1)

            @block.tensor
            def _(pe):
                def project(i, b, w, done):
                    for h, out in enumerate(halves(ps_w)):
                        mm = nc.tensor.matmul(out, w, x_pair[i][:, bass.ds(b * L + h * H, H)], start=True, stop=True)
                    mm.then_inc(done, 1)

                def gate_in(u, i, b):
                    at_least(pe, mixed_ready, b - 1)
                    at_least(pe, relu_ready, u)
                    project(i, b, w_gate[i], z_ready)

                def conv_in(u, i, b):
                    pe.wait_ge(z_taken, u + 1)
                    project(i, b, w_conv[i][:, :], xp_ready)

                def low_rank(u, i):
                    pe.wait_ge(xc_ready, u + 1)
                    for h, out in enumerate(halves(ps_w)):
                        mm = nc.tensor.matmul(out[0:DT_ROW + R, :], w_x[i], halves(xc[i])[h], start=True, stop=True)
                    mm.then_inc(xdb_ready, 1)

                def dt_in(u, i):
                    pe.wait_ge(dt_low_ready, u + 1)
                    pe.wait_ge(rest_ready, u + 1)
                    for h, out in enumerate(halves(ps_w)):
                        mm = nc.tensor.matmul(out, w_dt[i][DT_ROW:DT_ROW + R + 1, :],
                                              halves(dt_low)[h][DT_ROW:DT_ROW + R + 1, :], start=True, stop=True)
                    mm.then_inc(dt_psum_ready, 1)

                def wide_b(n, s, i):
                    at_least(pe, drive_ready, n)
                    for h, out in enumerate(halves(ps_b)):
                        mm = nc.tensor.matmul(out, spread[:, s, :], halves(bc_parts[i])[h], start=True, stop=True)
                    mm.then_inc(b_wide_ready, 1)

                def wide_c(n, s, i):
                    at_least(pe, c_wide_ready, n)
                    for h, out in enumerate(halves(ps_c)):
                        mm = nc.tensor.matmul(out, spread[:, N + s, :], halves(bc_parts[i])[h], start=True, stop=True)
                    mm.then_inc(c_psum_ready, 1)

                def sum_states(n, k, u):
                    s = k % N
                    if s == 0:
                        at_least(pe, y_taken, u)
                    pe.wait_ge(prod_ready, n + 1)
                    for h, out in enumerate(halves(ps_y)):
                        mm = nc.tensor.matmul(out, ident[:, :], halves(prod[k % PAIR])[h], start=(s == 0), stop=(s == N - 1))
                    mm.then_inc(prod_summed, 1)

                def out_product(b, at_relu):
                    pe.wait_ge(gated_ready, 2 * b + 2)
                    at_least(pe, relu_ready, at_relu)
                    for h, out in enumerate(halves(ps_w)):
                        for i in range(2):
                            mm = nc.tensor.matmul(out[0:C, :], w_out[i], halves(gated[i])[h],
                                                  start=(i == 0), stop=(i == 1))
                    mm.then_inc(out_ready, 1)

                def batch(b, first=False, last=False):
                    for i in range(2):
                        u = 2 * b + i
                        pe.wait_ge(parts_ready, u + 1)
                        for s in range(N):
                            n, k = u * N + s, i * N + s
                            wide_b(n, s, i)
                            if not (first and k < Y_LAG):
                                sum_states(n - Y_LAG, (k - Y_LAG) % (2 * N), u if s >= Y_LAG else u - 1)
                            wide_c(n, s, i)
                            if not (last and i == 1):
                                v, j, bv = u + 1, 1 - i, (b if i == 0 else b + 1)
                                if s == 1:
                                    if first and i == 0:
                                        pe.wait_ge(first_in[1], FIRST)
                                        pe.wait_ge(w_conv_ready, 2)
                                    if first and i == 1:
                                        pe.wait_ge(x_in, X_LOADS)
                                    gate_in(v, j, bv)
                                if s == 4:
                                    conv_in(v, j, bv)
                                if s == 7:
                                    low_rank(v, j)
                                if s == 11:
                                    dt_in(v, j)
                            if i == 0 and s == 15 and not first:
                                out_product(b - 1, u + 2)

                pe.wait_ge(consts, CONSTS)
                pe.wait_ge(first_in[0], FIRST)
                gate_in(0, 0, 0)
                pe.wait_ge(w_conv_ready, 1)
                conv_in(0, 0, 0)
                pe.wait_ge(weights_in, WEIGHTS)
                low_rank(0, 0)
                dt_in(0, 0)
                pe.wait_ge(spread_ready, 1)
                batch(0, first=True)
                with pe.Fori(1, B - 1) as b:
                    batch(b)
                batch(B - 1, last=True)
                for k in range(2 * N - Y_LAG, 2 * N):
                    sum_states(2 * N * (B - 1) + k, k, 2 * B - 1)
                out_product(B - 1, 2 * B)

            @block.scalar
            def _(act):
                def take_z(u, i):
                    act.wait_ge(z_ready, u + 1)
                    at_least(act, gate_ready, u)
                    nc.scalar.activation(z_raw[:, :], ps_w[:, :], ACT.Copy).then_inc(z_taken, 1)

                def silu_input(u, i):
                    act.wait_ge(xp_ready, u + 1)
                    at_least(act, y_taken, u - 1)
                    nc.scalar.activation(xc[i][:, :], ps_w[:, :], ACT.Silu, bias=cols[i][:, 0:1]).then_inc(xc_ready, 1)

                def silu_gate(u, i, norm=None):
                    act.wait_ge(z_taken, u + 1)
                    at_least(act, gated_ready, u - 1)
                    nc.scalar.activation(gate[i][:, :], z_raw[:, :], ACT.Silu).then_inc(gate_ready, 1)
                    if norm is not None:
                        norm_silu(norm)
                    nc.scalar.preload_act_table_set("natural_log_exp_and_others")

                def norm_silu(b):
                    act.wait_ge(gn_ready, b + 1)
                    nc.scalar.activation(mixed[:, :], mixed[:, :], ACT.Silu, scale=gn[:, 4:5],
                                         bias=gn[:, 5:6]).then_inc(act_ready, 1)

                def split_high(u, i):
                    act.wait_ge(xdb_ready, u + 1)
                    at_least(act, c_psum_ready, N * (u - 1))
                    nc.scalar.activation(bc_parts[i][:, :], ps_w[0:DT_ROW, :], ACT.Copy).then_inc(high_ready, 1)
                    at_least(act, dt_psum_ready, u)
                    nc.scalar.activation(dt_low[DT_ROW:DT_ROW + R, :], ps_w[DT_ROW:DT_ROW + R, :],
                                         ACT.Copy).then_inc(dt_low_ready, 1)

                def softplus_exp(u, i):
                    act.wait_ge(dt_psum_ready, u + 1)
                    nc.scalar.activation(soft[:, :], ps_w[:, :], ACT.Abs).then_inc(abs_ready, 1)
                    act.wait_ge(abs_ready, u + 1)
                    nc.scalar.activation(soft[:, :], soft[:, :], ACT.Exp, scale=-1.0).then_inc(exp_ready, 1)

                def softplus_ln(u, i):
                    act.wait_ge(exp_ready, u + 2)
                    nc.scalar.activation(one_plus[:, :], soft[:, :], ACT.Identity, bias=1.0).then_inc(one_plus_ready, 1)
                    act.wait_ge(one_plus_ready, u + 1)
                    at_least(act, decay_ready, N * (u - 1))
                    at_least(act, dtx_ready, u - 1)
                    nc.scalar.activation(dt[i][:, :], one_plus[:, :], ACT.Ln).then_inc(ln_ready, 1)

                def decay_of(n, k, i, s):
                    at_least(act, hidden_ready, n - DEEP + 1)
                    nc.scalar.activation(decay[k % DEEP][:, :], dt[i][:, :], ACT.Exp,
                                         scale=a_neg[i][:, s:s + 1]).then_inc(decay_ready, 1)

                def take_c(n, k):
                    act.wait_ge(c_psum_ready, n + 1)
                    at_least(act, prod_ready, n - DEEP + 1)
                    nc.scalar.activation(c_wide[k % DEEP][:, :], ps_c[:, :], ACT.Copy).then_inc(c_wide_ready, 1)

                def batch(b, first=False, last=False):
                    for i in range(2):
                        u = 2 * b + i
                        act.wait_ge(dt_ready, u + 1)
                        for s in range(N):
                            for t in AHEAD[s]:
                                decay_of(u * N + t, i * N + t, i, t)
                            if s != 6:
                                take_c(u * N + s, i * N + s)
                            if last and i == 1:
                                if s == 5:
                                    take_c(u * N + s + 1, i * N + s + 1)
                                    norm_silu(b - 1)
                                    nc.scalar.preload_act_table_set("natural_log_exp_and_others")
                                continue
                            if s == 2:
                                take_z(u + 1, 1 - i)
                            if s == 5:
                                silu_input(u + 1, 1 - i)
                                take_c(u * N + s + 1, i * N + s + 1)
                                silu_gate(u + 1, 1 - i, norm=(b - 1 if i == 1 and not first else None))
                            if s == 8:
                                split_high(u + 1, 1 - i)
                            if s == 12:
                                softplus_exp(u + 1, 1 - i)
                            if s == 13:
                                softplus_ln(u + 1, 1 - i)

                take_z(0, 0)
                act.wait_ge(weights_in, WEIGHTS)
                act.wait_ge(a_log_ready, 2)
                nc.scalar.preload_act_table_set("natural_log_exp_and_others")
                for i in range(2):
                    last = nc.scalar.activation(a_neg[i][:, :], a_log[i], ACT.Exp)
                last.then_inc(exp_ready, 1)
                silu_input(0, 0)
                silu_gate(0, 0)
                split_high(0, 0)
                softplus_exp(0, 0)
                softplus_ln(0, 0)
                act.wait_ge(a_ready, 2)
                batch(0, first=True)
                with act.Fori(1, B - 1) as b:
                    batch(b)
                batch(B - 1, last=True)
                norm_silu(B - 1)

            @block.vector
            def _(dve):
                def split_low(u, i):
                    dve.wait_ge(high_ready, u + 1)
                    dve.wait_ge(dt_low_ready, u + 1)
                    at_least(dve, gated_ready, u - 1)
                    nc.vector.tensor_tensor(scratch[0:2 * BC, :], ps_w[0:2 * BC, :], bc_parts[i][0:2 * BC, :],
                                            ALU.subtract).then_inc(rest_ready, 1)

                def split_mid(u, i):
                    dve.wait_ge(rest_ready, u + 1)
                    nc.vector.tensor_copy(bc_parts[i][0:2 * BC, :], scratch[0:2 * BC, :]).then_inc(mid_ready, 1)

                def split_last(u, i):
                    dve.wait_ge(mid_ready, u + 1)
                    nc.vector.tensor_tensor(bc_parts[i][0:BC, :], scratch[0:BC, :], bc_parts[i][0:BC, :],
                                            ALU.subtract).then_inc(parts_ready, 1)

                def lost(u, i):
                    dve.wait_ge(one_plus_ready, u + 1)
                    dve.wait_ge(parts_ready, u + 1)
                    nc.vector.scalar_tensor_tensor(out=scratch[:, :], in0=one_plus[:, :], scalar=-1.0, in1=soft[:, :],
                                                   op0=ALU.add, op1=ALU.subtract).then_inc(lost_ready, 1)

                def relu(u, i):
                    dve.wait_ge(lost_ready, u + 1)
                    nc.vector.scalar_tensor_tensor(out=scratch[:, :], in0=ps_w[:, :], scalar=0.0, in1=scratch[:, :],
                                                   op0=ALU.max, op1=ALU.subtract).then_inc(relu_ready, 1)

                def dt_sum(u, i):
                    dve.wait_ge(ln_ready, u + 1)
                    dve.wait_ge(relu_ready, u + 1)
                    nc.vector.tensor_tensor(dt[i][:, :], scratch[:, :], dt[i][:, :], ALU.add).then_inc(dt_ready, 1)

                def dt_x(u, i):
                    dve.wait_ge(dt_ready, u + 1)
                    at_least(dve, drive_ready, N * (u - 1))
                    nc.vector.tensor_tensor(dtx[i][:, :], dt[i][:, :], xc[i][:, :], ALU.mult).then_inc(dtx_ready, 1)

                def take_y(u, i, last=False):
                    dve.wait_ge(prod_summed, N * (u + 1))
                    if not last:
                        dve.wait_ge(dt_ready, u + 2)
                    nc.vector.scalar_tensor_tensor(out=scratch[:, :], in0=xc[i][:, :], scalar=cols[i][:, 1:2],
                                                   in1=ps_y[:, :], op0=ALU.mult, op1=ALU.add).then_inc(y_taken, 1)

                def drive_step(n, k, i):
                    dve.wait_ge(b_wide_ready, n + 1)
                    at_least(dve, hidden_ready, n - PAIR + 1)
                    nc.vector.tensor_tensor(drive[k % PAIR][:, :], dtx[i][:, :], ps_b[:, :], ALU.mult).then_inc(drive_ready, 1)

                def scan_step(n, k):
                    dve.wait_ge(decay_ready, n + 1)
                    dve.wait_ge(drive_ready, n + 1)
                    at_least(dve, prod_ready, n - DEEP + 1)
                    order = slice(None) if k < N else slice(None, None, -1)
                    nc.vector.tensor_tensor_scan(hidden[k % DEEP][:, order], decay[k % DEEP][:, order],
                                                 drive[k % PAIR][:, order], 0.0, ALU.mult,
                                                 ALU.add).then_inc(hidden_ready, 1)

                def chain(step, instruction):
                    instruction.then_inc(gn_step, 1)
                    dve.wait_ge(gn_step, step)

                def norm_take(b):
                    dve.wait_ge(out_ready, b + 1)
                    at_least(dve, x1_ready, b)
                    nc.vector.tensor_copy(mixed[:, :], ps_w[0:C, :]).then_inc(mixed_ready, 1)

                def norm_stats(b):
                    at = GN_STEPS * b
                    dve.wait_ge(mixed_ready, b + 1)
                    for h, part in enumerate(halves(mixed)):
                        chain(at + h + 1, nc.vector.bn_stats(bn[:, h, :], part))
                    dve.sem_inc(aggregate, 1)
                    chain(at + 3, nc.vector.bn_aggr(stats[:, 0:2], bn[:, :, :].rearrange("c a b -> c (a b)")))
                    chain(at + 4, nc.vector.scalar_tensor_tensor(out=stats[:, 1:2], in0=stats[:, 0:1],
                                                                 scalar=stats[:, 0:1], in1=stats[:, 1:2],
                                                                 op0=ALU.mult, op1=ALU.add))
                    chain(at + 5, nc.vector.transpose(stats_t[:, :], stats[:, :]))
                    chain(at + 6, nc.vector.tensor_reduce(group_t[:, :],
                                                          stats_t[:, :].rearrange("c (g k) -> c g k", k=GROUP),
                                                          AX.X, ALU.add))
                    chain(at + 7, nc.vector.tensor_scalar(group_w[:, :].rearrange("c (g k) -> c g k", k=GROUP),
                                                          group_t[:, :].unsqueeze(2).to_broadcast([C, 2, GROUP]),
                                                          1.0 / GROUP, None, ALU.mult))
                    chain(at + 8, nc.vector.transpose(group[:, :], group_w[:, :]))
                    chain(at + 9, nc.vector.tensor_scalar(gn[:, 1:2], group[:, 0:1], group[:, 0:1], -1.0, ALU.mult, ALU.mult))
                    chain(at + 10, nc.vector.tensor_scalar(gn[:, 2:3], gn[:, 1:2], group[:, 1:2], GN_EPS, ALU.add, ALU.add))

                def norm_scale(b):
                    at = GN_STEPS * b
                    dve.wait_ge(rstd_ready, b + 1)
                    chain(at + 11, nc.vector.tensor_scalar(gn[:, 4:5], gn[:, 3:4], gn_cols[:, 0:1], None, ALU.mult))
                    chain(at + 12, nc.vector.tensor_scalar(gn[:, 1:2], group[:, 0:1], gn[:, 4:5], -1.0, ALU.mult, ALU.mult))
                    nc.vector.tensor_scalar(gn[:, 5:6], gn[:, 1:2], gn_cols[:, 1:2], None, ALU.add).then_inc(gn_ready, 1)

                def batch(b, first=False, last=False):
                    for i in range(2):
                        u = 2 * b + i
                        dve.wait_ge(dtx_ready, u + 1)
                        for s in range(N):
                            n, k = u * N + s, i * N + s
                            drive_step(n, k, i)
                            if not (first and k == 0):
                                scan_step(n - 1, (k - 1) % (2 * N))
                            if not (first and i == 0):
                                if s == 2:
                                    take_y(u - 1, 1 - i)
                                if s == 3:
                                    gate_of(u - 1, 1 - i, b)
                            if i == 1 and not first:
                                if s == 0:
                                    norm_take(b - 1)
                                if s == 1:
                                    norm_stats(b - 1)
                                if s == 3:
                                    norm_scale(b - 1)
                            if last and i == 1:
                                continue
                            for at, step in ((9, split_low), (10, split_mid), (11, split_last),
                                             (14, lost), (14, relu), (15, dt_sum), (15, dt_x)):
                                if s == at:
                                    step(u + 1, 1 - i)

                def gate_of(u, i, b):
                    dve.wait_ge(y_taken, u + 1)
                    at_least(dve, out_ready, b if i == 0 else b - 1)
                    nc.vector.tensor_tensor(gated[i][:, :], scratch[:, :], gate[i][:, :], ALU.mult).then_inc(gated_ready, 1)

                dve.wait_ge(first_in[0], FIRST)
                nc.vector.tensor_tensor(w_conv[0][:, :], w_in[0], taps[0], ALU.mult).then_inc(w_conv_ready, 1)
                dve.wait_ge(consts, CONSTS)
                nc.vector.tensor_copy(spread[:, :, :], pick[:, :].unsqueeze(2).to_broadcast([DT_ROW, BC, 128])
                                      ).then_inc(spread_ready, 1)
                dve.wait_ge(weights_in, WEIGHTS)
                for i in range(2):
                    nc.vector.tensor_scalar(a_log[i], a_log[i], A_LOG_MAX, None, ALU.min).then_inc(a_log_ready, 1)
                dve.wait_ge(first_in[1], FIRST)
                nc.vector.tensor_tensor(w_conv[1][:, :], w_in[1], taps[1], ALU.mult).then_inc(w_conv_ready, 1)
                dve.wait_ge(exp_ready, 1)
                for i in range(2):
                    nc.vector.tensor_scalar(a_neg[i][:, :], a_neg[i][:, :], -1.0, None, ALU.mult).then_inc(a_ready, 1)
                for step in (split_low, split_mid, split_last, lost, relu, dt_sum, dt_x):
                    step(0, 0)
                batch(0, first=True)
                with dve.Fori(1, B - 1) as b:
                    batch(b)
                batch(B - 1, last=True)
                u = 2 * B - 1
                scan_step(N * (u + 1) - 1, 2 * N - 1)
                take_y(u, 1, last=True)
                gate_of(u, 1, B)
                norm_take(B - 1)
                norm_stats(B - 1)
                norm_scale(B - 1)


def attention_stage(nc, ins, e, x1, x2, u_all, u_high, u_low):
    with ExitStack() as ctx:
        def sb(name, shape, dt=F32):
            return ctx.enter_context(nc.sbuf_tensor(name, shape, dt))

        def sem(name):
            return ctx.enter_context(nc.semaphore(name))

        ident = e.ident
        ident_r = sb("ident_r", [128, 128], F32R)
        ident_bf = sb("ident_bf", [128, 128], BF16)
        mask = sb("mask", [128, 2, 2, 128], BF16)
        mask_t = sb("mask_t", [128, 2, 2, 128], BF16)
        wq, wk = (sb(name, [C, 2, C]) for name in ("wq", "wk"))
        wv = sb("wv", [C, C])
        xs = sb("xs", [C, L])
        tok = sb("tok", [128, TILES, C])
        tok_res = sb("tok_res", [128, TILES, C])
        cen = sb("cen", [128, TILES, C])
        cen2 = sb("cen2", [128, TILES, C])
        sq = sb("sq", [128, TILES, C])
        xn = sb("xn", [128, TILES, C])
        un = sb("un", [128, TILES, C])
        small = sb("small", [128, 3, TILES])
        small2 = sb("small2", [128, 3, TILES])
        minus_half = sb("minus_half2", [128, TILES])
        xn_t = sb("xn_t", [C, L])
        q_parts = sb("q_parts", [128, L], F32R)
        k_high = sb("k_high", [128, L], F32R)
        q_row = sb("q_row", [C + 1, L], F32R)
        k_one = sb("k_one", [C + 1, L], F32R)
        v_one = sb("v_one", [128, TILES, C + 1])
        probs = [sb(f"probs_{i}", [128, 2 * SPAN]) for i in range(2)]
        max_parts = sb("max_parts", [128, TILES, 2])
        neg_max = sb("neg_max", [128, TILES], F32R)
        o_t = sb("o_t", [C + 1, SPAN])
        inv = sb("inv", [128, 2, 1])
        tok2 = sb("tok2", [128, TILES, C])

        ps_s = ctx.enter_context(nc.psum_tensor("ps_s", [128, 4, H], F32))
        ps_t = [ctx.enter_context(nc.psum_tensor(f"ps_t{i}", [128, H], F32)) for i in range(2)]
        ps_o = ctx.enter_context(nc.psum_tensor("ps_o", [128, H], F32))
        ps_m = ctx.enter_context(nc.psum_tensor("ps_m", [128, H], F32))
        TURN = 3
        NEXT = 3

        names = """qkv_in a_consts xs_ready tok_psum tok_ready ln_step ln_rstd xn_ready xnt_psum xnt_ready
            q_psum q_high_ready q_ready k_psum k_high_ready k_ready v_psum v_ready scores_ready part_ready max_ready
            row_psum row_ready st_ready probs_ready pv_done ot_ready back_psum inv_ready back_done tok_res_ready
            ln2_step ln2_rstd u_ready u_high_ready u_low_ready x2_ready u_all_ready ident_ready passed"""
        (qkv_in, a_consts, xs_ready, tok_psum, tok_ready, ln_step, ln_rstd, xn_ready, xnt_psum, xnt_ready,
         q_psum, q_high_ready, q_ready, k_psum, k_high_ready, k_ready, v_psum, v_ready, scores_ready, part_ready,
         max_ready, row_psum, row_ready, st_ready, probs_ready, pv_done, ot_ready, back_psum, inv_ready, back_done,
         tok_res_ready, ln2_step, ln2_rstd, u_ready, u_high_ready, u_low_ready, x2_ready, u_all_ready, ident_ready, passed,
         ) = [sem(name) for name in names.split()]
        LN = 5
        MASKED = -1e30
        CONSTS = 11

        def width(i):
            return (i // 2 + 1) * SPAN

        pieces = [(i, at, min(H, width(i) - at)) for i in range(TILES) for at in range(0, width(i), H)]
        blocks = [(d, g) for d in range(SPANS) for g in range(d + 1)]
        PIECES, BLOCKS_T = len(pieces), len(blocks)

        def halves(t):
            return [t[:, h * H:(h + 1) * H] for h in range(L // H)]

        def all_batches(engine, batch):
            batch(0, first=True)
            with engine.Fori(1, B - 1) as b:
                batch(b)
            batch(B - 1, last=True)

        with nc.Block() as block:

            @block.sync
            def _(sp):
                for w, name in ((wq, "Wq"), (wk, "Wk")):
                    for j in range(2):
                        sp.dma_start(w[:, j, :], ins[name]).then_inc(qkv_in, 16)
                sp.dma_start(wv[:, :], ins["Wv"]).then_inc(qkv_in, 16)
                load_expert_weights(sp, ins, e)

            @block.gpsimd
            def _(pool):
                nc.gpsimd.memset(ident[:, :], 0.0).then_inc(a_consts, 1)
                nc.gpsimd.memset(mask[:, :, :, :], 0.0).then_inc(a_consts, 1)
                nc.gpsimd.memset(mask_t[:, :, :, :], 0.0).then_inc(a_consts, 1)
                nc.gpsimd.memset(minus_half[:, :], -0.5).then_inc(a_consts, 1)
                nc.gpsimd.memset(v_one[:, :, C:C + 1], 1.0).then_inc(a_consts, 1)
                pool.wait_ge(a_consts, 5)
                nc.gpsimd.memset(k_one[C:C + 1, :].bitcast(F32), 1.0).then_inc(a_consts, 1)
                pool.wait_ge(a_consts, 6)
                nc.gpsimd.affine_select(out=ident[:, :], in_=ident[:, :], compare_op=ALU.not_equal, fill=1.0,
                                        base=0, pattern=[[-1, 128]], channel_multiplier=1).then_inc(a_consts, 1)
                for parity in range(2):
                    pool.wait_ge(a_consts, 7 + 2 * parity)
                    nc.gpsimd.affine_select(out=mask[:, parity, :, :], in_=mask[:, parity, :, :],
                                            compare_op=ALU.is_ge, fill=MASKED, base=parity,
                                            pattern=[[-1, 2], [-2, 128]], channel_multiplier=2).then_inc(a_consts, 1)
                    pool.wait_ge(a_consts, 8 + 2 * parity)
                    nc.gpsimd.affine_select(out=mask_t[:, parity, :, :], in_=mask_t[:, parity, :, :],
                                            compare_op=ALU.is_ge, fill=MASKED, base=-parity,
                                            pattern=[[1, 2], [2, 128]], channel_multiplier=-2).then_inc(a_consts, 1)

                def rstd(b):
                    pool.wait_ge(ln_step, LN * b + LN)
                    nc.gpsimd.tensor_tensor(small[:, 2, :], small[:, 1, :], minus_half[:, :], ALU.pow).then_inc(ln_rstd, 1)

                def rstd2(b):
                    pool.wait_ge(ln2_step, LN * b + LN)
                    nc.gpsimd.tensor_tensor(small2[:, 2, :], small2[:, 1, :], minus_half[:, :], ALU.pow).then_inc(ln2_rstd, 1)

                rstd(0)
                rstd(1)
                clear_blocks(nc, pool, e)
                rstd2(0)
                rstd(2)
                weigh_and_sum(nc, pool, e)
                rstd2(1)
                rstd(3)
                lag_matrices(nc, pool, e)
                tap_blocks(nc, pool, e)
                pool.wait_ge(e.ar_ready, 2)
                rstd2(2)
                pool.wait_ge(ln2_rstd, 3)
                pool.wait_ge(e.sum_step, SUMMED + 2 * EXPERTS)
                for slot in range(2):
                    filter_blocks(nc, pool, e, slot, slot)
                    pool.wait_ge(e.block_ready, BLOCKS * (slot + 1))
                rstd2(3)

            @block.tensor
            def _(pe):
                def tokens(b):
                    pe.wait_ge(xs_ready, b + 1)
                    at_least(pe, v_ready, b)
                    pe.sem_inc(passed, 1)
                    for i in range(TILES):
                        delta, parity = divmod(i, 2)
                        rows = xs[:, SPAN * delta + parity:SPAN * (delta + 1):2]
                        mm = nc.tensor.transpose(ps_s[:, NEXT, i * C:(i + 1) * C], rows, ident[0:C, 0:C])
                    mm.then_inc(tok_psum, 1)

                def normed(b, h):
                    pe.wait_ge(xn_ready, b + 1)
                    pe.wait_ge(tok_ready, b + 1)
                    at_least(pe, xnt_ready, 2 * b + h)
                    pe.sem_inc(passed, 1)
                    for i in range(TILES // 2):
                        mm = nc.tensor.transpose(ps_s[0:C, NEXT, i * 128:(i + 1) * 128], xn[:, h * TILES // 2 + i, :], ident[:, :])
                    mm.then_inc(xnt_psum, 1)

                def project(b):
                    pe.wait_ge(xnt_ready, 2 * b + 2)
                    at_least(pe, part_ready, PIECES * b)
                    for first, w, done in ((0, wq, q_psum), (2, wk, k_psum)):
                        for h in range(2):
                            mm = nc.tensor.matmul(ps_s[:, first + h, :], w[:, :, :].rearrange("d j e -> d (j e)"),
                                                  halves(xn_t)[h], start=True, stop=True)
                        mm.then_inc(done, 1)

                def values(b):
                    pe.wait_ge(k_ready, b + 1)
                    for i in range(TILES):
                        mm = nc.tensor.matmul(ps_s[:, NEXT, i * C:(i + 1) * C], xn_t[:, i * 128:(i + 1) * 128], wv[:, :],
                                              start=True, stop=True)
                    mm.then_inc(v_psum, 1)

                def scores(b, d):
                    if d == 0:
                        pe.wait_ge(q_ready, 2 * (b + 1))
                        pe.wait_ge(k_ready, b + 1)
                    for c, (i, at, n) in enumerate(pieces):
                        if i // 2 != d:
                            continue
                        at_least(pe, part_ready, PIECES * b + c - TURN + 1)
                        out = ps_s[:, c % TURN, :]
                        queries = slice(i * 128, (i + 1) * 128)
                        last = at + n == width(i)
                        nc.tensor.matmul(out[:, 0:n], q_parts[:, queries], k_high[:, at:at + n], start=True, stop=False)
                        mm = nc.tensor.matmul(out[:, 0:n], q_row[0:C, queries], k_one[0:C, at:at + n], start=False, stop=not last)
                        if last:
                            mm = nc.tensor.matmul(out[:, n - SPAN:n], ident_bf[:, :],
                                                  mask[:, i % 2, :, :].rearrange("p a b -> p (a b)"), start=False, stop=True)
                        mm.then_inc(scores_ready, 1)

                def maxima(b, d, back):
                    pe.wait_ge(max_ready, TILES * b + 2 * d + 2)
                    at_least(pe, back_done, SPANS * b + back)
                    at_least(pe, row_ready, SPANS * b + d)
                    for j in range(2):
                        mm = nc.tensor.matmul(ps_m[0:C + 1, SPAN + j * 128:SPAN + (j + 1) * 128],
                                              neg_max[:, 2 * d + j:2 * d + j + 1].to_broadcast([128, C + 1]),
                                              ident_r[:, :], start=True, stop=True)
                    mm.then_inc(row_psum, 1)

                def scores_t(b, d, g):
                    n = blocks.index((d, g))
                    if g == 0:
                        pe.wait_ge(row_ready, SPANS * b + d + 1)
                    at_least(pe, probs_ready, BLOCKS_T * b + n - 1)
                    queries = slice(SPAN * d, SPAN * (d + 1))
                    for j in range(2):
                        keys = slice(SPAN * g + 128 * j, SPAN * g + 128 * (j + 1))
                        out = ps_t[n % 2][:, SPAN * j:SPAN * (j + 1)]
                        nc.tensor.matmul(out, k_high[:, keys], q_parts[:, queries], start=True, stop=False)
                        mm = nc.tensor.matmul(out, k_one[:, keys], q_row[:, queries], start=False, stop=d != g)
                        if d == g:
                            mm = nc.tensor.matmul(out, ident_bf[:, :], mask_t[:, j, :, :].rearrange("p a b -> p (a b)"),
                                                  start=False, stop=True)
                    mm.then_inc(st_ready, 1)

                def attend(b, d, g):
                    n = blocks.index((d, g))
                    pe.wait_ge(probs_ready, BLOCKS_T * b + n + 1)
                    if g == 0:
                        at_least(pe, ot_ready, SPANS * b + d)
                        if d == 0:
                            pe.wait_ge(v_ready, b + 1)
                    for j in range(2):
                        mm = nc.tensor.matmul(ps_o[0:C + 1, 0:SPAN], v_one[:, 2 * g + j, :],
                                              probs[n % 2][:, SPAN * j:SPAN * (j + 1)],
                                              start=(g == 0 and j == 0), stop=(g == d and j == 1))
                    mm.then_inc(pv_done, 1)

                def turn_back(b, d, rows):
                    pe.wait_ge(ot_ready, SPANS * b + d + 1)
                    pe.wait_ge(row_ready, SPANS * b + rows)
                    at_least(pe, back_done, SPANS * b + d)
                    pe.sem_inc(passed, 1)
                    for j in range(2):
                        mm = nc.tensor.transpose(ps_m[:, j * (C + 1):(j + 1) * (C + 1)], o_t[:, j * 128:(j + 1) * 128],
                                                 ident[0:C + 1, 0:C + 1])
                    mm.then_inc(back_psum, 1)

                def batch(b, first=False, last=False):
                    scores(b, 0)
                    scores(b, 1)
                    maxima(b, 0, back=0)
                    if not last:
                        tokens(b + 1)
                    scores_t(b, 0, 0)
                    scores(b, 2)
                    maxima(b, 1, back=0)
                    attend(b, 0, 0)
                    scores_t(b, 1, 0)
                    scores(b, 3)
                    maxima(b, 2, back=0)
                    scores_t(b, 1, 1)
                    attend(b, 1, 0)
                    turn_back(b, 0, rows=3)
                    attend(b, 1, 1)
                    scores_t(b, 2, 0)
                    maxima(b, 3, back=1)
                    scores_t(b, 2, 1)
                    attend(b, 2, 0)
                    if not last:
                        normed(b + 1, 0)
                    scores_t(b, 2, 2)
                    attend(b, 2, 1)
                    turn_back(b, 1, rows=4)
                    attend(b, 2, 2)
                    scores_t(b, 3, 0)
                    if not last:
                        normed(b + 1, 1)
                    scores_t(b, 3, 1)
                    attend(b, 3, 0)
                    turn_back(b, 2, rows=4)
                    scores_t(b, 3, 2)
                    attend(b, 3, 1)
                    scores_t(b, 3, 3)
                    attend(b, 3, 2)
                    if not last:
                        project(b + 1)
                    attend(b, 3, 3)
                    turn_back(b, 3, rows=4)
                    if not last:
                        values(b + 1)

                pe.wait_ge(qkv_in, 16 * 5)
                pe.wait_ge(a_consts, CONSTS)
                pe.wait_ge(ident_ready, 2)
                tokens(0)
                normed(0, 0)
                normed(0, 1)
                project(0)
                values(0)
                all_batches(pe, batch)

            @block.scalar
            def _(act):
                def take_x(b):
                    at_least(act, tok_psum, b)
                    nc.scalar.activation(xs[:, :], x1[:, bass.ds(b * L, L)], ACT.Copy).then_inc(xs_ready, 1)

                def take_tokens(b):
                    act.wait_ge(tok_psum, b + 1)
                    at_least(act, tok_res_ready, b)
                    nc.scalar.activation(tok[:, :, :].rearrange("p i c -> p (i c)"), ps_s[:, NEXT, :],
                                         ACT.Copy).then_inc(tok_ready, 1)

                def take_normed(b, h):
                    act.wait_ge(xnt_psum, 2 * b + h + 1)
                    at_least(act, v_psum, b)
                    nc.scalar.activation(halves(xn_t)[h], ps_s[0:C, NEXT, :], ACT.Copy).then_inc(xnt_ready, 1)

                def take_qk(b):
                    at_least(act, st_ready, BLOCKS_T * b)
                    act.wait_ge(q_psum, b + 1)
                    nc.scalar.activation(q_parts[:, :].rearrange("p (h n) -> p h n", h=2), ps_s[:, 0:2, :],
                                         ACT.Copy, scale=float(C) ** -0.5).then_inc(q_high_ready, 1)
                    act.wait_ge(k_psum, b + 1)
                    nc.scalar.activation(k_high[:, :].rearrange("p (h n) -> p h n", h=2), ps_s[:, 2:4, :],
                                         ACT.Copy).then_inc(k_high_ready, 1)

                def row(b, d):
                    act.wait_ge(row_psum, SPANS * b + d + 1)
                    nc.scalar.activation(q_row[C:C + 1, SPAN * d:SPAN * (d + 1)], ps_m[C:C + 1, SPAN:2 * SPAN],
                                         ACT.Copy).then_inc(row_ready, 1)

                def exp(b, d, g):
                    n = blocks.index((d, g))
                    act.wait_ge(st_ready, BLOCKS_T * b + n + 1)
                    at_least(act, pv_done, BLOCKS_T * b + n - 1)
                    nc.scalar.activation(probs[n % 2][:, :], ps_t[n % 2][:, :], ACT.Exp).then_inc(probs_ready, 1)

                def take_output(b, d):
                    act.wait_ge(pv_done, BLOCKS_T * b + blocks.index((d, d)) + 1)
                    at_least(act, back_psum, SPANS * b + d)
                    nc.scalar.activation(o_t[:, :], ps_o[0:C + 1, 0:SPAN], ACT.Copy).then_inc(ot_ready, 1)

                def keep_x2(b):
                    act.wait_ge(back_done, SPANS * (b + 1))
                    nc.scalar.activation(x2[:, :, bass.ds(b, 1), :].rearrange("p i o c -> p i (o c)"), tok2[:, :, :],
                                         ACT.Copy).then_inc(x2_ready, 1)

                def keep_u(b):
                    act.wait_ge(u_ready, b + 1)
                    nc.scalar.activation(u_all[:, :, bass.ds(b, 1), :].rearrange("p i o c -> p i (o c)"), un[:, :, :],
                                         ACT.Copy).then_inc(u_all_ready, 1)

                def batch(b, first=False, last=False):
                    if not last:
                        take_x(b + 1)
                    row(b, 0)
                    if not first:
                        keep_x2(b - 1)
                    act.wait_ge(tok_ready, b + 1)
                    nc.scalar.activation(tok_res[:, :, :], tok[:, :, :], ACT.Copy).then_inc(tok_res_ready, 1)
                    if not last:
                        take_tokens(b + 1)
                    exp(b, 0, 0)
                    row(b, 1)
                    take_output(b, 0)
                    exp(b, 1, 0)
                    row(b, 2)
                    exp(b, 1, 1)
                    take_output(b, 1)
                    exp(b, 2, 0)
                    row(b, 3)
                    exp(b, 2, 1)
                    if not last:
                        take_normed(b + 1, 0)
                    exp(b, 2, 2)
                    take_output(b, 2)
                    exp(b, 3, 0)
                    if not last:
                        take_normed(b + 1, 1)
                    exp(b, 3, 1)
                    if not first:
                        keep_u(b - 1)
                    exp(b, 3, 2)
                    exp(b, 3, 3)
                    if not last:
                        take_qk(b + 1)
                    take_output(b, 3)

                act.wait_ge(a_consts, CONSTS)
                nc.scalar.activation(ident_r[:, :], ident[:, :], ACT.Copy).then_inc(ident_ready, 1)
                nc.scalar.activation(ident_bf[:, :], ident[:, :], ACT.Copy).then_inc(ident_ready, 1)
                take_x(0)
                take_tokens(0)
                take_normed(0, 0)
                take_normed(0, 1)
                take_qk(0)
                batch(0, first=True)
                act.wait_ge(e.w_step, 2)
                nc.scalar.activation(e.w[:, 2, :], e.w[:, 0, :], ACT.Exp, bias=e.w[:, 1, 0:1]).then_inc(e.softmax_ready, 1)
                with act.Fori(1, B - 1) as b:
                    batch(b)
                batch(B - 1, last=True)
                keep_x2(B - 1)
                keep_u(B - 1)

            @block.vector
            def _(dve):
                wide = [128, TILES, C]

                def center(b, semaphore, v, cen, small):
                    def chain(step, instruction):
                        instruction.then_inc(semaphore, 1)
                        dve.wait_ge(semaphore, LN * b + step)

                    chain(1, nc.vector.tensor_reduce(small[:, 0, :], v[:, :, :], AX.X, ALU.add))
                    chain(2, nc.vector.scalar_tensor_tensor(out=cen[:, :, :], in0=small[:, 0, :].unsqueeze(2).to_broadcast(wide),
                                                            scalar=-1.0 / C, in1=v[:, :, :], op0=ALU.mult, op1=ALU.add))
                    chain(3, nc.vector.tensor_tensor(sq[:, :, :], cen[:, :, :], cen[:, :, :], ALU.mult))
                    chain(4, nc.vector.tensor_reduce(small[:, 1, :], sq[:, :, :], AX.X, ALU.add))
                    nc.vector.tensor_scalar(small[:, 1, :], small[:, 1, :], 1.0 / C, LN_EPS, ALU.mult, ALU.add).then_inc(semaphore, 1)

                def center_x(b):
                    dve.wait_ge(tok_ready, b + 1)
                    center(b, ln_step, tok, cen, small)

                def norm_x(b):
                    dve.wait_ge(ln_rstd, b + 1)
                    at_least(dve, xnt_psum, 2 * b)
                    nc.vector.tensor_tensor(xn[:, :, :], cen[:, :, :], small[:, 2, :].unsqueeze(2).to_broadcast(wide),
                                            ALU.mult).then_inc(xn_ready, 1)

                def center_x2(b):
                    dve.wait_ge(back_done, SPANS * (b + 1))
                    center(b, ln2_step, tok2, cen2, small2)

                def norm_x2(b):
                    dve.wait_ge(ln2_rstd, b + 1)
                    at_least(dve, u_all_ready, b)
                    nc.vector.tensor_tensor(un[:, :, :], cen2[:, :, :], small2[:, 2, :].unsqueeze(2).to_broadcast(wide),
                                            ALU.mult).then_inc(u_ready, 1)
                    dve.wait_ge(u_ready, b + 1)
                    high = u_high[:, :, bass.ds(b, 1), :].rearrange("p i o c -> p i (o c)")
                    nc.vector.tensor_copy(high, un[:, :, :]).then_inc(u_high_ready, 1)
                    dve.wait_ge(u_high_ready, b + 1)
                    nc.vector.tensor_tensor(u_low[:, :, bass.ds(b, 1), :].rearrange("p i o c -> p i (o c)"), un[:, :, :],
                                            high.bitcast(F32), ALU.subtract).then_inc(u_low_ready, 1)

                def split_qk(b):
                    dve.wait_ge(q_high_ready, b + 1)
                    nc.vector.scalar_tensor_tensor(out=q_parts[C:, :].rearrange("p (h n) -> p h n", h=2),
                                                   in0=ps_s[C:, 0:2, :], scalar=float(C) ** -0.5,
                                                   in1=q_parts[C:, :].bitcast(F32).rearrange("p (h n) -> p h n", h=2),
                                                   op0=ALU.mult, op1=ALU.subtract).then_inc(q_ready, 1)
                    nc.vector.tensor_copy(q_row[0:C, :], q_parts[0:C, :].bitcast(F32)).then_inc(q_ready, 1)
                    dve.wait_ge(k_high_ready, b + 1)
                    nc.vector.tensor_tensor(k_one[0:C, :].rearrange("p (h n) -> p h n", h=2), ps_s[0:C, 2:4, :],
                                            k_high[0:C, :].bitcast(F32).rearrange("p (h n) -> p h n", h=2),
                                            ALU.subtract).then_inc(k_ready, 1)

                def take_values(b):
                    dve.wait_ge(v_psum, b + 1)
                    at_least(dve, pv_done, BLOCKS_T * b)
                    nc.vector.tensor_copy(v_one[:, :, 0:C], ps_s[:, NEXT, :].rearrange("p (i c) -> p i c", i=TILES)
                                          ).then_inc(v_ready, 1)

                def maximum(b, d):
                    at_least(dve, row_psum, SPANS * (b - 1) + d + 1)
                    for c, (i, at, n) in enumerate(pieces):
                        if i // 2 != d:
                            continue
                        dve.wait_ge(scores_ready, PIECES * b + c + 1)
                        if width(i) <= H:
                            nc.vector.tensor_reduce(max_parts[:, i, 0:1], ps_s[:, c % TURN, 0:n], AX.X, ALU.max,
                                                    negate=True).then_inc(part_ready, 1)
                            dve.wait_ge(part_ready, PIECES * b + c + 1)
                            nc.vector.tensor_copy(neg_max[:, i:i + 1], max_parts[:, i, 0:1]).then_inc(max_ready, 1)
                        else:
                            nc.vector.tensor_reduce(max_parts[:, i, at // H:at // H + 1], ps_s[:, c % TURN, 0:n], AX.X,
                                                    ALU.max, negate=True).then_inc(part_ready, 1)
                            if at:
                                dve.wait_ge(part_ready, PIECES * b + c + 1)
                                nc.vector.tensor_tensor(neg_max[:, i:i + 1], max_parts[:, i, 0:1], max_parts[:, i, 1:2],
                                                        ALU.min).then_inc(max_ready, 1)

                def output(b, d):
                    dve.wait_ge(back_psum, SPANS * b + d + 1)
                    if d == 0:
                        dve.wait_ge(tok_res_ready, b + 1)
                        at_least(dve, x2_ready, b)
                    got = ps_m[:, 0:2 * (C + 1)].rearrange("p (j c) -> p j c", j=2)
                    nc.vector.reciprocal(inv[:, :, :], got[:, :, C:C + 1]).then_inc(inv_ready, 1)
                    dve.wait_ge(inv_ready, SPANS * b + d + 1)
                    for j in range(2):
                        last = nc.vector.scalar_tensor_tensor(out=tok2[:, 2 * d + j, :], in0=got[:, j, 0:C],
                                                              scalar=inv[:, j, :], in1=tok_res[:, 2 * d + j, :],
                                                              op0=ALU.mult, op1=ALU.add)
                    last.then_inc(back_done, 1)

                def batch(b, first=False, last=False):
                    maximum(b, 0)
                    maximum(b, 1)
                    maximum(b, 2)
                    if not first:
                        center_x2(b - 1)
                    if not last:
                        center_x(b + 1)
                    maximum(b, 3)
                    output(b, 0)
                    if not first:
                        norm_x2(b - 1)
                    if not last:
                        norm_x(b + 1)
                    output(b, 1)
                    output(b, 2)
                    if not last:
                        split_qk(b + 1)
                    output(b, 3)
                    if not last:
                        take_values(b + 1)

                dve.wait_ge(a_consts, CONSTS)
                center_x(0)
                norm_x(0)
                split_qk(0)
                take_values(0)
                batch(0, first=True)
                filter_rows_and_weights(nc, dve, e)
                with dve.Fori(1, B - 1) as b:
                    batch(b)
                batch(B - 1, last=True)
                center_x2(B - 1)
                norm_x2(B - 1)


class ExpertTensors:
    pass


def expert_tensors(nc, ctx):
    def sb(name, shape, dt=F32):
        return ctx.enter_context(nc.sbuf_tensor(name, shape, dt))

    e = ExpertTensors()
    e.plus = sb("plus", [128, EXPERTS, FILTERS, C])
    e.minus = sb("minus", [128, EXPERTS, FILTERS, C])
    e.even = sb("even", [128, EXPERTS, FILTERS, C])
    e.odd = e.minus
    e.taps = sb("taps", [128, EXPERTS, AR_TAPS, C])
    e.ident = sb("ident_all", [128, 128])
    e.logits = sb("logits", [128, 2, EXPERTS])
    e.sigma = sb("sigma", [128, FILTERS])
    e.quarter = sb("quarter", [128, FILTERS])
    e.sigma4 = sb("sigma4", [128, FILTERS])
    e.w = sb("w", [128, 8, EXPERTS])
    e.wk = sb("w_sigma", [128, EXPERTS, FILTERS])
    spare = e.even.rearrange("p i k e -> p (i k e)")[0:FILTERS, :]
    e.rows = spare[:, 0:4 * PADS].bitcast(F32R).rearrange("k (r j) -> k r j", r=4)
    e.phi = spare[:, 4 * PADS:4 * PADS + L]
    e.hankel = [sb(f"hankel_{i}", [128, 4, H + 2], F32R) for i in range(2)]
    e.block_mix = [sb(f"block_mix_{i}", [128, EXPERTS, 2, 2, 128], F32R) for i in range(2)]
    e.ar_mix = sb("ar_mix", [128, EXPERTS, AR_TAPS, 2, 128], F32R)
    e.filters = nc.dram_tensor("filters", (FILTERS, 4, PADS), F32, kind="Internal").ap()
    names = """weights_in w_step softmax_ready wk_ready sum_step rows_step rows_ready filters_out
        zeros_ready ar_step ar_ready block_step block_ready passed"""
    (e.weights_in, e.w_step, e.softmax_ready, e.wk_ready, e.sum_step, e.rows_step, e.rows_ready, e.filters_out,
     e.zeros_ready, e.ar_step, e.ar_ready, e.block_step, e.block_ready, e.passed,
     ) = [ctx.enter_context(nc.semaphore(f"expert_{name}")) for name in names.split()]
    e.hankel_in = [ctx.enter_context(nc.semaphore(f"hankel_in_{i}")) for i in range(2)]
    return e


def load_hankel(sp, e, k, slot):
    sp.dma_start(e.hankel[slot][:, :, 0:H + 1].bitcast(F32),
                 bass.AP(e.filters.tensor, k * 4 * PADS, [[1, 128], [PADS, 4], [1, H + 1]])
                 ).then_inc(e.hankel_in[slot], 16)


def load_expert_weights(sp, ins, e):
    for j, name in enumerate(("log_weights", "gumbel")):
        sp.dma_start(e.logits[:, j, :], bass.AP(ins[name].tensor, 0, [[0, 128], [1, EXPERTS]])).then_inc(e.weights_in, 16)
    sp.dma_start(e.sigma[:, :], bass.AP(ins["sigma"].tensor, 0, [[0, 128], [1, FILTERS]])).then_inc(e.weights_in, 16)
    sp.dma_start(e.phi, ins["phi"][:, 0:L]).then_inc(e.weights_in, 16)
    for half in (0, C):
        for dst, name in ((e.plus, "M_phi_plus"), (e.minus, "M_phi_minus"), (e.taps, "M_u")):
            sp.dma_start(dst[half:half + C, :, :, :], ins[name].rearrange("i k d e -> d i k e")).then_inc(e.weights_in, 16)
    sp.wait_ge(e.rows_ready, 4)
    sp.dma_start(e.filters.rearrange("k r j -> k (r j)"),
                 e.rows.bitcast(F32).rearrange("k r j -> k (r j)")).then_inc(e.filters_out, 16)
    sp.wait_ge(e.filters_out, 16)
    for slot in range(2):
        load_hankel(sp, e, slot, slot)


def filter_rows_and_weights(nc, dve, e):
    def chain(semaphore, count, instruction):
        instruction.then_inc(semaphore, 1)
        dve.wait_ge(semaphore, count)

    w = e.w
    dve.wait_ge(e.weights_in, EXPERT_LOADS)
    chain(e.w_step, 1, nc.vector.tensor_tensor(w[:, 0, :], e.logits[:, 0, :], e.logits[:, 1, :], ALU.add))
    chain(e.w_step, 2, nc.vector.tensor_reduce(w[:, 1, 0:1], w[:, 0, :], AX.X, ALU.max, negate=True))
    chain(e.rows_step, 1, nc.vector.memset(e.rows.bitcast(F32), 0.0))
    for lag in range(2):
        reverse = e.phi[:, lag::2][:, ::-1]
        chain(e.rows_ready, 2 * lag + 1, nc.vector.tensor_copy(e.rows[:, 2 * lag, 0:H], reverse))
        chain(e.rows_ready, 2 * lag + 2, nc.vector.tensor_tensor(
            e.rows[:, 2 * lag + 1, 0:H], reverse, e.rows[:, 2 * lag, 0:H].bitcast(F32), ALU.subtract))
    dve.wait_ge(e.softmax_ready, 2)
    chain(e.w_step, 3, nc.vector.tensor_reduce(w[:, 1, 1:2], w[:, 2, :], AX.X, ALU.add))
    chain(e.w_step, 4, nc.vector.reciprocal(w[:, 1, 2:3], w[:, 1, 1:2]))
    chain(e.w_step, 5, nc.vector.tensor_scalar(w[:, 3, :], w[:, 2, :], w[:, 1, 2:3], None, ALU.mult))
    chain(e.w_step, 6, nc.vector.tensor_reduce(w[:, 1, 3:4], w[:, 3, :], AX.X, ALU.max))
    chain(e.w_step, 7, nc.vector.tensor_scalar(w[:, 4, :], w[:, 3, :], w[:, 1, 3:4], None, ALU.is_equal))
    chain(e.w_step, 8, nc.vector.tensor_copy(w[:, 5, 0:1], w[:, 4, 0:1]))
    for j in range(1, EXPERTS):
        chain(e.w_step, 8 + j, nc.vector.tensor_tensor(w[:, 5, j:j + 1], w[:, 5, j - 1:j], w[:, 4, j:j + 1], ALU.add))
    at = 8 + EXPERTS - 1
    chain(e.w_step, at + 1, nc.vector.tensor_scalar(w[:, 6, :], w[:, 5, :], 1.0, None, ALU.is_equal))
    chain(e.w_step, at + 2, nc.vector.tensor_tensor(w[:, 6, :], w[:, 6, :], w[:, 4, :], ALU.mult))
    chain(e.w_step, at + 3, nc.vector.tensor_tensor(w[:, 7, :], w[:, 6, :], w[:, 3, :], ALU.subtract))
    chain(e.w_step, at + 4, nc.vector.tensor_tensor(w[:, 7, :], w[:, 7, :], w[:, 3, :], ALU.add))
    for i in range(EXPERTS):
        nc.vector.tensor_scalar(e.wk[:, i, :], e.sigma4[:, :], w[:, 7, i:i + 1], None, ALU.mult).then_inc(e.wk_ready, 1)


def clear_blocks(nc, pool, e):
    nc.gpsimd.memset(e.quarter[:, :], 0.25).then_inc(e.zeros_ready, 1)
    pool.wait_ge(e.zeros_ready, 1)
    pool.wait_ge(e.weights_in, EXPERT_LOADS)
    nc.gpsimd.tensor_tensor(e.sigma4[:, :], e.sigma[:, :], e.quarter[:, :], ALU.pow).then_inc(e.softmax_ready, 1)
    for i in range(2):
        nc.gpsimd.memset(e.block_mix[i][:, :, :, :, :].bitcast(F32), 0.0).then_inc(e.zeros_ready, 1)
    nc.gpsimd.memset(e.ar_mix[:, :, :, :, :].bitcast(F32), 0.0).then_inc(e.zeros_ready, 1)


def weigh_and_sum(nc, pool, e):
    pool.wait_ge(e.wk_ready, EXPERTS)
    done = 0
    for m in (e.plus, e.minus):
        for i in range(EXPERTS):
            done += 1
            nc.gpsimd.tensor_tensor(m[:, i, :, :], m[:, i, :, :], e.wk[:, i, :].unsqueeze(2).to_broadcast([128, FILTERS, C]),
                                    ALU.mult).then_inc(e.sum_step, 1)
            pool.wait_ge(e.sum_step, done)
            if i:
                done += 1
                nc.gpsimd.tensor_tensor(m[:, i, :, :], m[:, i, :, :], m[:, i - 1, :, :], ALU.add).then_inc(e.sum_step, 1)
                pool.wait_ge(e.sum_step, done)


SUMMED = 2 * (2 * EXPERTS - 1)


def lag_matrices(nc, pool, e):
    pool.wait_ge(e.filters_out, 16)
    pool.wait_ge(e.sum_step, SUMMED)
    for i in range(EXPERTS):
        nc.gpsimd.tensor_tensor(e.even[:, i, :, :], e.plus[:, i, :, :], e.minus[:, i, :, :], ALU.add).then_inc(e.sum_step, 1)
        pool.wait_ge(e.sum_step, SUMMED + i + 1)
    for i in range(EXPERTS):
        nc.gpsimd.tensor_tensor(e.odd[:, i, :, :], e.plus[:, i, :, :], e.minus[:, i, :, :], ALU.subtract).then_inc(e.sum_step, 1)


def tap_blocks(nc, pool, e):
    done = 0
    for i in range(EXPERTS):
        done += 1
        nc.gpsimd.tensor_tensor(e.taps[:, i, :, :], e.taps[:, i, :, :],
                                e.w[:, 7, i:i + 1].unsqueeze(2).to_broadcast([128, AR_TAPS, C]),
                                ALU.mult).then_inc(e.ar_step, 1)
        pool.wait_ge(e.ar_step, done)
        if i:
            done += 1
            nc.gpsimd.tensor_tensor(e.taps[:, i, :, :], e.taps[:, i, :, :], e.taps[:, i - 1, :, :],
                                    ALU.add).then_inc(e.ar_step, 1)
            pool.wait_ge(e.ar_step, done)
    pool.wait_ge(e.zeros_ready, 4)
    for half in (0, C):
        dst = e.ar_mix[half:half + C, :, :, :, half:half + C]
        nc.gpsimd.tensor_copy(dst[:, :, :, 0, :], e.taps[half:half + C]).then_inc(e.ar_step, 1)
    pool.wait_ge(e.ar_step, done + 2)
    for half in (0, C):
        dst = e.ar_mix[half:half + C, :, :, :, half:half + C]
        nc.gpsimd.tensor_tensor(dst[:, :, :, 1, :], e.taps[half:half + C], dst[:, :, :, 0, :].bitcast(F32),
                                ALU.subtract).then_inc(e.ar_ready, 1)


def filter_blocks(nc, pool, e, k, slot):
    parts = [(half, lag, src[half:half + C, :, bass.ds(k, 1), :].rearrange("p n o e -> p (n o) e"))
             for half in (0, C) for lag, src in enumerate((e.even, e.odd))]
    for half, lag, src in parts:
        dst = e.block_mix[slot][half:half + C, :, lag, :, half:half + C]
        nc.gpsimd.tensor_copy(dst[:, :, 0, :], src).then_inc(e.block_step, 1)
    pool.wait_ge(e.block_step, BLOCKS * (k + 1))
    pool.sem_inc(e.passed, 1)
    for half, lag, src in parts:
        dst = e.block_mix[slot][half:half + C, :, lag, :, half:half + C]
        nc.gpsimd.tensor_tensor(dst[:, :, 1, :], src, dst[:, :, 0, :].bitcast(F32), ALU.subtract).then_inc(e.block_ready, 1)


def expert_stage(nc, ins, e, x2, u_all, u_high, u_low, out):
    HEAD_BANDS = [(0, 64, 3), (64, 128, 2)]
    HEAD = 128
    TAIL_BANDS = [(128, 256, 1), (256, 512, 0)]
    TERMS = [(0, 0), (1, 0), (0, 1)]
    PAIRS = B // 2
    STEPS = 2 * PAIRS

    with ExitStack() as ctx:
        def sb(name, shape, dt=F32):
            return ctx.enter_context(nc.sbuf_tensor(name, shape, dt))

        def sem(name):
            return ctx.enter_context(nc.semaphore(name))

        u_t = [sb(f"u_t_{part}", [128, PAIRS, 2, H + 2], F32R) for part in range(2)]
        head = [[sb(f"head_{i}_{part}", [128, 2, PAIRS, 2, HEAD], F32R) for part in range(2)] for i in range(2)]
        tail = [[sb(f"tail_{q}_{part}", [128, 2, 2, H - HEAD], F32R) for part in range(2)] for q in range(PAIRS)]
        spent = e.plus.rearrange("p i k e -> p (i k e)")
        result = [spent[:, q * L:(q + 1) * L] for q in range(PAIRS)]

        ps_conv = [ctx.enter_context(nc.psum_tensor(f"ps_conv{i}", [128, 2 * H], F32)) for i in range(2)]
        ps_head = ctx.enter_context(nc.psum_tensor("ps_head", [128, PAIRS, 2, HEAD], F32))
        ps_mid = ctx.enter_context(nc.psum_tensor("ps_mid", [128, PAIRS, 2, HEAD], F32))
        ps_tail = [ctx.enter_context(nc.psum_tensor(f"ps_tail{q}", [128, 2, 2 * HEAD], F32)) for q in range(PAIRS)]

        names = "pads_ready ut_psum ut_high ut_low conv_psum conv_high conv_low mixed_in out_done"
        (pads_ready, ut_psum, ut_high, ut_low, conv_psum, conv_high, conv_low, mixed_in,
         out_done) = [sem(name) for name in names.split()]
        result_ready = [sem(f"result_ready_{q}") for q in range(PAIRS)]

        def converted(k, q, a, part):
            return [(head[k % 2][part][:, :, q, a, :], 0, HEAD), (tail[q][part][:, a, :, :], HEAD, H)]

        by_parity = [r.rearrange("p (i a) -> p a i", a=2) for r in result]
        head_out = [(q, by_parity[q][:, :, 0:HEAD], ps_head[:, q, :, :]) for q in range(PAIRS)]
        mid_out = [(q, by_parity[q][:, :, HEAD:2 * HEAD], ps_mid[:, q, :, :]) for q in range(PAIRS)]
        tail_out = [(q, by_parity[q][:, :, 2 * HEAD:], ps_tail[q][:, :, :]) for q in range(PAIRS)]

        with nc.Block() as block:

            @block.sync
            def _(sp):
                with sp.Fori(1, FILTERS // 2) as pair:
                    for slot in range(2):
                        k = 2 * pair + slot
                        sp.wait_ge(conv_psum, STEPS * (k - 1))
                        load_hankel(sp, e, k, slot)
                for q in range(PAIRS):
                    sp.wait_ge(result_ready[q], 3)
                    sp.dma_start(out.rearrange("b c t -> (b c) t")[128 * q:128 * (q + 1), :], result[q]).then_inc(out_done, 16)
                sp.wait_ge(out_done, 16 * PAIRS)

            @block.gpsimd
            def _(pool):
                for part in range(2):
                    nc.gpsimd.memset(u_t[part][:, :, :, 0:2].bitcast(F32), 0.0).then_inc(pads_ready, 1)
                with pool.Fori(1, FILTERS // 2) as pair:
                    for slot in range(2):
                        k = 2 * pair + slot
                        pool.wait_ge(mixed_in, 2 * (k - 1))
                        pool.wait_ge(e.block_ready, BLOCKS * k)
                        filter_blocks(nc, pool, e, k, slot)

            @block.tensor
            def _(pe):
                pairs = [[part[:, :, 2 * q:2 * q + 2, :].rearrange("p i b c -> p i (b c)") for part in (u_high, u_low)]
                         for q in range(PAIRS)]
                cleared = set()

                def add_out(bank, dst, w_block, data):
                    mm = nc.tensor.matmul(dst, w_block, data, start=bank not in cleared, stop=True, skip_group_check=True)
                    cleared.add(bank)
                    return mm

                def convolve(slot, q, a, at):
                    dst = ps_conv[at % 2]
                    for lag in range(2):
                        parity = a ^ lag
                        shift = 1 if lag and not a else 0
                        for delta in range(SPANS):
                            first = 128 * delta
                            for n, (wp, dp) in enumerate(TERMS):
                                row = e.hankel[slot][:, 2 * lag + dp, first + shift:H + shift][:, ::-1]
                                mm = nc.tensor.matmul(dst[:, lag * H + first:(lag + 1) * H],
                                                      pairs[q][wp][:, 2 * delta + parity, :], row,
                                                      start=(delta == 0 and n == 0),
                                                      stop=(delta == SPANS - 1 and n == len(TERMS) - 1))
                    mm.then_inc(conv_psum, 1)

                def mix_tail(slot, q):
                    for lag in range(2):
                        for (lo, hi, band), bank, dst in zip(TAIL_BANDS, ("mid", f"tail{q}"),
                                                             (ps_mid[:, q, :, :], ps_tail[q][:, :, :])):
                            for wp, dp in TERMS:
                                mm = add_out(bank, dst, e.block_mix[slot][:, band, lag, wp, :],
                                             tail[q][dp][:, :, lag, lo - HEAD:hi - HEAD])
                    return mm

                def mix_head(slot):
                    for lag in range(2):
                        for lo, hi, band in HEAD_BANDS:
                            for wp, dp in TERMS:
                                mm = add_out("head", ps_head[:, :, :, lo:hi].rearrange("p q a i -> p (q a) i"),
                                             e.block_mix[slot][:, band, lag, wp, :],
                                             head[slot][dp][:, lag, :, :, lo:hi].rearrange("p q a i -> p (q a) i"))
                    return mm

                for q in range(PAIRS):
                    for i in range(TILES):
                        at = (i % 2) * H + 128 * (i // 2)
                        mm = nc.tensor.transpose(ps_conv[q][:, at:at + 128],
                                                 u_all[:, i, 2 * q:2 * q + 2, :].rearrange("p b c -> p (b c)"),
                                                 e.ident[:, :])
                    mm.then_inc(ut_psum, 1)
                for q in range(PAIRS):
                    for a in range(2):
                        for delta in range(SPANS):
                            bank, dst = (("head", ps_head[:, q, a, :]), ("mid", ps_mid[:, q, a, :]),
                                         (f"tail{q}", ps_tail[q][:, a, 0:HEAD]),
                                         (f"tail{q}", ps_tail[q][:, a, HEAD:]))[delta]
                            add_out(bank, dst, x2[:, 2 * delta + a, 2 * q:2 * q + 2, :].rearrange("p b c -> p (b c)"),
                                    e.ident[:, :])
                pe.wait_ge(ut_low, PAIRS)
                pe.wait_ge(pads_ready, 2)
                pe.wait_ge(e.ar_ready, 2)
                for a in range(2):
                    for tap in range(AR_TAPS):
                        parity = (a + tap) % 2
                        back = (tap + parity - a) // 2
                        for wp, dp in TERMS:
                            for lo, hi, band in HEAD_BANDS:
                                add_out("head", ps_head[:, :, a, lo:hi], e.ar_mix[:, band, tap, wp, :],
                                        u_t[dp][:, :, parity, 2 + lo - back:2 + hi - back])
                            add_out("mid", ps_mid[:, :, a, :], e.ar_mix[:, 1, tap, wp, :],
                                    u_t[dp][:, :, parity, 2 + HEAD - back:2 + 2 * HEAD - back])
                            for q in range(PAIRS):
                                add_out(f"tail{q}", ps_tail[q][:, a, :], e.ar_mix[:, 0, tap, wp, :],
                                        u_t[dp][:, q, parity, 2 + 2 * HEAD - back:2 + H - back])

                def one_filter(pair, slot, first=False):
                    k = 2 * pair + slot
                    pe.wait_ge(e.hankel_in[slot], 16 * (pair + 1))
                    for j in range(STEPS):
                        q, a = divmod(j, 2)
                        m = STEPS * k + j
                        at_least(pe, conv_low, 2 * (m - 1))
                        convolve(slot, q, a, j)
                        if j == 0 and not first:
                            pe.wait_ge(conv_low, 2 * m)
                            mix_tail(1 - slot, PAIRS - 1)
                            mix_head(1 - slot).then_inc(mixed_in, 1)
                        if j == 2:
                            pe.wait_ge(conv_low, 2 * m)
                            pe.wait_ge(e.block_ready, BLOCKS * (k + 1))
                            mix_tail(slot, 0).then_inc(mixed_in, 1)

                one_filter(0, 0, first=True)
                one_filter(0, 1)
                with pe.Fori(1, FILTERS // 2) as pair:
                    one_filter(pair, 0)
                    one_filter(pair, 1)
                pe.wait_ge(conv_low, 2 * STEPS * FILTERS)
                mix_tail(1, PAIRS - 1)
                mix_head(1).then_inc(mixed_in, 1)

            @block.scalar
            def _(act):
                for q in range(PAIRS):
                    act.wait_ge(ut_psum, q + 1)
                    nc.scalar.activation(u_t[0][:, q, :, 2:], ps_conv[q][:, :].rearrange("p (a i) -> p a i", a=2),
                                         ACT.Copy).then_inc(ut_high, 1)

                def one_filter(k, slot, first=False):
                    for j in range(STEPS):
                        q, a = divmod(j, 2)
                        m = STEPS * k + j
                        act.wait_ge(conv_psum, m + 1)
                        if a == 0 and not first:
                            act.wait_ge(mixed_in, 2 * k - 1 + q)
                        for dst, lo, hi in converted(slot, q, a, 0):
                            nc.scalar.activation(dst, ps_conv[j % 2][:, :].rearrange("p (l i) -> p l i", l=2)[:, :, lo:hi],
                                                 ACT.Copy).then_inc(conv_high, 1)

                one_filter(0, 0, first=True)
                one_filter(1, 1)
                with act.Fori(1, FILTERS // 2) as pair:
                    for slot in range(2):
                        one_filter(2 * pair + slot, slot)
                act.wait_ge(mixed_in, 2 * FILTERS)
                for q, dst, src in [tail_out[0]] + mid_out:
                    nc.scalar.activation(dst, src, ACT.Copy).then_inc(result_ready[q], 1)

            @block.vector
            def _(dve):
                for q in range(PAIRS):
                    dve.wait_ge(ut_high, q + 1)
                    nc.vector.tensor_tensor(u_t[1][:, q, :, 2:], ps_conv[q][:, :].rearrange("p (a i) -> p a i", a=2),
                                            u_t[0][:, q, :, 2:].bitcast(F32), ALU.subtract).then_inc(ut_low, 1)

                def one_filter(k, slot):
                    for j in range(STEPS):
                        q, a = divmod(j, 2)
                        m = STEPS * k + j
                        dve.wait_ge(conv_high, 2 * (m + 1))
                        for n, (dst, lo, hi) in enumerate(converted(slot, q, a, 1)):
                            high = converted(slot, q, a, 0)[n][0]
                            nc.vector.tensor_tensor(dst, ps_conv[j % 2][:, :].rearrange("p (l i) -> p l i", l=2)[:, :, lo:hi],
                                                    high.bitcast(F32), ALU.subtract).then_inc(conv_low, 1)

                one_filter(0, 0)
                one_filter(1, 1)
                with dve.Fori(1, FILTERS // 2) as pair:
                    for slot in range(2):
                        one_filter(2 * pair + slot, slot)
                dve.wait_ge(mixed_in, 2 * FILTERS)
                for q, dst, src in head_out + [tail_out[1]]:
                    nc.vector.tensor_copy(dst, src).then_inc(result_ready[q], 1)


def build(nc, ins, out):
    with ExitStack() as ctx:
        x1 = ctx.enter_context(nc.sbuf_tensor("x1", [C, B * L], F32))
        mamba_stage(nc, ins, x1)
        x2 = ctx.enter_context(nc.sbuf_tensor("x2", [128, TILES, B, C], F32))
        u_all = ctx.enter_context(nc.sbuf_tensor("u_all", [128, TILES, B, C], F32))
        u_high = ctx.enter_context(nc.sbuf_tensor("u_high", [128, TILES, B, C], F32R))
        u_low = ctx.enter_context(nc.sbuf_tensor("u_low", [128, TILES, B, C], F32R))
        e = expert_tensors(nc, ctx)
        attention_stage(nc, ins, e, x1, x2, u_all, u_high, u_low)
        expert_stage(nc, ins, e, x2, u_all, u_high, u_low, out)


def kernel(**inputs):
    import numpy as np
    import concourse.bacc as bacc
    from concourse.bass_utils import run_bass_kernel_spmd

    nc = bacc.Bacc("TRN2", target_bir_lowering=False, num_devices=1)
    given = {k.replace("L0_conv_", "").replace("L1_attn_", "").replace("L1_ffn_", ""): np.asarray(v)
             for k, v in inputs.items()}
    arrays = {"x": given["x"].reshape(B, C, L)}
    for d in DIRS:
        w_in, conv_w, w_x = given[f"W_in_{d}"], given[f"conv_w_{d}"], given[f"W_x_{d}"]
        tap = [np.broadcast_to(conv_w[:, j], (C, D)) for j in range(2)]
        arrays[f"packed_in_{d}"] = np.stack([np.concatenate([w_in[:, :D], w_in[:, :D]]),
                                             np.concatenate([tap[1], tap[0]]),
                                             np.concatenate([w_in[:, D:], np.zeros((C, D), w_in.dtype)])], axis=1)
        arrays[f"packed_inner_{d}"] = np.concatenate(
            [w_x[:, R:]] * PARTS + [w_x[:, :R], given[f"W_out_{d}"], given[f"A_log_{d}"],
                                    given[f"conv_b_{d}"][:, None], given[f"D_{d}"][:, None]], axis=1)
        arrays[f"W_dt_{d}"] = given[f"W_dt_{d}"]
        arrays[f"b_dt_{d}"] = given[f"b_dt_{d}"][None]
    for name in ("Wq", "Wk", "Wv"):
        arrays[name] = given[name].T
    for name in ("sigma", "M_phi_plus", "M_phi_minus", "M_u", "log_weights", "gumbel"):
        arrays[name] = given[name]
    arrays["phi"] = given["phi"].T
    arrays["gn_cols"] = np.stack([given["gn_gamma"], given["gn_beta"]], axis=1)
    feed, ins = {}, {}
    for name, a in arrays.items():
        a = np.ascontiguousarray(a)
        feed[f"in_{name}"] = a
        ins[name] = nc.dram_tensor(f"in_{name}", a.shape, mybir.dt.from_np(a.dtype), kind="ExternalInput").ap()
    out = nc.dram_tensor("out_0", (B, C, L), F32, kind="ExternalOutput").ap()
    build(nc, ins, out)
    r = run_bass_kernel_spmd(nc, [feed], core_ids=[0])
    return r.results[0]["out_0"].reshape(B, C, 32, 32)
```

```python
from contextlib import ExitStack

import concourse.bass as bass
from concourse import mybir

F32 = mybir.dt.float32
BF16 = mybir.dt.bfloat16
F32R = mybir.dt.float32r
ALU = mybir.AluOpType
ACT = mybir.ActivationFunctionType
AX = mybir.AxisListType

B = 4
C = 64
L = 1024
H = 512
D = 128
N = 16
R = 8
GROUP = 16
GN_EPS = 1e-5
LN_EPS = 1e-5
DIRS = "fb"
DEEP = 4
PAIR = 2
Y_LAG = 3
TILES = L // 128
SPANS = TILES // 2
SPAN = 2 * 128
EXPERTS = 4
FILTERS = 16
AR_TAPS = 3
PADS = 640
BLOCKS = 4
EXPERT_LOADS = 16 * (1 + 2 * 3)
ATTENTION_LOADS = 16 * (1 + 5)
MASKED = -1e30
A_LOG_MAX = 60.0
PARTS = 3
BC = 2 * N
DT_ROW = PARTS * BC


def at_least(engine, semaphore, count):
    if isinstance(count, int) and count <= 0:
        return
    engine.wait_ge(semaphore, count)


class Shared:
    pass


def attention_tensors(nc, ctx):
    def sb(name, shape, dt=F32):
        return ctx.enter_context(nc.sbuf_tensor(name, shape, dt))

    a = Shared()
    a.ident = sb("ident", [128, 128])
    a.ident_r = sb("ident_r", [128, 128], F32R)
    a.ident_bf = sb("ident_bf", [128, 128], BF16)
    a.mask = sb("mask", [128, 2, 2, 128], BF16)
    a.mask_t = sb("mask_t", [128, 2, 2, 128], BF16)
    a.wq, a.wk = (sb(name, [C, 2, C]) for name in ("wq", "wk"))
    a.wv = sb("wv", [C, C])
    a.tok = sb("tok", [128, TILES, C])
    a.small = sb("small", [128, 3, TILES])
    a.minus_half = sb("minus_half", [128, TILES])
    a.q_parts = sb("q_parts", [128, L], F32R)
    a.k_high = sb("k_high", [128, L], F32R)
    a.q_row = sb("q_row", [128, L], F32R)
    a.k_one = sb("k_one", [128, L], F32R)
    a.v_one = sb("v_one", [128, TILES, C + 1])
    names = "zeros consts weights_in idents"
    a.zeros, a.consts, a.weights_in, a.idents = [ctx.enter_context(nc.semaphore(f"a_{name}")) for name in names.split()]
    return a


def norm_tensors(nc, ctx):
    def sb(name, shape, dt=F32):
        return ctx.enter_context(nc.sbuf_tensor(name, shape, dt))

    g = Shared()
    g.cols = sb("gn_cols", [C, 2])
    g.mixed = sb("mixed", [C, L])
    g.bn = sb("bn", [C, 2, 6])
    g.stats = sb("stats", [C, 32])
    g.stats_t = sb("stats_t", [C, 32])
    g.group_t = sb("group_t", [C, 2])
    g.group_w = sb("group_w", [C, 32])
    g.group = sb("group", [C, 32])
    g.gn = sb("gn", [C, 6])
    names = "aggregate mixed_ready step rstd_ready ready act_ready x1_ready"
    (g.aggregate, g.mixed_ready, g.step, g.rstd_ready, g.ready, g.act_ready,
     g.x1_ready) = [ctx.enter_context(nc.semaphore(f"gn_{name}")) for name in names.split()]
    return g


GN_STEPS = 12


def norm_stats(nc, dve, g, b):
    gn, group, stats = g.gn, g.group, g.stats

    def chain(step, instruction):
        instruction.then_inc(g.step, 1)
        dve.wait_ge(g.step, GN_STEPS * b + step)

    dve.wait_ge(g.mixed_ready, b + 1)
    for h in range(2):
        chain(h + 1, nc.vector.bn_stats(g.bn[:, h, :], g.mixed[:, h * H:(h + 1) * H]))
    dve.sem_inc(g.aggregate, 1)
    chain(3, nc.vector.bn_aggr(stats[:, 0:2], g.bn[:, :, :].rearrange("c a b -> c (a b)")))
    chain(4, nc.vector.scalar_tensor_tensor(out=stats[:, 1:2], in0=stats[:, 0:1], scalar=stats[:, 0:1],
                                            in1=stats[:, 1:2], op0=ALU.mult, op1=ALU.add))
    chain(5, nc.vector.transpose(g.stats_t[:, :], stats[:, :]))
    chain(6, nc.vector.tensor_reduce(g.group_t[:, :], g.stats_t[:, :].rearrange("c (g k) -> c g k", k=GROUP),
                                     AX.X, ALU.add))
    chain(7, nc.vector.tensor_scalar(g.group_w[:, :].rearrange("c (g k) -> c g k", k=GROUP),
                                     g.group_t[:, :].unsqueeze(2).to_broadcast([C, 2, GROUP]),
                                     1.0 / GROUP, None, ALU.mult))
    chain(8, nc.vector.transpose(group[:, :], g.group_w[:, :]))
    chain(9, nc.vector.tensor_scalar(gn[:, 1:2], group[:, 0:1], group[:, 0:1], -1.0, ALU.mult, ALU.mult))
    chain(10, nc.vector.tensor_scalar(gn[:, 2:3], gn[:, 1:2], group[:, 1:2], GN_EPS, ALU.add, ALU.add))


def norm_rstd(nc, pool, g, minus_half, b):
    pool.wait_ge(g.step, GN_STEPS * b + 10)
    nc.gpsimd.tensor_tensor(g.gn[:, 3:4], g.gn[:, 2:3], minus_half[0:C, 0:1], ALU.pow).then_inc(g.rstd_ready, 1)


def norm_scale(nc, dve, g, b):
    gn = g.gn

    def chain(step, instruction):
        instruction.then_inc(g.step, 1)
        dve.wait_ge(g.step, GN_STEPS * b + step)

    dve.wait_ge(g.rstd_ready, b + 1)
    chain(11, nc.vector.tensor_scalar(gn[:, 4:5], gn[:, 3:4], g.cols[:, 0:1], None, ALU.mult))
    chain(12, nc.vector.tensor_scalar(gn[:, 1:2], g.group[:, 0:1], gn[:, 4:5], -1.0, ALU.mult, ALU.mult))
    nc.vector.tensor_scalar(gn[:, 5:6], gn[:, 1:2], g.cols[:, 1:2], None, ALU.add).then_inc(g.ready, 1)


def norm_silu(nc, act, g, b):
    act.wait_ge(g.ready, b + 1)
    nc.scalar.activation(g.mixed[:, :], g.mixed[:, :], ACT.Silu, scale=g.gn[:, 4:5],
                         bias=g.gn[:, 5:6]).then_inc(g.act_ready, 1)


TOKEN_NORM = 5


def center_tokens(nc, dve, semaphore, count, v, cen, sq, small, lo=0, hi=TILES):
    v, cen, sq, small = v[:, lo:hi, :], cen[:, lo:hi, :], sq[:, lo:hi, :], small[:, :, lo:hi]

    def chain(step, instruction):
        instruction.then_inc(semaphore, 1)
        dve.wait_ge(semaphore, count + step)

    chain(1, nc.vector.tensor_reduce(small[:, 0, :], v, AX.X, ALU.add))
    chain(2, nc.vector.scalar_tensor_tensor(out=cen, in0=small[:, 0, :].unsqueeze(2).to_broadcast([128, hi - lo, C]),
                                            scalar=-1.0 / C, in1=v, op0=ALU.mult, op1=ALU.add))
    chain(3, nc.vector.tensor_tensor(sq, cen, cen, ALU.mult))
    chain(4, nc.vector.tensor_reduce(small[:, 1, :], sq, AX.X, ALU.add))
    nc.vector.tensor_scalar(small[:, 1, :], small[:, 1, :], 1.0 / C, LN_EPS, ALU.mult, ALU.add).then_inc(semaphore, 1)


def mamba_stage(nc, ins, a, g, e, x1):
    with ExitStack() as ctx:
        def sb(name, shape, dt=F32):
            return ctx.enter_context(nc.sbuf_tensor(name, shape, dt))

        def sem(name):
            return ctx.enter_context(nc.semaphore(name))

        x_pair = sb("x_pair", [2 * C, B, L + 1])
        x_flat = x_pair.rearrange("c b t -> c (b t)")
        packed_in = [sb(f"packed_in_{d}", [2 * C, 3, D]) for d in DIRS]
        w_in, taps, w_gate = ([p[:, j, :] for p in packed_in] for j in range(3))
        w_conv = [sb(f"w_conv_{d}", [2 * C, D]) for d in DIRS]
        packed_inner = [sb(f"packed_inner_{d}", [D, DT_ROW + R + C + N + 2]) for d in DIRS]
        w_x = [p[:, 0:DT_ROW + R] for p in packed_inner]
        w_out = [p[:, DT_ROW + R:DT_ROW + R + C] for p in packed_inner]
        a_log = [p[:, DT_ROW + R + C:DT_ROW + R + C + N] for p in packed_inner]
        cols = [p[:, DT_ROW + R + C + N:] for p in packed_inner]
        w_dt = [sb(f"w_dt_{d}", [128, D]) for d in DIRS]
        a_neg = [sb(f"a_neg_{d}", [D, N]) for d in DIRS]
        ident = a.ident
        pick = sb("pick", [DT_ROW, BC], BF16)
        spread = sb("spread", [DT_ROW, BC, 128], BF16)
        xc = [sb(f"xc_{d}", [D, L]) for d in DIRS]
        gate = [sb(f"gate_{d}", [D, L]) for d in DIRS]
        dt = [sb(f"dt_{d}", [D, L]) for d in DIRS]
        dtx = [sb(f"dtx_{d}", [D, L]) for d in DIRS]
        bc_parts = [sb(f"bc_parts_{d}", [DT_ROW, L], BF16) for d in DIRS]
        gated = [sb(f"gated_{d}", [D, L]) for d in DIRS]
        z_raw = sb("z_raw", [D, L])
        scratch = sb("scratch", [D, L])
        soft = sb("soft", [D, L])
        one_plus = sb("one_plus", [D, L])
        dt_low = sb("dt_low", [128, L])
        decay = [sb(f"decay_{i}", [D, L]) for i in range(DEEP)]
        hidden = [sb(f"hidden_{i}", [D, L]) for i in range(DEEP)]
        c_wide = [sb(f"c_wide_{i}", [D, L]) for i in range(DEEP)]
        drive = [sb(f"drive_{i}", [D, L]) for i in range(PAIR)]
        prod = [sb(f"prod_{i}", [D, L]) for i in range(PAIR)]
        mixed = g.mixed
        xn_t = z_raw[0:C, :]
        cen, sq = (soft[:, j * H:(j + 1) * H].rearrange("p (i c) -> p i c", c=C) for j in range(2))
        xn = one_plus[:, 0:H].rearrange("p (i c) -> p i c", c=C)

        ps_b = ctx.enter_context(nc.psum_tensor("ps_b", [128, L], F32))
        ps_c = ctx.enter_context(nc.psum_tensor("ps_c", [128, L], F32))
        ps_y = ctx.enter_context(nc.psum_tensor("ps_y", [128, L], F32))
        ps_w = ctx.enter_context(nc.psum_tensor("ps_w", [128, L], F32))

        names = """weights_in x_in z_taken consts w_conv_ready spread_ready a_ready b_wide_ready c_psum_ready
            c_wide_ready decay_ready drive_ready hidden_ready prod_ready prod_summed xp_ready xc_ready
            z_ready gate_ready xdb_ready high_ready dt_low_ready rest_ready mid_ready parts_ready
            dt_psum_ready abs_ready exp_ready ln_ready relu_ready dt_ready dtx_ready y_taken gated_ready
            out_ready a_log_ready one_plus_ready lost_ready tok_psum tok_ready ln_step ln_rstd xn_ready
            xnt_psum xnt_ready q_psum q_high_ready q_ready k_psum k_high_ready k_ready v_psum v_ready"""
        (weights_in, x_in, z_taken, consts, w_conv_ready, spread_ready, a_ready, b_wide_ready, c_psum_ready,
         c_wide_ready, decay_ready, drive_ready, hidden_ready, prod_ready, prod_summed, xp_ready, xc_ready,
         z_ready, gate_ready, xdb_ready, high_ready, dt_low_ready, rest_ready, mid_ready, parts_ready,
         dt_psum_ready, abs_ready, exp_ready, ln_ready, relu_ready, dt_ready, dtx_ready, y_taken,
         gated_ready, out_ready, a_log_ready, one_plus_ready, lost_ready, tok_psum, tok_ready, ln_step,
         ln_rstd, xn_ready, xnt_psum, xnt_ready, q_psum, q_high_ready, q_ready, k_psum, k_high_ready,
         k_ready, v_psum, v_ready,
         ) = [sem(name) for name in names.split()]
        first_in = [sem(f"first_in_{d}") for d in DIRS]
        FIRST = 16 * 3, 16
        WEIGHTS = 16 * (2 * 3 + 1)
        X_LOADS = 16 * 2
        CONSTS = 9 + PARTS

        AHEAD = [[0], [1, 2], [3, 4]] + [[s + 2] for s in range(3, N - 2)] + [[], []]

        def halves(t):
            return [t[:, h * H:(h + 1) * H] for h in range(L // H)]

        with nc.Block() as block:

            @block.sync
            def _(sp):
                src = ins["x"].rearrange("b c t -> c b t")

                def load_x(lo, hi, done):
                    sp.dma_start(x_pair[0:C, lo:hi, 0:L], src[:, lo:hi, :]).then_inc(done, 16)
                    sp.dma_start(x_pair[C:, lo:hi, 1:], src[:, lo:hi, :]).then_inc(done, 16)

                sp.dma_start(packed_in[0][:, :, :], ins["packed_in_f"]).then_inc(first_in[0], 16)
                load_x(0, 1, first_in[0])
                for i, d in enumerate(DIRS):
                    if i:
                        sp.dma_start(packed_in[i][:, :, :], ins[f"packed_in_{d}"]).then_inc(first_in[i], 16)
                    sp.dma_start(packed_inner[i][:, :], ins[f"packed_inner_{d}"]).then_inc(weights_in, 16)
                    sp.dma_start(w_dt[i][DT_ROW:DT_ROW + R, :], ins[f"W_dt_{d}"]).then_inc(weights_in, 16)
                    sp.dma_start(w_dt[i][DT_ROW + R:DT_ROW + R + 1, :], ins[f"b_dt_{d}"]).then_inc(weights_in, 16)
                sp.dma_start(g.cols[:, :], ins["gn_cols"]).then_inc(weights_in, 16)
                load_x(1, B, x_in)
                sp.dma_start(x1[:, (B - 1) * L:], ins["x"][B - 1]).then_inc(a.weights_in, 16)
                for w, name in ((a.wq, "Wq"), (a.wk, "Wk")):
                    for j in range(2):
                        sp.dma_start(w[:, j, :], ins[name]).then_inc(a.weights_in, 16)
                sp.dma_start(a.wv[:, :], ins["Wv"]).then_inc(a.weights_in, 16)
                for j, name in enumerate(("log_weights", "gumbel")):
                    sp.dma_start(e.logits[:, j, :], bass.AP(ins[name].tensor, 0, [[0, 128], [1, EXPERTS]])
                                 ).then_inc(e.logits_in, 16)
                sp.dma_start(e.sigma[:, :], bass.AP(ins["sigma"].tensor, 0, [[0, 128], [1, FILTERS]])
                             ).then_inc(e.logits_in, 16)

            @block.gpsimd
            def _(pool):
                zeros = [x_pair[C:, :, 0:1], x_pair[0:C, :, L:], ident[:, :], pick[:, :], g.stats[:, :]]
                for i, part in enumerate(zeros):
                    nc.gpsimd.memset(part, 0.0).then_inc(consts, 1)
                    pool.wait_ge(consts, i + 1)
                nc.gpsimd.memset(dt_low[DT_ROW:, :], 1.0).then_inc(consts, 1)
                pool.wait_ge(consts, 6)
                nc.gpsimd.memset(a.k_one[C:C + 2, :].bitcast(F32), 1.0).then_inc(consts, 1)
                pool.wait_ge(consts, 7)
                nc.gpsimd.memset(a.minus_half[:, :], -0.5).then_inc(consts, 1)
                nc.gpsimd.affine_select(out=ident[:, :], in_=ident[:, :], compare_op=ALU.not_equal, fill=1.0,
                                        base=0, pattern=[[-1, 128]], channel_multiplier=1).then_inc(consts, 1)
                for k in range(PARTS):
                    pool.wait_ge(consts, 9 + k)
                    nc.gpsimd.affine_select(out=pick[:, :], in_=pick[:, :], compare_op=ALU.not_equal, fill=1.0,
                                            base=-BC * k, pattern=[[-1, BC]], channel_multiplier=1).then_inc(consts, 1)
                for i, (part, value) in enumerate(((a.mask[:, :, :, :], 0.0), (a.mask_t[:, :, :, :], 0.0),
                                                   (a.v_one[:, :, C:C + 1], 1.0), (e.quarter[:, :], 0.25))):
                    nc.gpsimd.memset(part, value).then_inc(a.zeros, 1)
                pool.wait_ge(a.zeros, 4)
                for parity in range(2):
                    nc.gpsimd.affine_select(out=a.mask[:, parity, :, :], in_=a.mask[:, parity, :, :],
                                            compare_op=ALU.is_ge, fill=MASKED, base=parity,
                                            pattern=[[-1, 2], [-2, 128]], channel_multiplier=2).then_inc(a.consts, 1)
                    nc.gpsimd.affine_select(out=a.mask_t[:, parity, :, :], in_=a.mask_t[:, parity, :, :],
                                            compare_op=ALU.is_ge, fill=MASKED, base=-parity,
                                            pattern=[[1, 2], [2, 128]], channel_multiplier=-2).then_inc(a.consts, 1)
                pool.wait_ge(a.consts, 4)
                pool.wait_ge(e.logits_in, 16 * 3)
                nc.gpsimd.tensor_tensor(e.sigma4[:, :], e.sigma[:, :], e.quarter[:, :], ALU.pow).then_inc(e.softmax_ready, 1)

                def residual(b):
                    pool.wait_ge(g.act_ready, b + 1)
                    nc.gpsimd.tensor_tensor(x1[:, bass.ds(b * L, L)], mixed[:, :], x_flat[0:C, bass.ds(b * (L + 1), L)],
                                            ALU.add).then_inc(g.x1_ready, 1)

                def batch(b, first=False, last=False):
                    for i in range(2):
                        for s in range(N):
                            n, k = (2 * b + i) * N + s, i * N + s
                            pool.wait_ge(hidden_ready, n + 1)
                            pool.wait_ge(c_wide_ready, n + 1)
                            at_least(pool, prod_summed, n - PAIR + 1)
                            nc.gpsimd.tensor_tensor(prod[k % PAIR][:, :], hidden[k % DEEP][:, :],
                                                    c_wide[k % DEEP][:, :], ALU.mult).then_inc(prod_ready, 1)
                            if i == 1 and not first:
                                if s == 1:
                                    norm_rstd(nc, pool, g, a.minus_half, b - 1)
                                if s == 8:
                                    residual(b - 1)
                            if i == 1 and last and s == 5:
                                pool.wait_ge(ln_step, TOKEN_NORM)
                                nc.gpsimd.tensor_tensor(a.small[:, 2, :], a.small[:, 1, :], a.minus_half[:, :],
                                                        ALU.pow).then_inc(ln_rstd, 1)

                pool.wait_ge(first_in[0], FIRST[0])
                pool.wait_ge(x_in, X_LOADS)
                batch(0, first=True)
                with pool.Fori(1, B - 1) as b:
                    batch(b)
                batch(B - 1, last=True)

            @block.tensor
            def _(pe):
                def project(i, b, w, done, ps=ps_w):
                    for h, out in enumerate(halves(ps)):
                        mm = nc.tensor.matmul(out, w, x_flat[:, bass.ds(b * (L + 1) + i + h * H, H)], start=True, stop=True)
                    mm.then_inc(done, 1)

                def gate_in(u, i, b):
                    at_least(pe, g.mixed_ready, b - 1)
                    at_least(pe, relu_ready, u)
                    project(i, b, w_gate[i], z_ready)

                def conv_in(u, i, b):
                    pe.wait_ge(z_taken, u)
                    project(i, b, w_conv[i][:, :], xp_ready)

                def low_rank(u, i):
                    pe.wait_ge(xc_ready, u + 1)
                    for h, out in enumerate(halves(ps_w)):
                        mm = nc.tensor.matmul(out[0:DT_ROW + R, :], w_x[i], halves(xc[i])[h], start=True, stop=True)
                    mm.then_inc(xdb_ready, 1)

                def dt_in(u, i):
                    pe.wait_ge(dt_low_ready, u + 1)
                    pe.wait_ge(rest_ready, u + 1)
                    for h, out in enumerate(halves(ps_w)):
                        mm = nc.tensor.matmul(out, w_dt[i][DT_ROW:DT_ROW + R + 1, :],
                                              halves(dt_low)[h][DT_ROW:DT_ROW + R + 1, :], start=True, stop=True)
                    mm.then_inc(dt_psum_ready, 1)

                def wide_b(n, s, i):
                    at_least(pe, drive_ready, n)
                    for h, out in enumerate(halves(ps_b)):
                        mm = nc.tensor.matmul(out, spread[:, s, :], halves(bc_parts[i])[h], start=True, stop=True)
                    mm.then_inc(b_wide_ready, 1)

                def wide_c(n, s, i):
                    at_least(pe, c_wide_ready, n)
                    for h, out in enumerate(halves(ps_c)):
                        mm = nc.tensor.matmul(out, spread[:, N + s, :], halves(bc_parts[i])[h], start=True, stop=True)
                    mm.then_inc(c_psum_ready, 1)

                def sum_states(n, k, u):
                    s = k % N
                    if s == 0:
                        at_least(pe, y_taken, u)
                    pe.wait_ge(prod_ready, n + 1)
                    for h, out in enumerate(halves(ps_y)):
                        mm = nc.tensor.matmul(out, ident[:, :], halves(prod[k % PAIR])[h], start=(s == 0), stop=(s == N - 1))
                    mm.then_inc(prod_summed, 1)

                def out_product(b, at_relu):
                    pe.wait_ge(gated_ready, 2 * b + 2)
                    at_least(pe, relu_ready, at_relu)
                    for h, out in enumerate(halves(ps_w)):
                        for i in range(2):
                            mm = nc.tensor.matmul(out[0:C, :], w_out[i], halves(gated[i])[h],
                                                  start=(i == 0), stop=(i == 1))
                    mm.then_inc(out_ready, 1)

                def batch(b, first=False, last=False):
                    for i in range(2):
                        u = 2 * b + i
                        pe.wait_ge(parts_ready, u + 1)
                        for s in range(N):
                            n, k = u * N + s, i * N + s
                            wide_b(n, s, i)
                            if not (first and k < Y_LAG):
                                sum_states(n - Y_LAG, (k - Y_LAG) % (2 * N), u if s >= Y_LAG else u - 1)
                            wide_c(n, s, i)
                            if not (last and i == 1):
                                v, j, bv = u + 1, 1 - i, (b if i == 0 else b + 1)
                                if s == 2:
                                    if first and i == 0:
                                        pe.wait_ge(first_in[1], FIRST[1])
                                        pe.wait_ge(w_conv_ready, 2)
                                    if first and i == 1:
                                        pe.wait_ge(x_in, X_LOADS)
                                    gate_in(v, j, bv)
                                if s == 4:
                                    conv_in(v, j, bv)
                                if s == 7:
                                    low_rank(v, j)
                                if s == 11:
                                    dt_in(v, j)
                            elif s in first_attention:
                                first_attention[s]()
                            if i == 0 and s == 15 and not first:
                                out_product(b - 1, u + 2)

                def tokens():
                    pe.wait_ge(g.mixed_ready, B - 1)
                    for t in range(TILES):
                        delta, parity = divmod(t, 2)
                        mm = nc.tensor.transpose(ps_w[:, t * C:(t + 1) * C],
                                                 x1[:, SPAN * delta + parity:SPAN * (delta + 1):2], ident[0:C, 0:C])
                    mm.then_inc(tok_psum, 1)

                def normed():
                    pe.wait_ge(xn_ready, 1)
                    pe.wait_ge(tok_ready, 1)
                    for t in range(TILES):
                        mm = nc.tensor.transpose(ps_w[0:C, t * 128:(t + 1) * 128], xn[:, t, :], ident[:, :])
                    mm.then_inc(xnt_psum, 1)

                def queries_or_keys(w, done):
                    for h, out in enumerate(halves(ps_w)):
                        mm = nc.tensor.matmul(out, w[:, :, :].rearrange("d j e -> d (j e)"), xn_t[:, h * H:(h + 1) * H],
                                              start=True, stop=True)
                    mm.then_inc(done, 1)

                def queries():
                    pe.wait_ge(a.weights_in, ATTENTION_LOADS)
                    pe.wait_ge(xnt_ready, 1)
                    queries_or_keys(a.wq, q_psum)

                def keys():
                    pe.wait_ge(q_ready, 1)
                    queries_or_keys(a.wk, k_psum)

                def values():
                    pe.wait_ge(k_ready, 1)
                    for t in range(TILES):
                        mm = nc.tensor.matmul(ps_w[:, t * C:(t + 1) * C], xn_t[:, t * 128:(t + 1) * 128], a.wv[:, :],
                                              start=True, stop=True)
                    mm.then_inc(v_psum, 1)

                first_attention = {2: tokens, 8: normed, 11: queries, 14: keys}

                pe.wait_ge(consts, CONSTS)
                pe.wait_ge(first_in[0], FIRST[0])
                pe.wait_ge(w_conv_ready, 1)
                project(0, 0, w_conv[0][:, :], xp_ready)
                project(0, 0, w_gate[0], z_ready, ps=ps_y)
                pe.wait_ge(weights_in, WEIGHTS)
                low_rank(0, 0)
                dt_in(0, 0)
                pe.wait_ge(spread_ready, 1)
                pe.wait_ge(gate_ready, 1)
                batch(0, first=True)
                with pe.Fori(1, B - 1) as b:
                    batch(b)
                batch(B - 1, last=True)
                for k in range(2 * N - Y_LAG, 2 * N):
                    sum_states(2 * N * (B - 1) + k, k, 2 * B - 1)
                values()
                pe.wait_ge(v_ready, 1)
                out_product(B - 1, 2 * B)

            @block.scalar
            def _(act):
                def take_z(u, i):
                    act.wait_ge(z_ready, u + 1)
                    at_least(act, gate_ready, u)
                    nc.scalar.activation(z_raw[:, :], ps_w[:, :], ACT.Copy).then_inc(z_taken, 1)

                def silu_input(u, i):
                    act.wait_ge(xp_ready, u + 1)
                    at_least(act, y_taken, u - 1)
                    nc.scalar.activation(xc[i][:, :], ps_w[:, :], ACT.Silu, bias=cols[i][:, 0:1]).then_inc(xc_ready, 1)

                def silu_gate(u, i, norm=None):
                    act.wait_ge(z_taken, u)
                    at_least(act, gated_ready, u - 1)
                    nc.scalar.activation(gate[i][:, :], z_raw[:, :], ACT.Silu).then_inc(gate_ready, 1)
                    if norm is not None:
                        norm_silu(nc, act, g, norm)
                    nc.scalar.preload_act_table_set("natural_log_exp_and_others")

                def norm_take(b):
                    act.wait_ge(out_ready, b + 1)
                    at_least(act, g.x1_ready, b)
                    nc.scalar.activation(mixed[:, :], ps_w[0:C, :], ACT.Copy).then_inc(g.mixed_ready, 1)

                def split_high(u, i):
                    act.wait_ge(xdb_ready, u + 1)
                    at_least(act, c_psum_ready, N * (u - 1))
                    nc.scalar.activation(bc_parts[i][:, :], ps_w[0:DT_ROW, :], ACT.Copy).then_inc(high_ready, 1)
                    at_least(act, dt_psum_ready, u)
                    nc.scalar.activation(dt_low[DT_ROW:DT_ROW + R, :], ps_w[DT_ROW:DT_ROW + R, :],
                                         ACT.Copy).then_inc(dt_low_ready, 1)

                def softplus_exp(u, i):
                    act.wait_ge(dt_psum_ready, u + 1)
                    nc.scalar.activation(soft[:, :], ps_w[:, :], ACT.Abs).then_inc(abs_ready, 1)
                    act.wait_ge(abs_ready, u + 1)
                    nc.scalar.activation(soft[:, :], soft[:, :], ACT.Exp, scale=-1.0).then_inc(exp_ready, 1)

                def softplus_ln(u, i):
                    act.wait_ge(exp_ready, u + 2)
                    nc.scalar.activation(one_plus[:, :], soft[:, :], ACT.Identity, bias=1.0).then_inc(one_plus_ready, 1)
                    act.wait_ge(one_plus_ready, u + 1)
                    at_least(act, decay_ready, N * (u - 1))
                    at_least(act, dtx_ready, u - 1)
                    nc.scalar.activation(dt[i][:, :], one_plus[:, :], ACT.Ln).then_inc(ln_ready, 1)

                def decay_of(n, k, i, s):
                    at_least(act, hidden_ready, n - DEEP + 1)
                    nc.scalar.activation(decay[k % DEEP][:, :], dt[i][:, :], ACT.Exp,
                                         scale=a_neg[i][:, s:s + 1]).then_inc(decay_ready, 1)

                def take_c(n, k):
                    act.wait_ge(c_psum_ready, n + 1)
                    at_least(act, prod_ready, n - DEEP + 1)
                    nc.scalar.activation(c_wide[k % DEEP][:, :], ps_c[:, :], ACT.Copy).then_inc(c_wide_ready, 1)

                def batch(b, first=False, last=False):
                    for i in range(2):
                        u = 2 * b + i
                        act.wait_ge(dt_ready, u + 1)
                        for s in range(N):
                            for t in AHEAD[s]:
                                decay_of(u * N + t, i * N + t, i, t)
                            if s != 6:
                                take_c(u * N + s, i * N + s)
                            if s == 0 and i == 1 and not first:
                                norm_take(b - 1)
                            if last and i == 1:
                                if s == 3:
                                    act.wait_ge(tok_psum, 1)
                                    nc.scalar.activation(a.tok[:, :, :].rearrange("p i c -> p (i c)"), ps_w[:, 0:H],
                                                         ACT.Copy).then_inc(tok_ready, 1)
                                if s == 5:
                                    take_c(u * N + s + 1, i * N + s + 1)
                                    norm_silu(nc, act, g, b - 1)
                                    nc.scalar.preload_act_table_set("natural_log_exp_and_others")
                                if s == 9:
                                    act.wait_ge(xnt_psum, 1)
                                    nc.scalar.activation(xn_t, ps_w[0:C, :], ACT.Copy).then_inc(xnt_ready, 1)
                                if s == 12:
                                    act.wait_ge(q_psum, 1)
                                    nc.scalar.activation(a.q_parts[:, :], ps_w[:, :], ACT.Copy,
                                                         scale=float(C) ** -0.5).then_inc(q_high_ready, 1)
                                if s == 15:
                                    act.wait_ge(k_psum, 1)
                                    nc.scalar.activation(a.k_high[:, :], ps_w[:, :], ACT.Copy).then_inc(k_high_ready, 1)
                                continue
                            if first and i == 0 and s == 1:
                                act.wait_ge(e.w_step, 2)
                                nc.scalar.activation(e.w[:, 2, :], e.w[:, 0, :], ACT.Exp,
                                                     bias=e.w[:, 1, 0:1]).then_inc(e.softmax_ready, 1)
                            if s == 3:
                                take_z(u + 1, 1 - i)
                            if s == 5:
                                silu_input(u + 1, 1 - i)
                                take_c(u * N + s + 1, i * N + s + 1)
                                silu_gate(u + 1, 1 - i, norm=(b - 1 if i == 1 and not first else None))
                            if s == 8:
                                split_high(u + 1, 1 - i)
                            if s == 11:
                                softplus_exp(u + 1, 1 - i)
                            if s == 12:
                                softplus_ln(u + 1, 1 - i)

                act.wait_ge(weights_in, WEIGHTS)
                silu_input(0, 0)
                act.wait_ge(z_ready, 1)
                nc.scalar.activation(gate[0][:, :], ps_y[:, :], ACT.Silu).then_inc(gate_ready, 1)
                nc.scalar.preload_act_table_set("natural_log_exp_and_others")
                split_high(0, 0)
                act.wait_ge(a_log_ready, 2)
                for i in range(2):
                    last = nc.scalar.activation(a_neg[i][:, :], a_log[i], ACT.Exp)
                last.then_inc(exp_ready, 1)
                softplus_exp(0, 0)
                softplus_ln(0, 0)
                act.wait_ge(consts, CONSTS)
                nc.scalar.activation(a.ident_r[:, :], ident[:, :], ACT.Copy).then_inc(a.idents, 1)
                nc.scalar.activation(a.ident_bf[:, :], ident[:, :], ACT.Copy).then_inc(a.idents, 1)
                act.wait_ge(a_ready, 2)
                batch(0, first=True)
                with act.Fori(1, B - 1) as b:
                    batch(b)
                batch(B - 1, last=True)
                norm_take(B - 1)

            @block.vector
            def _(dve):
                def split_low(u, i):
                    dve.wait_ge(high_ready, u + 1)
                    dve.wait_ge(dt_low_ready, u + 1)
                    at_least(dve, gated_ready, u - 1)
                    nc.vector.tensor_tensor(scratch[0:2 * BC, :], ps_w[0:2 * BC, :], bc_parts[i][0:2 * BC, :],
                                            ALU.subtract).then_inc(rest_ready, 1)

                def split_mid(u, i):
                    dve.wait_ge(rest_ready, u + 1)
                    nc.vector.tensor_copy(bc_parts[i][0:2 * BC, :], scratch[0:2 * BC, :]).then_inc(mid_ready, 1)

                def split_last(u, i):
                    dve.wait_ge(mid_ready, u + 1)
                    nc.vector.tensor_tensor(bc_parts[i][0:BC, :], scratch[0:BC, :], bc_parts[i][0:BC, :],
                                            ALU.subtract).then_inc(parts_ready, 1)

                def lost(u, i):
                    dve.wait_ge(one_plus_ready, u + 1)
                    dve.wait_ge(parts_ready, u + 1)
                    nc.vector.scalar_tensor_tensor(out=scratch[:, :], in0=one_plus[:, :], scalar=-1.0, in1=soft[:, :],
                                                   op0=ALU.add, op1=ALU.subtract).then_inc(lost_ready, 1)

                def relu(u, i):
                    dve.wait_ge(lost_ready, u + 1)
                    nc.vector.scalar_tensor_tensor(out=scratch[:, :], in0=ps_w[:, :], scalar=0.0, in1=scratch[:, :],
                                                   op0=ALU.max, op1=ALU.subtract).then_inc(relu_ready, 1)

                def dt_sum(u, i):
                    dve.wait_ge(ln_ready, u + 1)
                    dve.wait_ge(relu_ready, u + 1)
                    nc.vector.tensor_tensor(dt[i][:, :], scratch[:, :], dt[i][:, :], ALU.add).then_inc(dt_ready, 1)

                def dt_x(u, i):
                    dve.wait_ge(dt_ready, u + 1)
                    at_least(dve, drive_ready, N * (u - 1))
                    nc.vector.tensor_tensor(dtx[i][:, :], dt[i][:, :], xc[i][:, :], ALU.mult).then_inc(dtx_ready, 1)

                def take_y(u, i, last=False):
                    dve.wait_ge(prod_summed, N * (u + 1))
                    if not last:
                        dve.wait_ge(dt_ready, u + 2)
                    nc.vector.scalar_tensor_tensor(out=scratch[:, :], in0=xc[i][:, :], scalar=cols[i][:, 1:2],
                                                   in1=ps_y[:, :], op0=ALU.mult, op1=ALU.add).then_inc(y_taken, 1)

                def drive_step(n, k, i):
                    dve.wait_ge(b_wide_ready, n + 1)
                    at_least(dve, hidden_ready, n - PAIR + 1)
                    nc.vector.tensor_tensor(drive[k % PAIR][:, :], dtx[i][:, :], ps_b[:, :], ALU.mult).then_inc(drive_ready, 1)

                def scan_step(n, k):
                    dve.wait_ge(decay_ready, n + 1)
                    dve.wait_ge(drive_ready, n + 1)
                    at_least(dve, prod_ready, n - DEEP + 1)
                    order = slice(None) if k < N else slice(None, None, -1)
                    nc.vector.tensor_tensor_scan(hidden[k % DEEP][:, order], decay[k % DEEP][:, order],
                                                 drive[k % PAIR][:, order], 0.0, ALU.mult,
                                                 ALU.add).then_inc(hidden_ready, 1)

                def center_x():
                    dve.wait_ge(tok_ready, 1)
                    center_tokens(nc, dve, ln_step, 0, a.tok, cen, sq, a.small)

                def norm_x():
                    dve.wait_ge(ln_rstd, 1)
                    nc.vector.tensor_tensor(xn, cen, a.small[:, 2, :].unsqueeze(2).to_broadcast([128, TILES, C]),
                                            ALU.mult).then_inc(xn_ready, 1)

                def split_q():
                    dve.wait_ge(q_high_ready, 1)
                    nc.vector.scalar_tensor_tensor(out=a.q_parts[C:, :], in0=ps_w[C:, :], scalar=float(C) ** -0.5,
                                                   in1=a.q_parts[C:, :].bitcast(F32), op0=ALU.mult,
                                                   op1=ALU.subtract).then_inc(q_ready, 1)
                    nc.vector.tensor_copy(a.q_row[0:C, :], a.q_parts[0:C, :].bitcast(F32)).then_inc(q_ready, 1)

                def split_k():
                    dve.wait_ge(k_high_ready, 1)
                    nc.vector.tensor_tensor(a.k_one[0:C, :], ps_w[0:C, :], a.k_high[0:C, :].bitcast(F32),
                                            ALU.subtract).then_inc(k_ready, 1)

                def take_values():
                    dve.wait_ge(v_psum, 1)
                    nc.vector.tensor_copy(a.v_one[:, :, 0:C], ps_w[:, 0:H].rearrange("p (i c) -> p i c", i=TILES)
                                          ).then_inc(v_ready, 1)

                first_attention = {4: center_x, 6: norm_x, 13: split_q}

                def batch(b, first=False, last=False):
                    for i in range(2):
                        u = 2 * b + i
                        dve.wait_ge(dtx_ready, u + 1)
                        for s in range(N):
                            n, k = u * N + s, i * N + s
                            drive_step(n, k, i)
                            if not (first and k == 0):
                                scan_step(n - 1, (k - 1) % (2 * N))
                            if not (first and i == 0):
                                if s == 2:
                                    take_y(u - 1, 1 - i)
                                if s == 3:
                                    gate_of(u - 1, 1 - i, b)
                            if i == 1 and not first:
                                if s == 1:
                                    norm_stats(nc, dve, g, b - 1)
                                if s == 3:
                                    norm_scale(nc, dve, g, b - 1)
                            if first and i == 0 and s in (0, 3):
                                (expert_logits if s == 0 else expert_weights)(nc, dve, e)
                            if last and i == 1:
                                if s in first_attention:
                                    first_attention[s]()
                                continue
                            for at, step in ((9, split_low), (10, split_mid), (10, split_last),
                                             (13, lost), (14, relu), (14, dt_sum), (15, dt_x)):
                                if s == at:
                                    step(u + 1, 1 - i)

                def gate_of(u, i, b):
                    dve.wait_ge(y_taken, u + 1)
                    at_least(dve, out_ready, b if i == 0 else b - 1)
                    nc.vector.tensor_tensor(gated[i][:, :], scratch[:, :], gate[i][:, :], ALU.mult).then_inc(gated_ready, 1)

                dve.wait_ge(first_in[0], FIRST[0])
                nc.vector.tensor_tensor(w_conv[0][:, :], w_in[0], taps[0], ALU.mult).then_inc(w_conv_ready, 1)
                dve.wait_ge(consts, CONSTS)
                nc.vector.tensor_copy(spread[:, :, :], pick[:, :].unsqueeze(2).to_broadcast([DT_ROW, BC, 128])
                                      ).then_inc(spread_ready, 1)
                dve.wait_ge(weights_in, WEIGHTS)
                for i in range(2):
                    nc.vector.tensor_scalar(a_log[i], a_log[i], A_LOG_MAX, None, ALU.min).then_inc(a_log_ready, 1)
                dve.wait_ge(first_in[1], FIRST[1])
                nc.vector.tensor_tensor(w_conv[1][:, :], w_in[1], taps[1], ALU.mult).then_inc(w_conv_ready, 1)
                for step in (split_low, split_mid, split_last):
                    step(0, 0)
                dve.wait_ge(exp_ready, 1)
                for i in range(2):
                    nc.vector.tensor_scalar(a_neg[i][:, :], a_neg[i][:, :], -1.0, None, ALU.mult).then_inc(a_ready, 1)
                for step in (lost, relu, dt_sum, dt_x):
                    step(0, 0)
                batch(0, first=True)
                with dve.Fori(1, B - 1) as b:
                    batch(b)
                batch(B - 1, last=True)
                u = 2 * B - 1
                scan_step(N * (u + 1) - 1, 2 * N - 1)
                split_k()
                take_values()
                take_y(u, 1, last=True)
                gate_of(u, 1, B)


def attention_stage(nc, ins, a, g, e, x1, x2, u_all, u_high, u_low):
    with ExitStack() as ctx:
        def sb(name, shape, dt=F32):
            return ctx.enter_context(nc.sbuf_tensor(name, shape, dt))

        def sem(name):
            return ctx.enter_context(nc.semaphore(name))

        ident, tok, small = a.ident, a.tok, a.small
        q_parts, k_high, q_row, k_one, v_one = a.q_parts, a.k_high, a.q_row, a.k_one, a.v_one
        xs = sb("xs", [C, L])
        tok_res = sb("tok_res", [128, TILES, C])
        cen = sb("cen", [128, TILES, C])
        cen2 = sb("cen2", [128, TILES, C])
        sq = sb("sq", [128, TILES, C])
        xn = sb("xn", [128, TILES, C])
        un = sb("un", [128, TILES, C])
        small2 = sb("small2", [128, 3, TILES])
        xn_t = sb("xn_t", [C, L])
        probs = [sb(f"probs_{i}", [128, 2 * SPAN]) for i in range(2)]
        max_parts = sb("max_parts", [128, TILES, 2])
        lowest = sb("lowest", [128, TILES])
        neg_max = sb("neg_max", [128, TILES, C + 2], F32R)
        o_t = sb("o_t", [C + 1, SPAN])
        inv = sb("inv", [128, 2, 1])
        tok2 = sb("tok2", [128, TILES, C])

        ps_s = ctx.enter_context(nc.psum_tensor("ps_s", [128, 4, H], F32))
        ps_t = [ctx.enter_context(nc.psum_tensor(f"ps_t{i}", [128, H], F32)) for i in range(2)]
        ps_o = ctx.enter_context(nc.psum_tensor("ps_o", [128, H], F32))
        ps_m = ctx.enter_context(nc.psum_tensor("ps_m", [128, H], F32))
        TURN = 3
        NEXT = 3

        names = """xs_ready tok_psum tok_ready ln_step ln_rstd xn_ready xnt_psum xnt_ready q_psum q_high_ready
            q_ready k_psum k_high_ready k_ready v_psum v_ready scores_ready part_ready lowest_ready
            max_high_ready max_ready row_psum row_ready st_ready probs_ready pv_done ot_ready back_psum
            inv_ready back_done tok_res_ready ln2_step ln2_rstd u_ready u_high_ready u_low_ready x2_ready
            u_all_ready zeroed passed"""
        (xs_ready, tok_psum, tok_ready, ln_step, ln_rstd, xn_ready, xnt_psum, xnt_ready, q_psum,
         q_high_ready, q_ready, k_psum, k_high_ready, k_ready, v_psum, v_ready, scores_ready, part_ready,
         lowest_ready, max_high_ready, max_ready, row_psum, row_ready, st_ready, probs_ready, pv_done,
         ot_ready, back_psum, inv_ready, back_done, tok_res_ready, ln2_step, ln2_rstd, u_ready, u_high_ready,
         u_low_ready, x2_ready, u_all_ready, zeroed, passed,
         ) = [sem(name) for name in names.split()]

        def width(i):
            return (i // 2 + 1) * SPAN

        pieces = [(i, at, min(H, width(i) - at)) for i in range(TILES) for at in range(0, width(i), H)]
        blocks = [(d, g) for d in range(SPANS) for g in range(d + 1)]
        PIECES, BLOCKS_T = len(pieces), len(blocks)

        EARLY = TILES - 2

        def halves(t):
            return [t[:, h * H:(h + 1) * H] for h in range(L // H)]

        def all_batches(engine, batch):
            batch(0, first=True)
            with engine.Fori(1, B - 1) as b:
                batch(b)
            batch(B - 1, last=True)

        with nc.Block() as block:

            @block.sync
            def _(sp):
                load_expert_weights(sp, ins, e)

            @block.gpsimd
            def _(pool):
                def rstd(b):
                    pool.wait_ge(ln_step, TOKEN_NORM * b)
                    nc.gpsimd.tensor_tensor(small[:, 2, :], small[:, 1, :], a.minus_half[:, :], ALU.pow).then_inc(ln_rstd, 1)

                def rstd2(n, lo=0, hi=TILES):
                    pool.wait_ge(ln2_step, TOKEN_NORM * (n + 1))
                    nc.gpsimd.tensor_tensor(small2[:, 2, lo:hi], small2[:, 1, lo:hi], a.minus_half[:, lo:hi],
                                            ALU.pow).then_inc(ln2_rstd, 1)

                nc.gpsimd.memset(neg_max[:, :, 0:C].bitcast(F32), 0.0).then_inc(zeroed, 1)
                nc.gpsimd.memset(e.rows.bitcast(F32), 0.0).then_inc(e.rows_step, 1)
                norm_rstd(nc, pool, g, a.minus_half, B - 1)
                rstd(1)
                clear_blocks(nc, pool, e)
                pool.wait_ge(g.act_ready, B)
                nc.gpsimd.tensor_tensor(x1[:, (B - 1) * L:], g.mixed[:, :], x1[:, (B - 1) * L:], ALU.add).then_inc(g.x1_ready, 1)
                rstd2(0)
                rstd(2)
                weigh_and_sum(nc, pool, e)
                rstd2(1)
                rstd(3)
                lag_matrices(nc, pool, e)
                tap_blocks(nc, pool, e)
                pool.wait_ge(e.ar_ready, 2)
                rstd2(2)
                rstd2(3, 0, EARLY)
                rstd2(4, EARLY, TILES)

            @block.tensor
            def _(pe):
                def tokens(b):
                    pe.wait_ge(xs_ready, b)
                    at_least(pe, v_ready, b - 1)
                    pe.sem_inc(passed, 1)
                    for i in range(TILES):
                        delta, parity = divmod(i, 2)
                        rows = xs[:, SPAN * delta + parity:SPAN * (delta + 1):2]
                        mm = nc.tensor.transpose(ps_s[:, NEXT, i * C:(i + 1) * C], rows, ident[0:C, 0:C])
                    mm.then_inc(tok_psum, 1)

                def normed(b, h):
                    pe.wait_ge(xn_ready, b)
                    pe.wait_ge(tok_ready, b)
                    at_least(pe, xnt_ready, 2 * (b - 1) + h)
                    pe.sem_inc(passed, 1)
                    for i in range(TILES // 2):
                        mm = nc.tensor.transpose(ps_s[0:C, NEXT, i * 128:(i + 1) * 128], xn[:, h * TILES // 2 + i, :], ident[:, :])
                    mm.then_inc(xnt_psum, 1)

                def project(b):
                    pe.wait_ge(xnt_ready, 2 * b)
                    at_least(pe, part_ready, PIECES * b)
                    for first, w, done in ((0, a.wq, q_psum), (2, a.wk, k_psum)):
                        for h in range(2):
                            mm = nc.tensor.matmul(ps_s[:, first + h, :], w[:, :, :].rearrange("d j e -> d (j e)"),
                                                  halves(xn_t)[h], start=True, stop=True)
                        mm.then_inc(done, 1)

                def values(b):
                    pe.wait_ge(k_ready, b)
                    for i in range(TILES):
                        mm = nc.tensor.matmul(ps_s[:, NEXT, i * C:(i + 1) * C], xn_t[:, i * 128:(i + 1) * 128], a.wv[:, :],
                                              start=True, stop=True)
                    mm.then_inc(v_psum, 1)

                def scores(b, d):
                    if d == 0:
                        at_least(pe, q_ready, 2 * b)
                        at_least(pe, k_ready, b)
                    for c, (i, at, n) in enumerate(pieces):
                        if i // 2 != d:
                            continue
                        at_least(pe, part_ready, PIECES * b + c - TURN + 1)
                        out = ps_s[:, c % TURN, :]
                        queries = slice(i * 128, (i + 1) * 128)
                        last = at + n == width(i)
                        nc.tensor.matmul(out[:, 0:n], q_parts[:, queries], k_high[:, at:at + n], start=True, stop=False)
                        mm = nc.tensor.matmul(out[:, 0:n], q_row[0:C, queries], k_one[0:C, at:at + n], start=False, stop=not last)
                        if last:
                            mm = nc.tensor.matmul(out[:, n - SPAN:n], a.ident_bf[:, :],
                                                  a.mask[:, i % 2, :, :].rearrange("p a b -> p (a b)"), start=False, stop=True)
                        mm.then_inc(scores_ready, 1)

                def maxima(b, d, back):
                    pe.wait_ge(max_ready, SPANS * b + d + 1)
                    at_least(pe, back_done, SPANS * b + back)
                    at_least(pe, row_ready, SPANS * b + d)
                    for j in range(2):
                        mm = nc.tensor.matmul(ps_m[0:C + 2, SPAN + j * 128:SPAN + (j + 1) * 128],
                                              neg_max[:, 2 * d + j, :], a.ident_r[:, :], start=True, stop=True)
                    mm.then_inc(row_psum, 1)

                def scores_t(b, d, g):
                    n = blocks.index((d, g))
                    if g == 0:
                        pe.wait_ge(row_ready, SPANS * b + d + 1)
                    at_least(pe, probs_ready, BLOCKS_T * b + n - 1)
                    queries = slice(SPAN * d, SPAN * (d + 1))
                    for j in range(2):
                        keys = slice(SPAN * g + 128 * j, SPAN * g + 128 * (j + 1))
                        out = ps_t[n % 2][:, SPAN * j:SPAN * (j + 1)]
                        nc.tensor.matmul(out, k_high[:, keys], q_parts[:, queries], start=True, stop=False)
                        mm = nc.tensor.matmul(out, k_one[0:C + 2, keys], q_row[0:C + 2, queries], start=False, stop=d != g)
                        if d == g:
                            mm = nc.tensor.matmul(out, a.ident_bf[:, :], a.mask_t[:, j, :, :].rearrange("p a b -> p (a b)"),
                                                  start=False, stop=True)
                    mm.then_inc(st_ready, 1)

                def attend(b, d, g):
                    n = blocks.index((d, g))
                    pe.wait_ge(probs_ready, BLOCKS_T * b + n + 1)
                    if g == 0:
                        at_least(pe, ot_ready, SPANS * b + d)
                        if d == 0:
                            at_least(pe, v_ready, b)
                    for j in range(2):
                        mm = nc.tensor.matmul(ps_o[0:C + 1, 0:SPAN], v_one[:, 2 * g + j, :],
                                              probs[n % 2][:, SPAN * j:SPAN * (j + 1)],
                                              start=(g == 0 and j == 0), stop=(g == d and j == 1))
                    mm.then_inc(pv_done, 1)

                def turn_back(b, d, rows):
                    pe.wait_ge(ot_ready, SPANS * b + d + 1)
                    pe.wait_ge(row_ready, SPANS * b + rows)
                    at_least(pe, back_done, SPANS * b + d)
                    pe.sem_inc(passed, 1)
                    for j in range(2):
                        mm = nc.tensor.transpose(ps_m[:, j * (C + 1):(j + 1) * (C + 1)], o_t[:, j * 128:(j + 1) * 128],
                                                 ident[0:C + 1, 0:C + 1])
                    mm.then_inc(back_psum, 1)

                def batch(b, first=False, last=False):
                    scores(b, 0)
                    scores(b, 1)
                    maxima(b, 0, back=0)
                    if not last:
                        tokens(b + 1)
                    scores_t(b, 0, 0)
                    scores(b, 2)
                    maxima(b, 1, back=0)
                    attend(b, 0, 0)
                    scores_t(b, 1, 0)
                    scores(b, 3)
                    maxima(b, 2, back=0)
                    scores_t(b, 1, 1)
                    attend(b, 1, 0)
                    turn_back(b, 0, rows=3)
                    attend(b, 1, 1)
                    scores_t(b, 2, 0)
                    maxima(b, 3, back=1)
                    scores_t(b, 2, 1)
                    attend(b, 2, 0)
                    scores_t(b, 2, 2)
                    attend(b, 2, 1)
                    turn_back(b, 1, rows=4)
                    attend(b, 2, 2)
                    scores_t(b, 3, 0)
                    if not last:
                        normed(b + 1, 0)
                    scores_t(b, 3, 1)
                    attend(b, 3, 0)
                    turn_back(b, 2, rows=4)
                    scores_t(b, 3, 2)
                    attend(b, 3, 1)
                    if not last:
                        normed(b + 1, 1)
                    scores_t(b, 3, 3)
                    attend(b, 3, 2)
                    if not last:
                        project(b + 1)
                    attend(b, 3, 3)
                    turn_back(b, 3, rows=4)
                    if not last:
                        values(b + 1)

                pe.wait_ge(a.consts, 4)
                pe.wait_ge(a.idents, 2)
                pe.wait_ge(zeroed, 1)
                all_batches(pe, batch)

            @block.scalar
            def _(act):
                def take_x(b):
                    at_least(act, tok_psum, b - 1)
                    if not isinstance(b, int):
                        act.wait_ge(g.x1_ready, B)
                    nc.scalar.activation(xs[:, :], x1[:, bass.ds(b * L, L)], ACT.Copy).then_inc(xs_ready, 1)

                def take_tokens(b):
                    act.wait_ge(tok_psum, b)
                    at_least(act, tok_res_ready, b)
                    nc.scalar.activation(tok[:, :, :].rearrange("p i c -> p (i c)"), ps_s[:, NEXT, :],
                                         ACT.Copy).then_inc(tok_ready, 1)

                def take_normed(b, h):
                    act.wait_ge(xnt_psum, 2 * (b - 1) + h + 1)
                    at_least(act, v_psum, b - 1)
                    nc.scalar.activation(halves(xn_t)[h], ps_s[0:C, NEXT, :], ACT.Copy).then_inc(xnt_ready, 1)

                def take_qk(b):
                    at_least(act, st_ready, BLOCKS_T * b)
                    act.wait_ge(q_psum, b)
                    nc.scalar.activation(q_parts[:, :].rearrange("p (h n) -> p h n", h=2), ps_s[:, 0:2, :],
                                         ACT.Copy, scale=float(C) ** -0.5).then_inc(q_high_ready, 1)
                    act.wait_ge(k_psum, b)
                    nc.scalar.activation(k_high[:, :].rearrange("p (h n) -> p h n", h=2), ps_s[:, 2:4, :],
                                         ACT.Copy).then_inc(k_high_ready, 1)

                def row(b, d):
                    act.wait_ge(row_psum, SPANS * b + d + 1)
                    nc.scalar.activation(q_row[C:C + 2, SPAN * d:SPAN * (d + 1)], ps_m[C:C + 2, SPAN:2 * SPAN],
                                         ACT.Copy).then_inc(row_ready, 1)

                def exp(b, d, g):
                    n = blocks.index((d, g))
                    act.wait_ge(st_ready, BLOCKS_T * b + n + 1)
                    at_least(act, pv_done, BLOCKS_T * b + n - 1)
                    nc.scalar.activation(probs[n % 2][:, :], ps_t[n % 2][:, :], ACT.Exp).then_inc(probs_ready, 1)

                def take_output(b, d):
                    act.wait_ge(pv_done, BLOCKS_T * b + blocks.index((d, d)) + 1)
                    at_least(act, back_psum, SPANS * b + d)
                    nc.scalar.activation(o_t[:, :], ps_o[0:C + 1, 0:SPAN], ACT.Copy).then_inc(ot_ready, 1)

                def keep_x2(b, lo=0, hi=TILES):
                    act.wait_ge(back_done, SPANS * b + hi // 2)
                    nc.scalar.activation(x2[:, lo:hi, bass.ds(b, 1), :].rearrange("p i o c -> p i (o c)"), tok2[:, lo:hi, :],
                                         ACT.Copy).then_inc(x2_ready, 1)

                def keep_u(b, n=None, lo=0, hi=TILES):
                    act.wait_ge(u_ready, (b if n is None else n) + 1)
                    nc.scalar.activation(u_all[:, lo:hi, bass.ds(b, 1), :].rearrange("p i o c -> p i (o c)"), un[:, lo:hi, :],
                                         ACT.Copy).then_inc(u_all_ready, 1)

                def batch(b, first=False, last=False):
                    if not last:
                        take_x(b + 1)
                    row(b, 0)
                    if not first:
                        keep_x2(b - 1)
                    at_least(act, tok_ready, b)
                    nc.scalar.activation(tok_res[:, :, :], tok[:, :, :], ACT.Copy).then_inc(tok_res_ready, 1)
                    if not last:
                        take_tokens(b + 1)
                    exp(b, 0, 0)
                    row(b, 1)
                    take_output(b, 0)
                    exp(b, 1, 0)
                    row(b, 2)
                    exp(b, 1, 1)
                    take_output(b, 1)
                    exp(b, 2, 0)
                    row(b, 3)
                    exp(b, 2, 1)
                    exp(b, 2, 2)
                    take_output(b, 2)
                    exp(b, 3, 0)
                    if not last:
                        take_normed(b + 1, 0)
                    exp(b, 3, 1)
                    if not first:
                        keep_u(b - 1)
                    exp(b, 3, 2)
                    if not last:
                        take_normed(b + 1, 1)
                    exp(b, 3, 3)
                    if not last:
                        take_qk(b + 1)
                    take_output(b, 3)

                batch(0, first=True)
                norm_silu(nc, act, g, B - 1)
                nc.scalar.preload_act_table_set("natural_log_exp_and_others")
                with act.Fori(1, B - 1) as b:
                    batch(b)
                batch(B - 1, last=True)
                keep_x2(B - 1, 0, EARLY)
                keep_u(B - 1, 3, 0, EARLY)
                keep_x2(B - 1, EARLY, TILES)
                keep_u(B - 1, 4, EARLY, TILES)

            @block.vector
            def _(dve):
                wide = [128, TILES, C]

                def center_x(b):
                    dve.wait_ge(tok_ready, b)
                    center_tokens(nc, dve, ln_step, TOKEN_NORM * (b - 1), tok, cen, sq, small)

                def norm_x(b):
                    dve.wait_ge(ln_rstd, b)
                    at_least(dve, xnt_psum, 2 * (b - 1))
                    nc.vector.tensor_tensor(xn[:, :, :], cen[:, :, :], small[:, 2, :].unsqueeze(2).to_broadcast(wide),
                                            ALU.mult).then_inc(xn_ready, 1)

                def center_x2(b, n=None, lo=0, hi=TILES):
                    dve.wait_ge(back_done, SPANS * b + hi // 2)
                    center_tokens(nc, dve, ln2_step, TOKEN_NORM * (b if n is None else n), tok2, cen2, sq, small2, lo, hi)

                def norm_x2(b, n=None, lo=0, hi=TILES):
                    n = b if n is None else n
                    dve.wait_ge(ln2_rstd, n + 1)
                    at_least(dve, u_all_ready, b)
                    nc.vector.tensor_tensor(un[:, lo:hi, :], cen2[:, lo:hi, :],
                                            small2[:, 2, lo:hi].unsqueeze(2).to_broadcast([128, hi - lo, C]),
                                            ALU.mult).then_inc(u_ready, 1)
                    dve.wait_ge(u_ready, n + 1)
                    high = u_high[:, lo:hi, bass.ds(b, 1), :].rearrange("p i o c -> p i (o c)")
                    nc.vector.tensor_copy(high, un[:, lo:hi, :]).then_inc(u_high_ready, 1)
                    dve.wait_ge(u_high_ready, n + 1)
                    nc.vector.tensor_tensor(u_low[:, lo:hi, bass.ds(b, 1), :].rearrange("p i o c -> p i (o c)"), un[:, lo:hi, :],
                                            high.bitcast(F32), ALU.subtract).then_inc(u_low_ready, 1)

                def split_qk(b):
                    dve.wait_ge(q_high_ready, b)
                    nc.vector.scalar_tensor_tensor(out=q_parts[C:, :].rearrange("p (h n) -> p h n", h=2),
                                                   in0=ps_s[C:, 0:2, :], scalar=float(C) ** -0.5,
                                                   in1=q_parts[C:, :].bitcast(F32).rearrange("p (h n) -> p h n", h=2),
                                                   op0=ALU.mult, op1=ALU.subtract).then_inc(q_ready, 1)
                    nc.vector.tensor_copy(q_row[0:C, :], q_parts[0:C, :].bitcast(F32)).then_inc(q_ready, 1)
                    dve.wait_ge(k_high_ready, b)
                    nc.vector.tensor_tensor(k_one[0:C, :].rearrange("p (h n) -> p h n", h=2), ps_s[0:C, 2:4, :],
                                            k_high[0:C, :].bitcast(F32).rearrange("p (h n) -> p h n", h=2),
                                            ALU.subtract).then_inc(k_ready, 1)

                def take_values(b):
                    dve.wait_ge(v_psum, b)
                    at_least(dve, pv_done, BLOCKS_T * b)
                    nc.vector.tensor_copy(v_one[:, :, 0:C], ps_s[:, NEXT, :].rearrange("p (i c) -> p i c", i=TILES)
                                          ).then_inc(v_ready, 1)

                def maximum(b, d):
                    at_least(dve, row_psum, SPANS * (b - 1) + d + 1)
                    tiles = slice(2 * d, 2 * d + 2)
                    for c, (i, at, n) in enumerate(pieces):
                        if i // 2 != d:
                            continue
                        dve.wait_ge(scores_ready, PIECES * b + c + 1)
                        nc.vector.tensor_reduce(max_parts[:, i, at // H:at // H + 1], ps_s[:, c % TURN, 0:n], AX.X,
                                                ALU.max, negate=True).then_inc(part_ready, 1)
                        count = PIECES * b + c + 1
                    dve.wait_ge(part_ready, count)
                    if width(2 * d) <= H:
                        low = max_parts[:, tiles, 0]
                    else:
                        low = lowest[:, tiles]
                        nc.vector.tensor_tensor(low, max_parts[:, tiles, 0], max_parts[:, tiles, 1],
                                                ALU.min).then_inc(lowest_ready, 1)
                        dve.wait_ge(lowest_ready, 2 * b + d - 1)
                    nc.vector.tensor_copy(neg_max[:, tiles, C], low).then_inc(max_high_ready, 1)
                    dve.wait_ge(max_high_ready, SPANS * b + d + 1)
                    nc.vector.tensor_tensor(neg_max[:, tiles, C + 1], low, neg_max[:, tiles, C].bitcast(F32),
                                            ALU.subtract).then_inc(max_ready, 1)

                def output(b, d):
                    dve.wait_ge(back_psum, SPANS * b + d + 1)
                    if d == 0:
                        dve.wait_ge(tok_res_ready, b + 1)
                        at_least(dve, x2_ready, b)
                    got = ps_m[:, 0:2 * (C + 1)].rearrange("p (j c) -> p j c", j=2)
                    nc.vector.reciprocal(inv[:, :, :], got[:, :, C:C + 1]).then_inc(inv_ready, 1)
                    dve.wait_ge(inv_ready, SPANS * b + d + 1)
                    for j in range(2):
                        last = nc.vector.scalar_tensor_tensor(out=tok2[:, 2 * d + j, :], in0=got[:, j, 0:C],
                                                              scalar=inv[:, j, :], in1=tok_res[:, 2 * d + j, :],
                                                              op0=ALU.mult, op1=ALU.add)
                    last.then_inc(back_done, 1)

                def batch(b, first=False, last=False):
                    maximum(b, 0)
                    if not first:
                        center_x2(b - 1)
                    maximum(b, 1)
                    maximum(b, 2)
                    maximum(b, 3)
                    output(b, 0)
                    if first:
                        norm_stats(nc, dve, g, B - 1)
                    if not last:
                        center_x(b + 1)
                    if first:
                        norm_scale(nc, dve, g, B - 1)
                    else:
                        norm_x2(b - 1)
                    if not last:
                        norm_x(b + 1)
                    output(b, 1)
                    output(b, 2)
                    if last:
                        center_x2(b, 3, 0, EARLY)
                    else:
                        split_qk(b + 1)
                    output(b, 3)
                    if not last:
                        take_values(b + 1)

                batch(0, first=True)
                filter_rows(nc, dve, e)
                with dve.Fori(1, B - 1) as b:
                    batch(b)
                batch(B - 1, last=True)
                norm_x2(B - 1, 3, 0, EARLY)
                center_x2(B - 1, 4, EARLY, TILES)
                norm_x2(B - 1, 4, EARLY, TILES)


def weight_tensors(nc, ctx):
    def sb(name, shape, dt=F32):
        return ctx.enter_context(nc.sbuf_tensor(name, shape, dt))

    e = Shared()
    e.logits = sb("logits", [128, 2, EXPERTS])
    e.sigma = sb("sigma", [128, FILTERS])
    e.quarter = sb("quarter", [128, FILTERS])
    e.sigma4 = sb("sigma4", [128, FILTERS])
    e.w = sb("w", [128, 8, EXPERTS])
    e.wk = sb("w_sigma", [128, EXPERTS, FILTERS])
    names = """logits_in weights_in w_step softmax_ready wk_ready sum_step rows_step rows_ready filters_out
        zeros_ready ar_step ar_ready block_step block_ready passed"""
    (e.logits_in, e.weights_in, e.w_step, e.softmax_ready, e.wk_ready, e.sum_step, e.rows_step, e.rows_ready,
     e.filters_out, e.zeros_ready, e.ar_step, e.ar_ready, e.block_step, e.block_ready, e.passed,
     ) = [ctx.enter_context(nc.semaphore(f"expert_{name}")) for name in names.split()]
    e.hankel_in = [ctx.enter_context(nc.semaphore(f"hankel_in_{i}")) for i in range(2)]
    return e


def expert_tensors(nc, ctx, e):
    def sb(name, shape, dt=F32):
        return ctx.enter_context(nc.sbuf_tensor(name, shape, dt))

    e.plus = sb("plus", [128, EXPERTS, FILTERS, C])
    e.minus = sb("minus", [128, EXPERTS, FILTERS, C])
    e.even = sb("even", [128, EXPERTS, FILTERS, C])
    e.odd = e.minus
    e.taps = sb("taps", [128, EXPERTS, AR_TAPS, C])
    spare = e.even.rearrange("p i k e -> p (i k e)")[0:FILTERS, :]
    e.rows = spare[:, 0:4 * PADS].bitcast(F32R).rearrange("k (r j) -> k r j", r=4)
    e.phi = spare[:, 4 * PADS:4 * PADS + L]
    e.hankel = [sb(f"hankel_{i}", [128, 4, H + 2], F32R) for i in range(2)]
    e.block_mix = [sb(f"block_mix_{i}", [128, EXPERTS, 2, 2, 128], F32R) for i in range(2)]
    e.ar_mix = sb("ar_mix", [128, EXPERTS, AR_TAPS, 2, 128], F32R)
    e.filters = nc.dram_tensor("filters", (FILTERS, 4, PADS), F32, kind="Internal").ap()


def load_hankel(sp, e, k, slot):
    sp.dma_start(e.hankel[slot][:, :, 0:H + 1].bitcast(F32),
                 bass.AP(e.filters.tensor, k * 4 * PADS, [[1, 128], [PADS, 4], [1, H + 1]])
                 ).then_inc(e.hankel_in[slot], 16)


def load_expert_weights(sp, ins, e):
    sp.dma_start(e.phi, ins["phi"][:, 0:L]).then_inc(e.weights_in, 16)
    for half in (0, C):
        for dst, name in ((e.plus, "M_phi_plus"), (e.minus, "M_phi_minus"), (e.taps, "M_u")):
            sp.dma_start(dst[half:half + C, :, :, :], ins[name].rearrange("i k d e -> d i k e")).then_inc(e.weights_in, 16)
    sp.wait_ge(e.rows_ready, 4)
    sp.dma_start(e.filters.rearrange("k r j -> k (r j)"),
                 e.rows.bitcast(F32).rearrange("k r j -> k (r j)")).then_inc(e.filters_out, 16)
    sp.wait_ge(e.filters_out, 16)
    for slot in range(2):
        load_hankel(sp, e, slot, slot)


def chain_on(dve, semaphore, count, instruction):
    instruction.then_inc(semaphore, 1)
    dve.wait_ge(semaphore, count)


def filter_rows(nc, dve, e):
    dve.wait_ge(e.weights_in, EXPERT_LOADS)
    dve.wait_ge(e.rows_step, 1)
    for lag in range(2):
        reverse = e.phi[:, lag::2][:, ::-1]
        chain_on(dve, e.rows_ready, 2 * lag + 1, nc.vector.tensor_copy(e.rows[:, 2 * lag, 0:H], reverse))
        chain_on(dve, e.rows_ready, 2 * lag + 2, nc.vector.tensor_tensor(
            e.rows[:, 2 * lag + 1, 0:H], reverse, e.rows[:, 2 * lag, 0:H].bitcast(F32), ALU.subtract))


def expert_logits(nc, dve, e):
    dve.wait_ge(e.logits_in, 16 * 3)
    chain_on(dve, e.w_step, 1, nc.vector.tensor_tensor(e.w[:, 0, :], e.logits[:, 0, :], e.logits[:, 1, :], ALU.add))
    chain_on(dve, e.w_step, 2, nc.vector.tensor_reduce(e.w[:, 1, 0:1], e.w[:, 0, :], AX.X, ALU.max, negate=True))


def expert_weights(nc, dve, e):
    def chain(semaphore, count, instruction):
        chain_on(dve, semaphore, count, instruction)

    w = e.w
    dve.wait_ge(e.softmax_ready, 2)
    chain(e.w_step, 3, nc.vector.tensor_reduce(w[:, 1, 1:2], w[:, 2, :], AX.X, ALU.add))
    chain(e.w_step, 4, nc.vector.reciprocal(w[:, 1, 2:3], w[:, 1, 1:2]))
    chain(e.w_step, 5, nc.vector.tensor_scalar(w[:, 3, :], w[:, 2, :], w[:, 1, 2:3], None, ALU.mult))
    chain(e.w_step, 6, nc.vector.tensor_reduce(w[:, 1, 3:4], w[:, 3, :], AX.X, ALU.max))
    chain(e.w_step, 7, nc.vector.tensor_scalar(w[:, 4, :], w[:, 3, :], w[:, 1, 3:4], None, ALU.is_equal))
    chain(e.w_step, 8, nc.vector.tensor_copy(w[:, 5, 0:1], w[:, 4, 0:1]))
    for j in range(1, EXPERTS):
        chain(e.w_step, 8 + j, nc.vector.tensor_tensor(w[:, 5, j:j + 1], w[:, 5, j - 1:j], w[:, 4, j:j + 1], ALU.add))
    at = 8 + EXPERTS - 1
    chain(e.w_step, at + 1, nc.vector.tensor_scalar(w[:, 6, :], w[:, 5, :], 1.0, None, ALU.is_equal))
    chain(e.w_step, at + 2, nc.vector.tensor_tensor(w[:, 6, :], w[:, 6, :], w[:, 4, :], ALU.mult))
    chain(e.w_step, at + 3, nc.vector.tensor_tensor(w[:, 7, :], w[:, 6, :], w[:, 3, :], ALU.subtract))
    chain(e.w_step, at + 4, nc.vector.tensor_tensor(w[:, 7, :], w[:, 7, :], w[:, 3, :], ALU.add))
    for i in range(EXPERTS):
        nc.vector.tensor_scalar(e.wk[:, i, :], e.sigma4[:, :], w[:, 7, i:i + 1], None, ALU.mult).then_inc(e.wk_ready, 1)


def clear_blocks(nc, pool, e):
    for i in range(2):
        nc.gpsimd.memset(e.block_mix[i][:, :, :, :, :].bitcast(F32), 0.0).then_inc(e.zeros_ready, 1)
    nc.gpsimd.memset(e.ar_mix[:, :, :, :, :].bitcast(F32), 0.0).then_inc(e.zeros_ready, 1)


def weigh_and_sum(nc, pool, e):
    pool.wait_ge(e.wk_ready, EXPERTS)
    pool.wait_ge(e.weights_in, EXPERT_LOADS)
    done = 0
    for m in (e.plus, e.minus):
        for i in range(EXPERTS):
            done += 1
            nc.gpsimd.tensor_tensor(m[:, i, :, :], m[:, i, :, :], e.wk[:, i, :].unsqueeze(2).to_broadcast([128, FILTERS, C]),
                                    ALU.mult).then_inc(e.sum_step, 1)
            pool.wait_ge(e.sum_step, done)
            if i:
                done += 1
                nc.gpsimd.tensor_tensor(m[:, i, :, :], m[:, i, :, :], m[:, i - 1, :, :], ALU.add).then_inc(e.sum_step, 1)
                pool.wait_ge(e.sum_step, done)


SUMMED = 2 * (2 * EXPERTS - 1)


def lag_matrices(nc, pool, e):
    pool.wait_ge(e.filters_out, 16)
    pool.wait_ge(e.sum_step, SUMMED)
    for i in range(EXPERTS):
        nc.gpsimd.tensor_tensor(e.even[:, i, :, :], e.plus[:, i, :, :], e.minus[:, i, :, :], ALU.add).then_inc(e.sum_step, 1)
        pool.wait_ge(e.sum_step, SUMMED + i + 1)
    for i in range(EXPERTS):
        nc.gpsimd.tensor_tensor(e.odd[:, i, :, :], e.plus[:, i, :, :], e.minus[:, i, :, :], ALU.subtract).then_inc(e.sum_step, 1)


def tap_blocks(nc, pool, e):
    done = 0
    for i in range(EXPERTS):
        done += 1
        nc.gpsimd.tensor_tensor(e.taps[:, i, :, :], e.taps[:, i, :, :],
                                e.w[:, 7, i:i + 1].unsqueeze(2).to_broadcast([128, AR_TAPS, C]),
                                ALU.mult).then_inc(e.ar_step, 1)
        pool.wait_ge(e.ar_step, done)
        if i:
            done += 1
            nc.gpsimd.tensor_tensor(e.taps[:, i, :, :], e.taps[:, i, :, :], e.taps[:, i - 1, :, :],
                                    ALU.add).then_inc(e.ar_step, 1)
            pool.wait_ge(e.ar_step, done)
    pool.wait_ge(e.zeros_ready, 3)
    for half in (0, C):
        dst = e.ar_mix[half:half + C, :, :, :, half:half + C]
        nc.gpsimd.tensor_copy(dst[:, :, :, 0, :], e.taps[half:half + C]).then_inc(e.ar_step, 1)
    pool.wait_ge(e.ar_step, done + 2)
    for half in (0, C):
        dst = e.ar_mix[half:half + C, :, :, :, half:half + C]
        nc.gpsimd.tensor_tensor(dst[:, :, :, 1, :], e.taps[half:half + C], dst[:, :, :, 0, :].bitcast(F32),
                                ALU.subtract).then_inc(e.ar_ready, 1)


def filter_blocks(nc, pool, e, k, slot):
    parts = [(half, lag, src[half:half + C, :, bass.ds(k, 1), :].rearrange("p n o e -> p (n o) e"))
             for half in (0, C) for lag, src in enumerate((e.even, e.odd))]
    for half, lag, src in parts:
        dst = e.block_mix[slot][half:half + C, :, lag, :, half:half + C]
        nc.gpsimd.tensor_copy(dst[:, :, 0, :], src).then_inc(e.block_step, 1)
    pool.wait_ge(e.block_step, BLOCKS * (k + 1))
    pool.sem_inc(e.passed, 1)
    for half, lag, src in parts:
        dst = e.block_mix[slot][half:half + C, :, lag, :, half:half + C]
        nc.gpsimd.tensor_tensor(dst[:, :, 1, :], src, dst[:, :, 0, :].bitcast(F32), ALU.subtract).then_inc(e.block_ready, 1)


def expert_stage(nc, ins, att, e, x2, u_all, u_high, u_low, out):
    HEAD_BANDS = [(0, 64, 3), (64, 128, 2)]
    HEAD = 128
    TAIL_BANDS = [(128, 256, 1), (256, 512, 0)]
    TERMS = [(0, 0), (1, 0), (0, 1)]
    PAIRS = B // 2
    STEPS = 2 * PAIRS

    with ExitStack() as ctx:
        def sb(name, shape, dt=F32):
            return ctx.enter_context(nc.sbuf_tensor(name, shape, dt))

        def sem(name):
            return ctx.enter_context(nc.semaphore(name))

        u_t = [sb(f"u_t_{part}", [128, PAIRS, 2, H + 2], F32R) for part in range(2)]
        head = [[t.rearrange("p (l q a i) -> p l q a i", l=2, q=PAIRS, a=2) for t in pair]
                for pair in ((att.q_parts, att.k_high), (att.q_row, att.k_one))]
        spent_taps = e.ar_mix.rearrange("p n t w e -> p (n t w e)")
        tail = [[sb(f"tail_{part}", [128, 2, 2, H - HEAD], F32R) for part in range(2)],
                [spent_taps[:, part * 4 * (H - HEAD):(part + 1) * 4 * (H - HEAD)].rearrange("p (a l i) -> p a l i", a=2, l=2)
                 for part in range(2)]]
        spent = e.plus.rearrange("p i k e -> p (i k e)")
        result = [spent[:, q * L:(q + 1) * L] for q in range(PAIRS)]

        ps_conv = [ctx.enter_context(nc.psum_tensor(f"ps_conv{i}", [128, 2, 2, H // 2], F32)) for i in range(2)]
        ps_head = ctx.enter_context(nc.psum_tensor("ps_head", [128, PAIRS, 2, HEAD], F32))
        ps_mid = ctx.enter_context(nc.psum_tensor("ps_mid", [128, PAIRS, 2, HEAD], F32))
        ps_tail = [ctx.enter_context(nc.psum_tensor(f"ps_tail{q}", [128, 2, 2 * HEAD], F32)) for q in range(PAIRS)]

        names = "pads_ready ut_psum ut_high ut_low conv_psum conv_high conv_low mixed_in out_done"
        (pads_ready, ut_psum, ut_high, ut_low, conv_psum, conv_high, conv_low, mixed_in,
         out_done) = [sem(name) for name in names.split()]
        result_ready = [sem(f"result_ready_{q}") for q in range(PAIRS)]

        def converted(k, q, source, part):
            mid, end = (tail[q][part][:, source, :, lo:hi] for lo, hi in ((0, HEAD), (HEAD, H - HEAD)))
            return [(head[k % 2][part][:, :, q, source, :], 0, 0, HEAD), (mid, 0, HEAD, 2 * HEAD), (end, 1, 0, 2 * HEAD)]

        by_parity = [r.rearrange("p (i a) -> p a i", a=2) for r in result]
        head_out = [(q, by_parity[q][:, :, 0:HEAD], ps_head[:, q, :, :]) for q in range(PAIRS)]
        mid_out = [(q, by_parity[q][:, :, HEAD:2 * HEAD], ps_mid[:, q, :, :]) for q in range(PAIRS)]
        tail_out = [(q, by_parity[q][:, :, 2 * HEAD:], ps_tail[q][:, :, :]) for q in range(PAIRS)]

        with nc.Block() as block:

            @block.sync
            def _(sp):
                with sp.Fori(1, FILTERS // 2) as pair:
                    for slot in range(2):
                        k = 2 * pair + slot
                        sp.wait_ge(conv_psum, STEPS * (k - 1))
                        load_hankel(sp, e, k, slot)
                for q in range(PAIRS):
                    sp.wait_ge(result_ready[q], 3)
                    sp.dma_start(out.rearrange("b c t -> (b c) t")[128 * q:128 * (q + 1), :], result[q]).then_inc(out_done, 16)
                sp.wait_ge(out_done, 16 * PAIRS)

            @block.gpsimd
            def _(pool):
                for part in range(2):
                    nc.gpsimd.memset(u_t[part][:, :, :, 0:2].bitcast(F32), 0.0).then_inc(pads_ready, 1)
                pool.wait_ge(pads_ready, 2)
                pool.wait_ge(e.sum_step, SUMMED + 2 * EXPERTS)
                for slot in range(2):
                    filter_blocks(nc, pool, e, slot, slot)
                with pool.Fori(1, FILTERS // 2) as pair:
                    for slot in range(2):
                        k = 2 * pair + slot
                        pool.wait_ge(mixed_in, 2 * (k - 1))
                        pool.wait_ge(e.block_ready, BLOCKS * k)
                        filter_blocks(nc, pool, e, k, slot)

            @block.tensor
            def _(pe):
                pairs = [[part[:, :, 2 * q:2 * q + 2, :].rearrange("p i b c -> p i (b c)") for part in (u_high, u_low)]
                         for q in range(PAIRS)]
                cleared = set()

                def add_out(bank, dst, w_block, data):
                    mm = nc.tensor.matmul(dst, w_block, data, start=bank not in cleared, stop=True, skip_group_check=True)
                    cleared.add(bank)
                    return mm

                def convolve(slot, q, source, at):
                    shift = source
                    hankel = e.hankel[slot]
                    row = H + 2
                    for half in range(2):
                        for delta in range(2 * half + 2):
                            first = 128 * delta
                            lo = max(first, half * 2 * HEAD)
                            n = (half + 1) * 2 * HEAD - lo
                            out = ps_conv[at % 2][:, half, :, 2 * HEAD - n:]
                            for term, (wp, dp) in enumerate(TERMS):
                                rows = bass.AP(hankel, dp * row + H - 1 + first - lo,
                                               [[4 * row, 128], [2 * row + shift, 2], [-1, n]])
                                mm = nc.tensor.matmul(out, pairs[q][wp][:, 2 * delta + source, :], rows,
                                                      start=(delta == 0 and term == 0),
                                                      stop=(delta == 2 * half + 1 and term == len(TERMS) - 1))
                    mm.then_inc(conv_psum, 1)

                def mix_tail(slot, q):
                    for lag in range(2):
                        for (lo, hi, band), bank, dst in zip(TAIL_BANDS, ("mid", f"tail{q}"),
                                                             (ps_mid[:, q, :, :], ps_tail[q][:, :, :])):
                            for wp, dp in TERMS:
                                mm = add_out(bank, dst, e.block_mix[slot][:, band, lag, wp, :],
                                             tail[q][dp][:, ::1 - 2 * lag, lag, lo - HEAD:hi - HEAD])
                    return mm

                def mix_head(slot):
                    for lag in range(2):
                        for lo, hi, band in HEAD_BANDS:
                            for wp, dp in TERMS:
                                mm = add_out("head", ps_head[:, :, :, lo:hi], e.block_mix[slot][:, band, lag, wp, :],
                                             head[slot][dp][:, lag, :, ::1 - 2 * lag, lo:hi])
                    return mm

                for q in range(PAIRS):
                    for i in range(TILES):
                        half, at = divmod(128 * (i // 2), 2 * HEAD)
                        mm = nc.tensor.transpose(ps_conv[q][:, half, i % 2, at:at + 128],
                                                 u_all[:, i, 2 * q:2 * q + 2, :].rearrange("p b c -> p (b c)"),
                                                 att.ident[:, :])
                    mm.then_inc(ut_psum, 1)
                for q in range(PAIRS):
                    for a in range(2):
                        for delta in range(SPANS):
                            bank, dst = (("head", ps_head[:, q, a, :]), ("mid", ps_mid[:, q, a, :]),
                                         (f"tail{q}", ps_tail[q][:, a, 0:HEAD]),
                                         (f"tail{q}", ps_tail[q][:, a, HEAD:]))[delta]
                            add_out(bank, dst, x2[:, 2 * delta + a, 2 * q:2 * q + 2, :].rearrange("p b c -> p (b c)"),
                                    att.ident[:, :])
                pe.wait_ge(ut_low, 2 * PAIRS)
                pe.wait_ge(pads_ready, 2)
                pe.wait_ge(e.ar_ready, 2)
                for a in range(2):
                    for tap in range(AR_TAPS):
                        parity = (a + tap) % 2
                        back = (tap + parity - a) // 2
                        for wp, dp in TERMS:
                            for lo, hi, band in HEAD_BANDS:
                                add_out("head", ps_head[:, :, a, lo:hi], e.ar_mix[:, band, tap, wp, :],
                                        u_t[dp][:, :, parity, 2 + lo - back:2 + hi - back])
                            add_out("mid", ps_mid[:, :, a, :], e.ar_mix[:, 1, tap, wp, :],
                                    u_t[dp][:, :, parity, 2 + HEAD - back:2 + 2 * HEAD - back])
                            for q in range(PAIRS):
                                add_out(f"tail{q}", ps_tail[q][:, a, :], e.ar_mix[:, 0, tap, wp, :],
                                        u_t[dp][:, q, parity, 2 + 2 * HEAD - back:2 + H - back])

                def one_filter(pair, slot, first=False):
                    k = 2 * pair + slot
                    pe.wait_ge(e.hankel_in[slot], 16 * (pair + 1))
                    for j in range(STEPS):
                        q, source = divmod(j, 2)
                        m = STEPS * k + j
                        at_least(pe, conv_low, 3 * (m - 1))
                        convolve(slot, q, source, j)
                        if j == 0 and not first:
                            pe.wait_ge(conv_low, 3 * m)
                            mix_tail(1 - slot, PAIRS - 1)
                            mix_head(1 - slot).then_inc(mixed_in, 1)
                        if j == 2:
                            pe.wait_ge(conv_low, 3 * m)
                            pe.wait_ge(e.block_ready, BLOCKS * (k + 1))
                            mix_tail(slot, 0).then_inc(mixed_in, 1)

                one_filter(0, 0, first=True)
                one_filter(0, 1)
                with pe.Fori(1, FILTERS // 2) as pair:
                    one_filter(pair, 0)
                    one_filter(pair, 1)
                pe.wait_ge(conv_low, 3 * STEPS * FILTERS)
                mix_tail(1, PAIRS - 1)
                mix_head(1).then_inc(mixed_in, 1)

            @block.scalar
            def _(act):
                for q in range(PAIRS):
                    act.wait_ge(ut_psum, q + 1)
                    for half in range(2):
                        nc.scalar.activation(u_t[0][:, q, :, 2 + half * 2 * HEAD:2 + (half + 1) * 2 * HEAD],
                                             ps_conv[q][:, half, :, :], ACT.Copy).then_inc(ut_high, 1)

                def one_filter(k, slot, first=False):
                    for j in range(STEPS):
                        q, source = divmod(j, 2)
                        m = STEPS * k + j
                        act.wait_ge(conv_psum, m + 1)
                        if source == 0 and not first:
                            act.wait_ge(mixed_in, 2 * k - 1 + q)
                        for dst, half, lo, hi in converted(slot, q, source, 0):
                            nc.scalar.activation(dst, ps_conv[j % 2][:, half, :, lo:hi], ACT.Copy).then_inc(conv_high, 1)

                one_filter(0, 0, first=True)
                one_filter(1, 1)
                with act.Fori(1, FILTERS // 2) as pair:
                    for slot in range(2):
                        one_filter(2 * pair + slot, slot)
                act.wait_ge(mixed_in, 2 * FILTERS)
                for q, dst, src in [tail_out[0]] + mid_out:
                    nc.scalar.activation(dst, src, ACT.Copy).then_inc(result_ready[q], 1)

            @block.vector
            def _(dve):
                for q in range(PAIRS):
                    for half in range(2):
                        dve.wait_ge(ut_high, 2 * q + half + 1)
                        high, low = (t[:, q, :, 2 + half * 2 * HEAD:2 + (half + 1) * 2 * HEAD] for t in u_t)
                        nc.vector.tensor_tensor(low, ps_conv[q][:, half, :, :], high.bitcast(F32),
                                                ALU.subtract).then_inc(ut_low, 1)

                def one_filter(k, slot):
                    for j in range(STEPS):
                        q, source = divmod(j, 2)
                        m = STEPS * k + j
                        for n, (low, half, lo, hi) in enumerate(converted(slot, q, source, 1)):
                            dve.wait_ge(conv_high, 3 * m + max(2, n + 1))
                            high = converted(slot, q, source, 0)[n][0]
                            nc.vector.tensor_tensor(low, ps_conv[j % 2][:, half, :, lo:hi], high.bitcast(F32),
                                                    ALU.subtract).then_inc(conv_low, 1)

                one_filter(0, 0)
                one_filter(1, 1)
                with dve.Fori(1, FILTERS // 2) as pair:
                    for slot in range(2):
                        one_filter(2 * pair + slot, slot)
                dve.wait_ge(mixed_in, 2 * FILTERS)
                for q, dst, src in head_out + [tail_out[1]]:
                    nc.vector.tensor_copy(dst, src).then_inc(result_ready[q], 1)


def build(nc, ins, out):
    with ExitStack() as ctx:
        x1 = ctx.enter_context(nc.sbuf_tensor("x1", [C, B * L], F32))
        a = attention_tensors(nc, ctx)
        g = norm_tensors(nc, ctx)
        e = weight_tensors(nc, ctx)
        mamba_stage(nc, ins, a, g, e, x1)
        x2 = ctx.enter_context(nc.sbuf_tensor("x2", [128, TILES, B, C], F32))
        u_all = ctx.enter_context(nc.sbuf_tensor("u_all", [128, TILES, B, C], F32))
        u_high = ctx.enter_context(nc.sbuf_tensor("u_high", [128, TILES, B, C], F32R))
        u_low = ctx.enter_context(nc.sbuf_tensor("u_low", [128, TILES, B, C], F32R))
        expert_tensors(nc, ctx, e)
        attention_stage(nc, ins, a, g, e, x1, x2, u_all, u_high, u_low)
        expert_stage(nc, ins, a, e, x2, u_all, u_high, u_low, out)


def kernel(**inputs):
    import numpy as np
    import concourse.bacc as bacc
    from concourse.bass_utils import run_bass_kernel_spmd

    nc = bacc.Bacc("TRN2", target_bir_lowering=False, num_devices=1)
    given = {k.replace("L0_conv_", "").replace("L1_attn_", "").replace("L1_ffn_", ""): np.asarray(v)
             for k, v in inputs.items()}
    arrays = {"x": given["x"].reshape(B, C, L)}
    for d in DIRS:
        w_in, conv_w, w_x = given[f"W_in_{d}"], given[f"conv_w_{d}"], given[f"W_x_{d}"]
        tap = [np.broadcast_to(conv_w[:, j], (C, D)) for j in range(2)]
        rows = [np.stack([w_in[:, :D], tap[1], w_in[:, D:]], axis=1),
                np.stack([w_in[:, :D], tap[0], np.zeros((C, D), w_in.dtype)], axis=1)]
        arrays[f"packed_in_{d}"] = np.concatenate(rows if d == "f" else rows[::-1])
        arrays[f"packed_inner_{d}"] = np.concatenate(
            [w_x[:, R:]] * PARTS + [w_x[:, :R], given[f"W_out_{d}"], given[f"A_log_{d}"],
                                    given[f"conv_b_{d}"][:, None], given[f"D_{d}"][:, None]], axis=1)
        arrays[f"W_dt_{d}"] = given[f"W_dt_{d}"]
        arrays[f"b_dt_{d}"] = given[f"b_dt_{d}"][None]
    for name in ("Wq", "Wk", "Wv"):
        arrays[name] = given[name].T
    for name in ("sigma", "M_phi_plus", "M_phi_minus", "M_u", "log_weights", "gumbel"):
        arrays[name] = given[name]
    arrays["phi"] = given["phi"].T
    arrays["gn_cols"] = np.stack([given["gn_gamma"], given["gn_beta"]], axis=1)
    feed, ins = {}, {}
    for name, a in arrays.items():
        a = np.ascontiguousarray(a)
        feed[f"in_{name}"] = a
        ins[name] = nc.dram_tensor(f"in_{name}", a.shape, mybir.dt.from_np(a.dtype), kind="ExternalInput").ap()
    out = nc.dram_tensor("out_0", (B, C, L), F32, kind="ExternalOutput").ap()
    build(nc, ins, out)
    r = run_bass_kernel_spmd(nc, [feed], core_ids=[0])
    return r.results[0]["out_0"].reshape(B, C, 32, 32)
```
